# Optimizing a Trainium2 kernel written in Bass

```python
import numpy as np
import jax
import jax.numpy as jnp

def _softmax(x, axis=-1):
    return jax.nn.softmax(x, axis=axis)

def _gelu(x):
    return jax.nn.gelu(x, approximate=True)

def _silu(x):
    return jax.nn.silu(x)

def _sigmoid(x):
    return jax.nn.sigmoid(x)

def _layernorm(x, axis=-1, eps=1e-05):
    m = jnp.mean(x, axis=axis, keepdims=True)
    v = jnp.var(x, axis=axis, keepdims=True)
    return (x - m) / jnp.sqrt(v + eps)

def _scatter_add(tgt, idx, src, axis=0):
    return tgt.at[idx].add(src)

def _segment_sum(src, seg, n):
    return jax.ops.segment_sum(src, seg, n)
kernel_name = 'mk_audio_tower_d4_tok_audfeat512_r4_a65d64'

def setup_inputs(seed: int=0):
    np.random.seed(seed)
    _w = jnp.asarray

    def _rec_inputs():
        import jax
        import jax.numpy as jnp
        _rk = jax.random.key(seed)
        x = -3.53888e-05 + 1.00021 * jax.random.normal(jax.random.fold_in(_rk, 1), (4, 750, 23), jnp.float32)
        return x
    x = _rec_inputs()

    def _L0_tok_setup():
        import jax, jax.numpy as jnp
        import numpy as np
        CONTEXT = 5
        DILATION = 1
        BN_EPS = 1e-05

        def _tdnn_forward(x, W, b, gamma, beta):
            B, T, D = x.shape
            L = T - (CONTEXT - 1) * DILATION
            frames = jnp.stack([jax.lax.dynamic_slice_in_dim(x, k * DILATION, L, axis=1) for k in range(CONTEXT)], axis=2)
            patches = frames.reshape(B, L, CONTEXT * D)
            y = jnp.einsum('blf,of->blo', patches, W) + b
            y = jax.nn.relu(y)
            mean = jnp.mean(y, axis=(0, 1))
            var = jnp.var(y, axis=(0, 1))
            y = (y - mean) * jax.lax.rsqrt(var + BN_EPS) * gamma + beta
            return y
        key = jax.random.key(seed)
        k1, k2, k3 = jax.random.split(key, 3)
        B, T, D, O = (64, 1024, 23, 128)
        x = jax.random.normal(k1, (B, T, D), dtype=jnp.float32)
        fan_in = D * CONTEXT
        bound = 1.0 / np.sqrt(fan_in)
        W = jax.random.uniform(k2, (O, fan_in), dtype=jnp.float32, minval=-bound, maxval=bound)
        b = jax.random.uniform(k3, (O,), dtype=jnp.float32, minval=-bound, maxval=bound)
        gamma = jnp.ones((O,), dtype=jnp.float32)
        beta = jnp.zeros((O,), dtype=jnp.float32)
        return {'x': x, 'W': W, 'b': b, 'gamma': gamma, 'beta': beta}
    _L0_tok_all = _L0_tok_setup()
    _L0_tok_in = {k: v for k, v in _L0_tok_all.items() if k in ('W', 'b', 'gamma', 'beta')}
    del _L0_tok_all

    def _L0_attn_setup():
        import jax, jax.numpy as jnp
        import numpy as np
        HIGHEST = jax.lax.Precision.HIGHEST
        KEY_CHUNK_SIZE = 1024 * 4
        HEADS = 8
        DIM_HEAD = 64

        def _query_chunk_size(num_q: int) -> int:
            if num_q % 64 == 0:
                return num_q // 64
            if num_q % 16 == 0:
                return num_q // 16
            if num_q % 4 == 0:
                return num_q // 4
            return num_q

        def _me_attention(q, k, v, q_chunk: int, k_chunk: int):
            S, H, D = q.shape
            num_kv = k.shape[0]
            k_chunk = min(k_chunk, num_kv)
            q = q / jnp.sqrt(jnp.asarray(D, q.dtype))
            kc = k.reshape(-1, k_chunk, H, D)
            vc = v.reshape(-1, k_chunk, H, v.shape[-1])

            def per_qchunk(qch):

                def summarize(args):
                    kch, vch = args
                    s = jnp.einsum('qhd,khd->qhk', qch, kch, precision=HIGHEST)
                    m = jax.lax.stop_gradient(jnp.max(s, axis=-1, keepdims=True))
                    e = jnp.exp(s - m)
                    ev = jnp.einsum('khf,qhk->qhf', vch, e, precision=HIGHEST)
                    return (ev, e.sum(axis=-1), m[..., 0])
                evs, ews, ms = jax.lax.map(summarize, (kc, vc))
                gm = jnp.max(ms, axis=0)
                sc = jnp.exp(ms - gm)
                num = (evs * sc[..., None]).sum(axis=0)
                den = (ews * sc).sum(axis=0)
                return num / den[..., None]
            qs = q.reshape(-1, q_chunk, H, D)
            out = jax.lax.map(per_qchunk, qs)
            return out.reshape(S, H, -1)

        def _forward(hidden_states, w_q, w_k, w_v, w_out, b_out):
            B, S, Dm = hidden_states.shape
            H, dh = (HEADS, DIM_HEAD)
            q = hidden_states @ w_q
            k = hidden_states @ w_k
            v = hidden_states @ w_v

            def to_heads(t):
                return t.reshape(B, S, H, dh).transpose(0, 2, 1, 3).reshape(B * H, S, dh)
            qs, ks, vs = (to_heads(q), to_heads(k), to_heads(v))
            qcs = _query_chunk_size(S)
            attn = _me_attention(qs.transpose(1, 0, 2), ks.transpose(1, 0, 2), vs.transpose(1, 0, 2), qcs, KEY_CHUNK_SIZE)
            attn = attn.transpose(1, 0, 2)
            attn = attn.reshape(B, H, S, dh).transpose(0, 2, 1, 3).reshape(B, S, H * dh)
            return attn @ w_out + b_out
        key = jax.random.key(seed)
        ks = jax.random.split(key, 6)
        B, S, Dm = (2, 2048, 128)
        inner = HEADS * DIM_HEAD
        return {'hidden_states': jax.random.normal(ks[0], (B, S, Dm), dtype=jnp.float32), 'w_q': jax.random.normal(ks[1], (Dm, inner), dtype=jnp.float32) * 0.02, 'w_k': jax.random.normal(ks[2], (Dm, inner), dtype=jnp.float32) * 0.02, 'w_v': jax.random.normal(ks[3], (Dm, inner), dtype=jnp.float32) * 0.02, 'w_out': jax.random.normal(ks[4], (inner, Dm), dtype=jnp.float32) * 0.02, 'b_out': jnp.zeros((Dm,), dtype=jnp.float32)}
    _L0_attn_all = _L0_attn_setup()
    _L0_attn_in = {k: v for k, v in _L0_attn_all.items() if k in ('w_q', 'w_k', 'w_v', 'w_out', 'b_out')}
    del _L0_attn_all

    def _L0_ffn_setup():
        import jax, jax.numpy as jnp
        import numpy as np
        B, S, D, F, E = (4, 512, 128, 512, 8)
        key = jax.random.key(seed)
        k = jax.random.split(key, 5)
        x = jax.random.normal(k[0], (B, S, D), dtype=jnp.float32)
        Ws = jax.random.normal(k[1], (D, E), dtype=jnp.float32) * 0.02
        bs = jnp.zeros((E,), dtype=jnp.float32)
        W1 = jax.random.normal(k[2], (E, D, F), dtype=jnp.float32) * 0.02
        b1 = jnp.zeros((E, F), dtype=jnp.float32)
        W2 = jax.random.normal(k[3], (E, F, D), dtype=jnp.float32) * 0.02
        b2 = jnp.zeros((E, D), dtype=jnp.float32)
        return {'x': x, 'Ws': Ws, 'bs': bs, 'W1': W1, 'b1': b1, 'W2': W2, 'b2': b2}
    _L0_ffn_all = _L0_ffn_setup()
    _L0_ffn_in = {k: v for k, v in _L0_ffn_all.items() if k in ('Ws', 'bs', 'W1', 'b1', 'W2', 'b2')}
    del _L0_ffn_all

    def _L1_attn_setup():
        import jax, jax.numpy as jnp
        import numpy as np
        DIM = 128
        HEADS = 8
        HD = DIM // HEADS
        WIN = 64
        HALF = WIN // 2

        def _sliding_window_attn(q, k, v):
            B, H, S, Dh = q.shape
            scale = Dh ** (-0.5)
            pos = jnp.arange(S)
            offsets = list(range(-HALF, HALF + 1))
            scores = []
            for o in offsets:
                k_sh = jnp.roll(k, -o, axis=2)
                s = jnp.einsum('bhsd,bhsd->bhs', q, k_sh) * scale
                valid = (pos + o >= 0) & (pos + o < S)
                s = jnp.where(valid[None, None, :], s, -jnp.inf)
                scores.append(s)
            scores = jnp.stack(scores, axis=-1)
            p = jax.nn.softmax(scores, axis=-1)
            out = jnp.zeros_like(q)
            for idx, o in enumerate(offsets):
                out = out + p[..., idx:idx + 1] * jnp.roll(v, -o, axis=2)
            return out
        key = jax.random.key(seed)
        k0, k1, k2 = jax.random.split(key, 3)
        x = jax.random.normal(k0, (4, 1024, DIM), dtype=jnp.float32)
        W_qkv = jax.random.normal(k1, (DIM, 3 * DIM), dtype=jnp.float32) * 0.02
        b_qkv = jnp.zeros((3 * DIM,), dtype=jnp.float32)
        W_proj = jax.random.normal(k2, (DIM, DIM), dtype=jnp.float32) * 0.02
        b_proj = jnp.zeros((DIM,), dtype=jnp.float32)
        return {'x': x, 'W_qkv': W_qkv, 'b_qkv': b_qkv, 'W_proj': W_proj, 'b_proj': b_proj}
    _L1_attn_all = _L1_attn_setup()
    _L1_attn_in = {k: v for k, v in _L1_attn_all.items() if k in ('W_qkv', 'b_qkv', 'W_proj', 'b_proj')}
    del _L1_attn_all

    def _L1_ffn_setup():
        import jax, jax.numpy as jnp
        import numpy as np
        NUM_EXPERTS = 8
        TOP_K = 2
        key = jax.random.key(seed)
        k0, k1, k2, k3, k4 = jax.random.split(key, 5)
        sl, bs, hs, ffn = (512, 2, 128, 512)
        T = sl * bs
        x = jax.random.normal(k0, (sl, bs, hs), jnp.float32)
        expert_weights = jax.random.uniform(k1, (T, TOP_K), jnp.float32)
        expert_indices = jax.random.randint(k2, (T, TOP_K), 0, NUM_EXPERTS)
        w1 = jax.random.normal(k3, (NUM_EXPERTS, hs, ffn), jnp.float32) * hs ** (-0.5)
        w2 = jax.random.normal(k4, (NUM_EXPERTS, ffn, hs), jnp.float32) * ffn ** (-0.5)
        return dict(x=x, expert_weights=expert_weights, expert_indices=expert_indices, w1=w1, w2=w2)
    _L1_ffn_all = _L1_ffn_setup()
    _L1_ffn_in = {k: v for k, v in _L1_ffn_all.items() if k in ('expert_weights', 'expert_indices', 'w1', 'w2')}
    del _L1_ffn_all

    def _L2_attn_setup():
        import jax, jax.numpy as jnp
        import numpy as np
        import math
        D_MODEL = 128
        N_HEADS = 8
        HEAD_DIM = D_MODEL // N_HEADS
        V_DIM = 2 * D_MODEL * N_HEADS
        LAYER_INDEX = 0
        LAMBDA_INIT = 0.8
        key = jax.random.key(seed)
        ks = jax.random.split(key, 12)
        B, S = (2, 512)
        s_in = 1.0 / math.sqrt(D_MODEL)
        s_v = 1.0 / math.sqrt(V_DIM)
        return {'x': jax.random.normal(ks[0], (B, S, D_MODEL), jnp.float32), 'Wqkv': jax.random.normal(ks[1], (D_MODEL, 2 * D_MODEL), jnp.float32) * s_in, 'bqkv': jnp.zeros((2 * D_MODEL,), jnp.float32), 'Wv': jax.random.normal(ks[2], (D_MODEL, V_DIM), jnp.float32) * s_in, 'bv': jnp.zeros((V_DIM,), jnp.float32), 'Wo': jax.random.normal(ks[3], (V_DIM, D_MODEL), jnp.float32) * s_v, 'bo': jnp.zeros((D_MODEL,), jnp.float32), 'lq1': jax.random.normal(ks[4], (HEAD_DIM,), jnp.float32) * 0.1, 'lk1': jax.random.normal(ks[5], (HEAD_DIM,), jnp.float32) * 0.1, 'lq2': jax.random.normal(ks[6], (HEAD_DIM,), jnp.float32) * 0.1, 'lk2': jax.random.normal(ks[7], (HEAD_DIM,), jnp.float32) * 0.1}
    _L2_attn_all = _L2_attn_setup()
    _L2_attn_in = {k: v for k, v in _L2_attn_all.items() if k in ('Wqkv', 'bqkv', 'Wv', 'bv', 'Wo', 'bo', 'lq1', 'lk1', 'lq2', 'lk2')}
    del _L2_attn_all

    def _L2_ffn_setup():
        import jax, jax.numpy as jnp
        import numpy as np
        from jax import lax
        N_EXPERTS = 16
        TOP_K = 2
        D_MODEL = 128
        D_FF = 512
        key = jax.random.key(seed)
        ks = jax.random.split(key, 7)
        s_in = 1.0 / np.sqrt(D_MODEL)
        s_ff = 1.0 / np.sqrt(D_FF)
        x = jax.random.normal(ks[0], (2, 512, D_MODEL), dtype=jnp.float32)
        router_w = jax.random.uniform(ks[1], (N_EXPERTS, D_MODEL), jnp.float32, -s_in, s_in)
        router_b = jax.random.uniform(ks[2], (N_EXPERTS,), jnp.float32, -s_in, s_in)
        w1 = jax.random.uniform(ks[3], (N_EXPERTS, D_FF, D_MODEL), jnp.float32, -s_in, s_in)
        b1 = jax.random.uniform(ks[4], (N_EXPERTS, D_FF), jnp.float32, -s_in, s_in)
        w2 = jax.random.uniform(ks[5], (N_EXPERTS, D_MODEL, D_FF), jnp.float32, -s_ff, s_ff)
        b2 = jax.random.uniform(ks[6], (N_EXPERTS, D_MODEL), jnp.float32, -s_ff, s_ff)
        return {'x': x, 'router_w': router_w, 'router_b': router_b, 'w1': w1, 'b1': b1, 'w2': w2, 'b2': b2}
    _L2_ffn_all = _L2_ffn_setup()
    _L2_ffn_in = {k: v for k, v in _L2_ffn_all.items() if k in ('router_w', 'router_b', 'w1', 'b1', 'w2', 'b2')}
    del _L2_ffn_all

    def _L3_attn_setup():
        import jax, jax.numpy as jnp
        import numpy as np
        import math
        D_MODEL = 128
        SLOPE = 0.5
        key = jax.random.key(seed)
        k1, k2, k3, k4 = jax.random.split(key, 4)
        B, S, D = (4, 1024, D_MODEL)
        x = jax.random.normal(k1, (B, S, D), dtype=jnp.float32)
        lim = 1.0 / math.sqrt(D)
        W_qk = jax.random.uniform(k2, (D, D), jnp.float32, -lim, lim)
        W_v = jax.random.uniform(k3, (D, D), jnp.float32, -lim, lim)
        b_v = jax.random.uniform(k4, (D,), jnp.float32, -lim, lim)
        return {'x': x, 'W_qk': W_qk, 'W_v': W_v, 'b_v': b_v}
    _L3_attn_all = _L3_attn_setup()
    _L3_attn_in = {k: v for k, v in _L3_attn_all.items() if k in ('W_qk', 'W_v', 'b_v')}
    del _L3_attn_all

    def _L3_ffn_setup():
        import jax, jax.numpy as jnp
        import numpy as np
        D_IN, D_HID, E, K = (128, 512, 10, 2)
        KS = (9, 1)

        def conv1d_same(x, w, b):
            y = jax.lax.conv_general_dilated(x, w, window_strides=(1,), padding='SAME', dimension_numbers=('NCH', 'OIH', 'NCH'))
            return y + b[None, :, None]
        key = jax.random.key(seed)
        ks = jax.random.split(key, 16)
        s = 0.02
        B, T = (2, 512)
        return {'x': jax.random.normal(ks[0], (B, T, D_IN), jnp.float32), 'rc_w1': jax.random.normal(ks[1], (D_IN, D_IN, 3), jnp.float32) * s, 'rc_b1': jnp.zeros((D_IN,), jnp.float32), 'rc_w2': jax.random.normal(ks[2], (E, D_IN, 3), jnp.float32) * s, 'rc_b2': jnp.zeros((E,), jnp.float32), 'sh_w1': jax.random.normal(ks[3], (D_HID, D_IN, KS[0]), jnp.float32) * s, 'sh_b1': jnp.zeros((D_HID,), jnp.float32), 'sh_w2': jax.random.normal(ks[4], (D_IN, D_HID, KS[1]), jnp.float32) * s, 'sh_b2': jnp.zeros((D_IN,), jnp.float32), 'e_w1': jax.random.normal(ks[5], (E, D_IN, D_HID), jnp.float32) * s, 'e_b1': jnp.zeros((E, D_HID), jnp.float32), 'e_w2': jax.random.normal(ks[6], (E, D_HID, D_IN), jnp.float32) * s, 'e_b2': jnp.zeros((E, D_IN), jnp.float32), 'ln_g': jnp.ones((D_IN,), jnp.float32), 'ln_b': jnp.zeros((D_IN,), jnp.float32)}
    _L3_ffn_all = _L3_ffn_setup()
    _L3_ffn_in = {k: v for k, v in _L3_ffn_all.items() if k in ('rc_w1', 'rc_b1', 'rc_w2', 'rc_b2', 'sh_w1', 'sh_b1', 'sh_w2', 'sh_b2', 'e_w1', 'e_b1', 'e_w2', 'e_b2', 'ln_g', 'ln_b')}
    del _L3_ffn_all
    return {'x': x, 'L0_tok_W': _L0_tok_in['W'], 'L0_tok_b': _L0_tok_in['b'], 'L0_tok_gamma': _L0_tok_in['gamma'], 'L0_tok_beta': _L0_tok_in['beta'], 'L0_attn_w_q': _L0_attn_in['w_q'], 'L0_attn_w_k': _L0_attn_in['w_k'], 'L0_attn_w_v': _L0_attn_in['w_v'], 'L0_attn_w_out': _L0_attn_in['w_out'], 'L0_attn_b_out': _L0_attn_in['b_out'], 'L0_ffn_Ws': _L0_ffn_in['Ws'], 'L0_ffn_bs': _L0_ffn_in['bs'], 'L0_ffn_W1': _L0_ffn_in['W1'], 'L0_ffn_b1': _L0_ffn_in['b1'], 'L0_ffn_W2': _L0_ffn_in['W2'], 'L0_ffn_b2': _L0_ffn_in['b2'], 'L1_attn_W_qkv': _L1_attn_in['W_qkv'], 'L1_attn_b_qkv': _L1_attn_in['b_qkv'], 'L1_attn_W_proj': _L1_attn_in['W_proj'], 'L1_attn_b_proj': _L1_attn_in['b_proj'], 'L1_ffn_expert_weights': _L1_ffn_in['expert_weights'], 'L1_ffn_expert_indices': _L1_ffn_in['expert_indices'], 'L1_ffn_w1': _L1_ffn_in['w1'], 'L1_ffn_w2': _L1_ffn_in['w2'], 'L2_attn_Wqkv': _L2_attn_in['Wqkv'], 'L2_attn_bqkv': _L2_attn_in['bqkv'], 'L2_attn_Wv': _L2_attn_in['Wv'], 'L2_attn_bv': _L2_attn_in['bv'], 'L2_attn_Wo': _L2_attn_in['Wo'], 'L2_attn_bo': _L2_attn_in['bo'], 'L2_attn_lq1': _L2_attn_in['lq1'], 'L2_attn_lk1': _L2_attn_in['lk1'], 'L2_attn_lq2': _L2_attn_in['lq2'], 'L2_attn_lk2': _L2_attn_in['lk2'], 'L2_ffn_router_w': _L2_ffn_in['router_w'], 'L2_ffn_router_b': _L2_ffn_in['router_b'], 'L2_ffn_w1': _L2_ffn_in['w1'], 'L2_ffn_b1': _L2_ffn_in['b1'], 'L2_ffn_w2': _L2_ffn_in['w2'], 'L2_ffn_b2': _L2_ffn_in['b2'], 'L3_attn_W_qk': _L3_attn_in['W_qk'], 'L3_attn_W_v': _L3_attn_in['W_v'], 'L3_attn_b_v': _L3_attn_in['b_v'], 'L3_ffn_rc_w1': _L3_ffn_in['rc_w1'], 'L3_ffn_rc_b1': _L3_ffn_in['rc_b1'], 'L3_ffn_rc_w2': _L3_ffn_in['rc_w2'], 'L3_ffn_rc_b2': _L3_ffn_in['rc_b2'], 'L3_ffn_sh_w1': _L3_ffn_in['sh_w1'], 'L3_ffn_sh_b1': _L3_ffn_in['sh_b1'], 'L3_ffn_sh_w2': _L3_ffn_in['sh_w2'], 'L3_ffn_sh_b2': _L3_ffn_in['sh_b2'], 'L3_ffn_e_w1': _L3_ffn_in['e_w1'], 'L3_ffn_e_b1': _L3_ffn_in['e_b1'], 'L3_ffn_e_w2': _L3_ffn_in['e_w2'], 'L3_ffn_e_b2': _L3_ffn_in['e_b2'], 'L3_ffn_ln_g': _L3_ffn_in['ln_g'], 'L3_ffn_ln_b': _L3_ffn_in['ln_b']}

def reference(x, L0_tok_W, L0_tok_b, L0_tok_gamma, L0_tok_beta, L0_attn_w_q, L0_attn_w_k, L0_attn_w_v, L0_attn_w_out, L0_attn_b_out, L0_ffn_Ws, L0_ffn_bs, L0_ffn_W1, L0_ffn_b1, L0_ffn_W2, L0_ffn_b2, L1_attn_W_qkv, L1_attn_b_qkv, L1_attn_W_proj, L1_attn_b_proj, L1_ffn_expert_weights, L1_ffn_expert_indices, L1_ffn_w1, L1_ffn_w2, L2_attn_Wqkv, L2_attn_bqkv, L2_attn_Wv, L2_attn_bv, L2_attn_Wo, L2_attn_bo, L2_attn_lq1, L2_attn_lk1, L2_attn_lq2, L2_attn_lk2, L2_ffn_router_w, L2_ffn_router_b, L2_ffn_w1, L2_ffn_b1, L2_ffn_w2, L2_ffn_b2, L3_attn_W_qk, L3_attn_W_v, L3_attn_b_v, L3_ffn_rc_w1, L3_ffn_rc_b1, L3_ffn_rc_w2, L3_ffn_rc_b2, L3_ffn_sh_w1, L3_ffn_sh_b1, L3_ffn_sh_w2, L3_ffn_sh_b2, L3_ffn_e_w1, L3_ffn_e_b1, L3_ffn_e_w2, L3_ffn_e_b2, L3_ffn_ln_g, L3_ffn_ln_b):
    import jax
    import jax.numpy as jnp

    def _L0_tok_ref(x, W, b, gamma, beta):
        import jax, jax.numpy as jnp
        import numpy as np
        CONTEXT = 5
        DILATION = 1
        BN_EPS = 1e-05

        def _tdnn_forward(x, W, b, gamma, beta):
            B, T, D = x.shape
            L = T - (CONTEXT - 1) * DILATION
            frames = jnp.stack([jax.lax.dynamic_slice_in_dim(x, k * DILATION, L, axis=1) for k in range(CONTEXT)], axis=2)
            patches = frames.reshape(B, L, CONTEXT * D)
            y = jnp.einsum('blf,of->blo', patches, W) + b
            y = jax.nn.relu(y)
            mean = jnp.mean(y, axis=(0, 1))
            var = jnp.var(y, axis=(0, 1))
            y = (y - mean) * jax.lax.rsqrt(var + BN_EPS) * gamma + beta
            return y
        return _tdnn_forward(x, W, b, gamma, beta)

    def _L0_attn_ref(hidden_states, w_q, w_k, w_v, w_out, b_out):
        import jax, jax.numpy as jnp
        import numpy as np
        HIGHEST = jax.lax.Precision.HIGHEST
        KEY_CHUNK_SIZE = 1024 * 4
        HEADS = 8
        DIM_HEAD = 64

        def _query_chunk_size(num_q: int) -> int:
            if num_q % 64 == 0:
                return num_q // 64
            if num_q % 16 == 0:
                return num_q // 16
            if num_q % 4 == 0:
                return num_q // 4
            return num_q

        def _me_attention(q, k, v, q_chunk: int, k_chunk: int):
            S, H, D = q.shape
            num_kv = k.shape[0]
            k_chunk = min(k_chunk, num_kv)
            q = q / jnp.sqrt(jnp.asarray(D, q.dtype))
            kc = k.reshape(-1, k_chunk, H, D)
            vc = v.reshape(-1, k_chunk, H, v.shape[-1])

            def per_qchunk(qch):

                def summarize(args):
                    kch, vch = args
                    s = jnp.einsum('qhd,khd->qhk', qch, kch, precision=HIGHEST)
                    m = jax.lax.stop_gradient(jnp.max(s, axis=-1, keepdims=True))
                    e = jnp.exp(s - m)
                    ev = jnp.einsum('khf,qhk->qhf', vch, e, precision=HIGHEST)
                    return (ev, e.sum(axis=-1), m[..., 0])
                evs, ews, ms = jax.lax.map(summarize, (kc, vc))
                gm = jnp.max(ms, axis=0)
                sc = jnp.exp(ms - gm)
                num = (evs * sc[..., None]).sum(axis=0)
                den = (ews * sc).sum(axis=0)
                return num / den[..., None]
            qs = q.reshape(-1, q_chunk, H, D)
            out = jax.lax.map(per_qchunk, qs)
            return out.reshape(S, H, -1)

        def _forward(hidden_states, w_q, w_k, w_v, w_out, b_out):
            B, S, Dm = hidden_states.shape
            H, dh = (HEADS, DIM_HEAD)
            q = hidden_states @ w_q
            k = hidden_states @ w_k
            v = hidden_states @ w_v

            def to_heads(t):
                return t.reshape(B, S, H, dh).transpose(0, 2, 1, 3).reshape(B * H, S, dh)
            qs, ks, vs = (to_heads(q), to_heads(k), to_heads(v))
            qcs = _query_chunk_size(S)
            attn = _me_attention(qs.transpose(1, 0, 2), ks.transpose(1, 0, 2), vs.transpose(1, 0, 2), qcs, KEY_CHUNK_SIZE)
            attn = attn.transpose(1, 0, 2)
            attn = attn.reshape(B, H, S, dh).transpose(0, 2, 1, 3).reshape(B, S, H * dh)
            return attn @ w_out + b_out
        return _forward(hidden_states, w_q, w_k, w_v, w_out, b_out)

    def _L0_ffn_ref(x, Ws, bs, W1, b1, W2, b2):
        import jax, jax.numpy as jnp
        import numpy as np
        B, S, D, F, E = (4, 512, 128, 512, 8)
        Bb, Ss, Dd = x.shape
        xt = x.reshape(-1, Dd)
        logits = xt @ Ws + bs
        probs = jax.nn.softmax(logits, axis=-1)
        prob_max = jnp.max(probs, axis=-1)
        routes = jnp.argmax(probs, axis=-1)
        onehot = jax.nn.one_hot(routes, W1.shape[0], dtype=xt.dtype)

        def expert_ffn(w1, bb1, w2, bb2):
            h = jax.nn.gelu(xt @ w1 + bb1, approximate=False)
            return h @ w2 + bb2
        y = jax.vmap(expert_ffn)(W1, b1, W2, b2)
        out = jnp.einsum('te,etd->td', onehot, y)
        out = out * prob_max[:, None]
        return out.reshape(Bb, Ss, Dd)

    def _L1_attn_ref(x, W_qkv, b_qkv, W_proj, b_proj):
        import jax, jax.numpy as jnp
        import numpy as np
        DIM = 128
        HEADS = 8
        HD = DIM // HEADS
        WIN = 64
        HALF = WIN // 2

        def _sliding_window_attn(q, k, v):
            B, H, S, Dh = q.shape
            scale = Dh ** (-0.5)
            pos = jnp.arange(S)
            offsets = list(range(-HALF, HALF + 1))
            scores = []
            for o in offsets:
                k_sh = jnp.roll(k, -o, axis=2)
                s = jnp.einsum('bhsd,bhsd->bhs', q, k_sh) * scale
                valid = (pos + o >= 0) & (pos + o < S)
                s = jnp.where(valid[None, None, :], s, -jnp.inf)
                scores.append(s)
            scores = jnp.stack(scores, axis=-1)
            p = jax.nn.softmax(scores, axis=-1)
            out = jnp.zeros_like(q)
            for idx, o in enumerate(offsets):
                out = out + p[..., idx:idx + 1] * jnp.roll(v, -o, axis=2)
            return out
        B, S, _ = x.shape
        qkv = (x @ W_qkv + b_qkv).reshape(B, S, 3, HEADS, HD)
        qkv = jnp.transpose(qkv, (2, 0, 3, 1, 4))
        q, k, v = (qkv[0], qkv[1], qkv[2])
        attn = _sliding_window_attn(q, k, v)
        attn = jnp.transpose(attn, (0, 2, 1, 3)).reshape(B, S, DIM)
        return attn @ W_proj + b_proj

    def _L1_ffn_ref(x, expert_weights, expert_indices, w1, w2):
        import jax, jax.numpy as jnp
        import numpy as np
        NUM_EXPERTS = 8
        TOP_K = 2
        'Dropless MoE: sort assignments by expert, gather tokens, grouped MLP,\n            scatter-combine with top-k router weights (megablocks gather/scatter semantics).'
        in_shape = x.shape
        hs = in_shape[-1]
        x_flat = x.reshape(-1, hs)
        T = x_flat.shape[0]
        flat_ids = expert_indices.reshape(-1)
        order = jnp.argsort(flat_ids)
        bin_ids = flat_ids[order]
        token_ids = order // TOP_K
        xg = x_flat[token_ids]
        y = jnp.zeros_like(xg)
        for e in range(NUM_EXPERTS):
            h = jax.nn.gelu(xg @ w1[e], approximate=False)
            y = jnp.where((bin_ids == e)[:, None], h @ w2[e], y)
        w = expert_weights.reshape(-1)[order][:, None]
        out = jnp.zeros((T, hs), x.dtype).at[token_ids].add(w * y)
        return out.reshape(in_shape)

    def _L2_attn_ref(x, Wqkv, bqkv, Wv, bv, Wo, bo, lq1, lk1, lq2, lk2):
        import jax, jax.numpy as jnp
        import numpy as np
        import math
        D_MODEL = 128
        N_HEADS = 8
        HEAD_DIM = D_MODEL // N_HEADS
        V_DIM = 2 * D_MODEL * N_HEADS
        LAYER_INDEX = 0
        LAMBDA_INIT = 0.8
        qkv = x @ Wqkv + bqkv
        Q1, Q2, K1, K2 = jnp.split(qkv, 4, axis=-1)
        scale = 1.0 / math.sqrt(HEAD_DIM)
        attn1 = jax.nn.softmax(jnp.einsum('bqd,bkd->bqk', Q1, K1) * scale, axis=-1)
        attn2 = jax.nn.softmax(jnp.einsum('bqd,bkd->bqk', Q2, K2) * scale, axis=-1)
        lam = jnp.exp(jnp.sum(lq1 * lk1)) - jnp.exp(jnp.sum(lq2 * lk2)) + (LAMBDA_INIT - 0.6 * jnp.exp(jnp.asarray(-0.3 * LAYER_INDEX, jnp.float32)))
        diff_attn = attn1 - lam * attn2
        V = x @ Wv + bv
        out = jnp.einsum('bqk,bkv->bqv', diff_attn, V)
        return out @ Wo + bo

    def _L2_ffn_ref(x, router_w, router_b, w1, b1, w2, b2):
        import jax, jax.numpy as jnp
        import numpy as np
        from jax import lax
        N_EXPERTS = 16
        TOP_K = 2
        D_MODEL = 128
        D_FF = 512
        B, S, D = x.shape
        xt = x.reshape(-1, D)
        logits = xt @ router_w.T + router_b
        probs = jax.nn.softmax(logits, axis=-1)
        topk_p, topk_i = lax.top_k(probs, TOP_K)
        onehot = jax.nn.one_hot(topk_i, N_EXPERTS, dtype=probs.dtype)
        gates = jnp.sum(onehot * topk_p[..., None], axis=1)

        def expert_step(acc, packed):
            w1e, b1e, w2e, b2e, ge = packed
            h = jax.nn.gelu(xt @ w1e.T + b1e, approximate=False)
            y = h @ w2e.T + b2e
            return (acc + y * ge[:, None], None)
        out, _ = lax.scan(expert_step, jnp.zeros_like(xt), (w1, b1, w2, b2, gates.T))
        return out.reshape(B, S, D)

    def _L3_attn_ref(x, W_qk, W_v, b_v):
        import jax, jax.numpy as jnp
        import numpy as np
        import math
        D_MODEL = 128
        SLOPE = 0.5
        B, S, D = x.shape
        scale = 1.0 / math.sqrt(D)
        scores = jnp.einsum('bid,de,bje->bij', x, W_qk, x) * scale
        i = jnp.arange(S, dtype=x.dtype)[:, None]
        j = jnp.arange(S, dtype=x.dtype)[None, :]
        scores = scores + (j - i) * jnp.asarray(SLOPE, x.dtype)
        causal = j > i
        scores = jnp.where(causal, -jnp.inf, scores)
        attn = jax.nn.softmax(scores, axis=-1)
        v = jnp.einsum('bjd,ed->bje', x, W_v) + b_v
        return jnp.einsum('bij,bje->bie', attn, v)

    def _L3_ffn_ref(x, rc_w1, rc_b1, rc_w2, rc_b2, sh_w1, sh_b1, sh_w2, sh_b2, e_w1, e_b1, e_w2, e_b2, ln_g, ln_b):
        import jax, jax.numpy as jnp
        import numpy as np
        D_IN, D_HID, E, K = (128, 512, 10, 2)
        KS = (9, 1)

        def conv1d_same(x, w, b):
            y = jax.lax.conv_general_dilated(x, w, window_strides=(1,), padding='SAME', dimension_numbers=('NCH', 'OIH', 'NCH'))
            return y + b[None, :, None]
        B, T, d = x.shape
        residual = x
        xt = jnp.transpose(x, (0, 2, 1))
        rc = conv1d_same(xt, rc_w1, rc_b1)
        rc = jax.nn.gelu(rc, approximate=False)
        rc = conv1d_same(rc, rc_w2, rc_b2)
        logits = jnp.transpose(rc, (0, 2, 1)).reshape(-1, E)
        vals, idx = jax.lax.top_k(logits, K)
        gv = jax.nn.softmax(vals, axis=-1)
        N = logits.shape[0]
        gates = jnp.zeros((N, E), x.dtype).at[jnp.arange(N)[:, None], idx].set(gv)
        x2 = x.reshape(-1, d)
        h = jnp.einsum('nd,edh->enh', x2, e_w1) + e_b1[:, None, :]
        h = jax.nn.elu(h)
        eo = jnp.einsum('enh,ehd->end', h, e_w2) + e_b2[:, None, :]
        y = jnp.einsum('end,ne->nd', eo, gates).reshape(B, T, d)
        sh = conv1d_same(xt, sh_w1, sh_b1)
        sh = jax.nn.silu(sh)
        sh = conv1d_same(sh, sh_w2, sh_b2)
        sh = jnp.transpose(sh, (0, 2, 1))
        z = residual + y + sh
        mu = jnp.mean(z, axis=-1, keepdims=True)
        var = jnp.mean(jnp.square(z - mu), axis=-1, keepdims=True)
        return (z - mu) * jax.lax.rsqrt(var + 1e-05) * ln_g + ln_b
    h = _L0_tok_ref(x, L0_tok_W, L0_tok_b, L0_tok_gamma, L0_tok_beta)
    h = h + _L0_attn_ref(_layernorm(h, axis=-1), L0_attn_w_q, L0_attn_w_k, L0_attn_w_v, L0_attn_w_out, L0_attn_b_out)
    h = h + _L0_ffn_ref(_layernorm(h, axis=-1), L0_ffn_Ws, L0_ffn_bs, L0_ffn_W1, L0_ffn_b1, L0_ffn_W2, L0_ffn_b2)
    h = h + _L1_attn_ref(_layernorm(h, axis=-1), L1_attn_W_qkv, L1_attn_b_qkv, L1_attn_W_proj, L1_attn_b_proj)
    h = h + _L1_ffn_ref(_layernorm(h, axis=-1), L1_ffn_expert_weights, L1_ffn_expert_indices, L1_ffn_w1, L1_ffn_w2)
    h = h + _L2_attn_ref(_layernorm(h, axis=-1), L2_attn_Wqkv, L2_attn_bqkv, L2_attn_Wv, L2_attn_bv, L2_attn_Wo, L2_attn_bo, L2_attn_lq1, L2_attn_lk1, L2_attn_lq2, L2_attn_lk2)
    h = h + _L2_ffn_ref(_layernorm(h, axis=-1), L2_ffn_router_w, L2_ffn_router_b, L2_ffn_w1, L2_ffn_b1, L2_ffn_w2, L2_ffn_b2)
    h = h + _L3_attn_ref(_layernorm(h, axis=-1), L3_attn_W_qk, L3_attn_W_v, L3_attn_b_v)
    h = h + _L3_ffn_ref(_layernorm(h, axis=-1), L3_ffn_rc_w1, L3_ffn_rc_b1, L3_ffn_rc_w2, L3_ffn_rc_b2, L3_ffn_sh_w1, L3_ffn_sh_b1, L3_ffn_sh_w2, L3_ffn_sh_b2, L3_ffn_e_w1, L3_ffn_e_b1, L3_ffn_e_w2, L3_ffn_e_b2, L3_ffn_ln_g, L3_ffn_ln_b)
    return h

_drawn_inputs = setup_inputs


def setup_inputs(seed=0):
    import zlib

    import numpy as np

    out = dict(_drawn_inputs(seed))
    spreads = {'L0_tok_gamma': (1.0, 0.2),
     'L0_tok_beta': (0.0, 0.1),
     'L0_attn_b_out': (0.0, 0.1),
     'L0_ffn_bs': (0.0, 0.53),
     'L0_ffn_b1': (0.0, 0.8),
     'L0_ffn_b2': (0.0, 0.407),
     'L1_attn_b_qkv': (0.0, 0.374),
     'L1_attn_b_proj': (0.0, 0.1),
     'L2_attn_bqkv': (0.0, 0.295),
     'L2_attn_bv': (0.0, 0.1),
     'L2_attn_bo': (0.0, 0.1),
     'L3_ffn_rc_b1': (0.0, 0.318),
     'L3_ffn_rc_b2': (0.0, 0.1),
     'L3_ffn_sh_b1': (0.0, 0.634),
     'L3_ffn_sh_b2': (0.0, 0.1),
     'L3_ffn_e_b1': (0.0, 0.569),
     'L3_ffn_e_b2': (0.0, 0.29),
     'L3_ffn_ln_g': (1.0, 0.2),
     'L3_ffn_ln_b': (0.0, 0.1)}
    factors = {'L0_attn_w_q': 8.0,
     'L0_attn_w_k': 8.0,
     'L0_attn_w_v': 4.482,
     'L0_attn_w_out': 4.197,
     'L0_ffn_Ws': 2.753,
     'L0_ffn_W1': 5.068,
     'L0_ffn_W2': 4.733,
     'L1_attn_W_qkv': 4.915,
     'L2_attn_lq1': 4.73,
     'L2_attn_lk1': 5.409,
     'L2_attn_lq2': 8.0,
     'L2_attn_lk2': 5.45,
     'L2_ffn_router_b': 5.75,
     'L2_ffn_b1': 22.216,
     'L2_ffn_b2': 8.0}
    for name, (base, spread) in spreads.items():
        noise = np.random.default_rng([zlib.crc32(name.encode()), seed]).standard_normal(out[name].shape)
        drawn = base * np.exp(spread * noise) if base else spread * noise
        out[name] = jnp.asarray(drawn.astype(out[name].dtype))
    for name, factor in factors.items():
        out[name] = (out[name] * factor).astype(out[name].dtype)
    return out
```

```python
import math
from contextlib import ExitStack

import concourse.bass as bass
from concourse import mybir

F32 = mybir.dt.float32
I32 = mybir.dt.int32
U32 = mybir.dt.uint32
ALU = mybir.AluOpType
ACT = mybir.ActivationFunctionType
AX = mybir.AxisListType

P = 128
B, T_IN, D_IN, CTX = 4, 750, 23, 5
T = T_IN - CTX + 1
NT = 6
TP = NT * P
NTT = B * NT
LAST = T - (NT - 1) * P
HALF = 3 * P
SC = T // 2
HALO = 32
XW = HALO + TP + HALO
H0, DH0 = 8, 64
H1, DH1, WIN = 8, 16, 192
NF = 4
SLOTS = 6
EPS = 1e-5
NEG = -1e30

MIXES = [("L0", 8, 8), ("L1", 8, 3), ("L2", 16, 8), ("L3", 10, 8)]


class Ring:

    def __init__(self, nc, ctx, name, shape):
        self.t = ctx.enter_context(nc.psum_tensor(name, shape, F32))
        self.full = ctx.enter_context(nc.semaphore(name + "_full"))
        self.free = ctx.enter_context(nc.semaphore(name + "_free"))
        self.fills = 0


def build(nc, a, out):
    ctx = ExitStack()
    with ctx:
        def sb(name, shape, dt=F32):
            return ctx.enter_context(nc.sbuf_tensor(name, shape, dt))

        def sem(name):
            return ctx.enter_context(nc.semaphore(name))

        wide = [Ring(nc, ctx, f"wide{i}", [P, 2, 512]) for i in range(2)]
        turn = [Ring(nc, ctx, f"turn{i}", [P, 512]) for i in range(2)]
        accs = [Ring(nc, ctx, f"accs{i}", [P, 512]) for i in range(2)]

        h = sb("h", [P, NTT, P])
        xn = sb("xn", [P, NTT, P])
        xT = sb("xT", [P, B, XW])
        ident = sb("ident", [P, P])
        ones = sb("ones", [1, P])
        nhalf = sb("nhalf", [P, NT])
        iota_i = sb("iota_i", [P, 16], I32)
        iota = sb("iota", [P, 16])

        w1 = sb("w1", [P, SLOTS, 4 * P])
        w2 = sb("w2", [P, SLOTS, NF, P])
        WSHAPES = {
            "tokW": [CTX * D_IN, P], "tokv": [P, 3],
            "wq": [P, H0 * DH0], "wk": [P, H0 * DH0], "wv": [P, H0 * DH0], "wo": [P, NF, P],
            "bo": [1, P],
            "Ws0": [P, 8], "bs0": [1, 8], "b1_0": [P, 8, NF], "b2_0": [8, P],
            "wqkv1": [P, 3 * P], "bqk1": [P, 2], "bv1": [1, P], "wp1": [P, P], "bp1": [1, P],
            "wqk2": [P, 2 * P], "bqk2": [P, 2], "wvT2": [P, 16, P], "bv2": [P, 16],
            "wo2": [P, 16, P], "bo2": [1, P], "lam": [P, 4, 16],
            "rw2": [P, 16], "rb2": [1, 16], "b1_2": [P, 16, NF], "b2_2": [16, P],
            "wqk3": [P, P], "wv3": [P, P], "bv3": [1, P],
            "rc1": [P, 3, P], "rcb1": [P, 1], "rc2": [P, 3, 10], "rcb2": [1, 10],
            "sh1": [P, 9, 4 * P], "shb1": [P, NF], "sh2": [P, NF, P], "shb2": [1, P],
            "b1_3": [P, 10, NF], "b2_3": [10, P], "lng": [P, P], "lnb": [P, P],
        }
        W = {k: sb("w_" + k, s) for k, s in WSHAPES.items()}
        b1m = sb("b1m", [P, 10, NF])

        shared = sb("shared", [P, 18 * 1024])
        used = [0]

        def part(n, *dims):
            v = shared[:, used[0]:used[0] + n]
            used[0] += n
            assert used[0] <= 18 * 1024
            if len(dims) == 2:
                v = v.rearrange("p (a b) -> p a b", a=dims[0])
            if len(dims) == 3:
                v = v.rearrange("p (a b c) -> p a b c", a=dims[0], b=dims[1])
            return v

        st = sb("st", [P, NT, 6])
        mv = sb("mv", [P, NT, 2])
        ve = sb("ve", [P, NT])
        rstd = sb("rstd", [P, NT])
        nm = sb("nm", [P, 2, 8])
        ssum = sb("ssum", [P, 2, 8])
        rs = sb("rs", [P, 2, 8])
        rs1 = sb("rs1", [P, 4, 8])
        lg = sb("lg", [P, NTT, 16])
        ex = sb("ex", [P, NTT, 16])
        oh = sb("oh", [P, NTT, 16])
        gates = sb("gates", [P, NTT, 16])
        m8 = sb("m8", [P, NTT, 8])
        i8 = sb("i8", [P, NTT, 8], U32)
        i8f = sb("i8f", [P, NTT, 8])
        gw = sb("gw", [P, NTT, 2])
        ei = sb("ei", [P, 9, 2], I32)
        eif = sb("eif", [P, 9, 2])
        ew = sb("ew", [P, 9, 2])
        lamv = sb("lamv", [P, 4])

        patches, yT = part(B * T, B, T), part(B * TP, B, TP)
        st0, mv0, sc0 = part(48, 8, 6), part(2), part(8)
        used[0] = 0
        qT, kT = part(4 * TP, 4, TP), part(4 * TP, 4, TP)
        v0 = part(NT * 512, NT, 512)
        p0 = part(3 * TP, 3, TP)
        pT0 = part(2 * TP, 2, NT, P)
        o0, oT0 = part(512), part(512, NF, P)
        used[0] = 0
        qm = part(H1 * TP, H1, TP)
        k1 = part(XW)
        v1 = part(NT * 2 * P, NT, 2, P)
        s1 = part(3 * H1 * WIN).rearrange("p (s a b) -> p s a b", s=3, a=H1)
        pT1 = part(4 * H1 * P, 2, 2 * H1, P)
        o1, oT1 = part(P), part(P)
        wmask, hmask = part(3 * WIN, 3, WIN), part(H1)
        used[0] = 0
        qk2 = part(2 * TP, 2, TP)
        v2 = part(TP, NT, P)
        p2 = part(4 * TP, 4, TP)
        d2 = part(2 * TP, 2, TP)
        pT2 = part(2 * TP, 2, NT, P)
        wvo, bvo = part(P), part(P)
        used[0] = 0
        uT3, v3 = part(TP), part(TP, NT, P)
        s3, p3 = part(2 * TP, 2, TP), part(3 * TP, 3, TP)
        pT3 = part(2 * TP, 2, NT, P)
        rel = part(TP)
        used[0] = 0
        hid = part(2 * NF * HALF, 2, NF, HALF)
        gT = part(NTT * P)
        rcT = part(B * XW, B, XW)
        e3 = part(NF * HALF, NF, HALF)
        r3 = part(NF * HALF, NF, HALF)
        used[0] = 0
        zt = part(NTT * P, NTT, P)

        loaded = {k: sem("ld_" + k) for k in
                  ("patch", "tok", "attn0", "mix0", "attn1", "mix1", "attn2", "mix2", "attn3", "mix3")}
        experts_in = [sem(f"expert_in{i}") for i in range(SLOTS)]
        consts_ready = sem("consts_ready")
        pool_step = sem("pool_step")
        rstd_ready = sem("rstd_ready")
        var_ready = sem("var_ready")
        xn_ready = sem("xn_ready")
        v_step = sem("v_step")
        v_to_pe = sem("v_to_pe")
        probs_ready = sem("probs_ready")
        elu_ready = sem("elu_ready")
        max_ready = sem("max_ready")
        exp_ready = sem("exp_ready")
        tables_clear = sem("tables_clear")
        stage_done = sem("stage_done")
        out_done = sem("out_done")

        fill_of = {}
        free_of = {}

        def group(dst, loads):
            return [(dst, o, i) for o, i in loads]

        load_list = (
            group("patch", [(patches[k * D_IN:(k + 1) * D_IN, :, :],
                             a["x"].rearrange("b d t -> d b t")[:, :, k:k + T]) for k in range(CTX)])
            + group("tok", [(W[k][:, :], a[k]) for k in ("tokW", "tokv")])
            + group("attn0", [(W[k][:], a[k]) for k in ("wq", "wk", "wv", "wo", "bo")])
            + group("mix0", [(W[k][:], a[k]) for k in ("Ws0", "bs0", "b1_0", "b2_0")])
            + group("attn1", [(W[k][:], a[k]) for k in ("wqkv1", "bqk1", "bv1", "wp1", "bp1")])
            + group("attn2", [(W[k][:], a[k]) for k in
                              ("wqk2", "bqk2", "wvT2", "bv2", "wo2", "bo2")]
                    + [(W["lam"][:], a["lam"].partition_broadcast(P))])
            + group("mix2", [(W[k][:], a[k]) for k in ("rw2", "rb2", "b1_2", "b2_2")])
            + group("attn3", [(W[k][:], a[k]) for k in ("wqk3", "wv3", "bv3")])
            + group("mix3", [(W[k][:], a[k]) for k in
                             ("rc1", "rcb1", "rc2", "rcb2", "sh1", "shb1", "sh2", "shb2", "b1_3", "b2_3")]
                    + [(W[k][:], a[k].partition_broadcast(P)) for k in ("lng", "lnb")])
        )
        N1 = a["ei"].shape[0]
        for dst, src in ((ei, a["ei"]), (ew, a["ew"])):
            load_list += group("mix1", [
                (dst[:, 0:5, :], src[0:640].rearrange("(j p) k -> p j k", p=P)),
                (dst[0:LAST, 5, :], src[640:T]),
                (dst[:, 6:8, :], src[T:T + 256].rearrange("(j p) k -> p j k", p=P)),
                (dst[0:N1 - T - 256, 8, :], src[T + 256:N1])])
        n_loads = {k: 16 * sum(g == k for g, _, _ in load_list) for k in loaded}

        block = ctx.enter_context(nc.Block())

        @block.tensor
        def _(pe):
            v_n, xn_n = [0], [0]

            def opened(ring):
                if ring.fills:
                    pe.wait_ge(ring.free, ring.fills)

            def filled(ring, ins, key=None):
                ins.then_inc(ring.full, 1)
                ring.fills += 1
                fill_of[key] = (ring.full, ring.fills)
                free_of[key] = (ring.free, ring.fills)

            def taken(ring):
                pe.wait_ge(ring.free, ring.fills)

            def moved(*key):
                pe.wait_ge(*free_of[key])

            def from_dve():
                v_n[0] += 1
                pe.wait_ge(v_to_pe, v_n[0])

            def rows(t):
                return LAST if t == NT - 1 else P

            def mm(o, l, r, start=True, stop=True):
                return pe.matmul(o, l, r, start=start, stop=stop)

            def norm_turn(stage, b):
                for half in range(2):
                    xn_n[0] += 1
                    pe.wait_ge(xn_ready, xn_n[0])
                    opened(turn[half])
                    for j in range(3):
                        ins = pe.transpose(turn[half].t[:, j * P:(j + 1) * P],
                                           xn[:, b * NT + 3 * half + j, :], ident[:, :])
                    filled(turn[half], ins, (stage, "norm", b, half))
                for half in range(2):
                    taken(turn[half])

            def xs(b, t0, n):
                return xT[:, b, HALO + t0:HALO + t0 + n]

            def turn_rows(src, key, n=NT):
                for half in range(2):
                    tiles = range(3 * half, min(3 * half + 3, n))
                    if not len(tiles):
                        continue
                    opened(turn[half])
                    for j in tiles:
                        ins = pe.transpose(turn[half].t[:, (j - 3 * half) * P:(j - 3 * half + 1) * P],
                                           src[:, j * P:(j + 1) * P], ident[:, :])
                    filled(turn[half], ins, key + (half,))

            pe.wait_ge(loaded["patch"], n_loads["patch"])
            pe.wait_ge(loaded["tok"], n_loads["tok"])
            for b in range(B):
                ring = wide[b % 2]
                opened(ring)
                for half in range(2):
                    ins = mm(ring.t[:, half, 0:SC], W["tokW"][:, :], patches[0:CTX * D_IN, b, half * SC:(half + 1) * SC])
                filled(ring, ins, ("tok", b))
            pe.wait_ge(consts_ready, 1)
            from_dve()
            for b in range(B):
                turn_rows(yT[:, b, :], ("tokT", b))

            pe.wait_ge(loaded["attn0"], n_loads["attn0"])
            for b in range(B):
                norm_turn("A0", b)
                n = 0
                for nm_, w in (("q", "wq"), ("k", "wk")):
                    for c in range(NF):
                        ring = wide[n % 2]
                        opened(ring)
                        for half in range(2):
                            ins = mm(ring.t[:, half, 0:HALF], W[w][:, c * P:(c + 1) * P], xs(b, half * HALF, HALF))
                        filled(ring, ins, ("A0" + nm_, b, c))
                        n += 1
                for c in range(3):
                    ring = wide[n % 2]
                    opened(ring)
                    for half in range(2):
                        ins = mm(ring.t[:, half, :], xs(b, (2 * c + half) * P, P), W["wv"][:, :])
                    filled(ring, ins, ("A0v", b, c))
                    n += 1
                taken(wide[0])
                taken(wide[1])
                N = NT * H0

                def scores(u):
                    t, hd = divmod(u, H0)
                    ring, r0 = wide[u % 2], DH0 * (hd % 2)
                    opened(ring)
                    for half in range(2):
                        ins = mm(ring.t[:, half, 0:SC], qT[r0:r0 + DH0, hd // 2, t * P:(t + 1) * P],
                                 kT[r0:r0 + DH0, hd // 2, half * SC:(half + 1) * SC])
                    filled(ring, ins, ("S0", b, u))

                def values(u):
                    t, hd = divmod(u, H0)
                    moved("T0", b, u, 0)
                    moved("T0", b, u, 1)
                    if hd == 0:
                        opened(accs[0])
                    for k in range(NT):
                        ins = mm(accs[0].t[:, hd * DH0:(hd + 1) * DH0], pT0[:, u % 2, k, :],
                                 v0[:, k, hd * DH0:(hd + 1) * DH0], k == 0, k == NT - 1)
                    if hd == H0 - 1:
                        filled(accs[0], ins, ("O0", b, t))

                def out_turn(t):
                    moved("O0", b, t)
                    opened(accs[1])
                    for c in range(NF):
                        ins = pe.transpose(accs[1].t[:, c * P:(c + 1) * P], o0[:, c * P:(c + 1) * P], ident[:, :])
                    filled(accs[1], ins, ("OT0", b, t))

                def out_proj(t):
                    moved("OT0", b, t)
                    opened(accs[1])
                    for c in range(NF):
                        mm(accs[1].t[:, 0:P], oT0[:, c, :], W["wo"][:, c, :], c == 0, False)
                    filled(accs[1], mm(accs[1].t[:, 0:P], ones[:, :], W["bo"][:, :], False, True), ("Y0", b, t))

                for s in range(N + 6):
                    if s < N:
                        scores(s)
                    if 3 <= s < N + 3:
                        values(s - 3)
                    if s >= 4 and (s - 4) % H0 == H0 - 1:
                        out_turn((s - 4) // H0)
                    if s >= 5 and (s - 5) % H0 == H0 - 1:
                        out_proj((s - 5) // H0)
                    if 2 <= s < N + 2:
                        moved("S0", b, s - 2)
                        turn_rows(p0[:, (s - 2) % 3, :], ("T0", b, s - 2))

            expert_n = [0]

            def router(stage, w, bias, n_e):
                opened(accs[0])
                for g in range(NTT):
                    b, t = divmod(g, NT)
                    o = accs[0].t[:, g * n_e:(g + 1) * n_e]
                    mm(o, xs(b, t * P, P), w[:, :], True, False)
                    ins = mm(o, ones[:, :], bias[:, :], False, True)
                filled(accs[0], ins, (stage, "logits"))

            def gate_bias(stage, n_e, b2):
                from_dve()
                for q in range(NTT // 4):
                    ring = turn[q % 2]
                    opened(ring)
                    for j in range(4):
                        ins = pe.transpose(ring.t[0:n_e, j * P:(j + 1) * P], gates[:, 4 * q + j, 0:n_e], ident[:, :])
                    filled(ring, ins, (stage, "gT", q))
                taken(turn[0])
                taken(turn[1])
                for q in range(NTT // 4):
                    ring = accs[q % 2]
                    opened(ring)
                    for j in range(4):
                        ins = mm(ring.t[:, j * P:(j + 1) * P], gT[0:n_e, (4 * q + j) * P:(4 * q + j + 1) * P], b2[:, :])
                    filled(ring, ins, (stage, "gb", q))

            def mixture(stage, n_e, n_g):
                first = expert_n[0]
                items = [(e, g) for e in range(n_e) for g in range(n_g)]

                def up(i):
                    e, g = items[i]
                    n = first + e
                    if g == 0:
                        pe.wait_ge(experts_in[n % SLOTS], 32 * (n // SLOTS + 1))
                    b, half = divmod(g, 2)
                    for pair in range(2):
                        opened(wide[pair])
                        for f in range(2):
                            c = 2 * pair + f
                            ins = mm(wide[pair].t[:, f, 0:HALF], w1[:, n % SLOTS, c * P:(c + 1) * P],
                                     xs(b, half * HALF, HALF))
                        filled(wide[pair], ins, (stage, "up", e, g, pair))

                def down(i):
                    e, g = items[i]
                    n = first + e
                    for pair in range(2):
                        if stage == "L3":
                            pe.wait_ge(elu_ready, 2 * i + pair + 1)
                        else:
                            moved(stage, "up", e, g, pair)
                    ring = accs[i % 2]
                    opened(ring)
                    for j in range(3):
                        for c in range(NF):
                            ins = mm(ring.t[:, j * P:(j + 1) * P], hid[:, i % 2, c, j * P:(j + 1) * P],
                                     w2[:, n % SLOTS, c, :], c == 0, c == NF - 1)
                    filled(ring, ins, (stage, "down", e, g))

                for i in range(len(items) + 1):
                    if i < len(items):
                        up(i)
                    if i >= 1:
                        down(i - 1)
                for e in range(n_e):
                    fill_of["expert", first + e] = fill_of[stage, "down", e, n_g - 1]
                expert_n[0] += n_e

            pe.wait_ge(loaded["mix0"], n_loads["mix0"])
            for b in range(B):
                norm_turn("F0", b)
            router("L0", W["Ws0"], W["bs0"], 8)
            mixture("L0", 8, 8)
            gate_bias("L0", 8, W["b2_0"])

            pe.wait_ge(loaded["attn1"], n_loads["attn1"])
            for b in range(B):
                norm_turn("A1", b)
                for i in range(2):
                    opened(wide[i])
                    for half in range(2):
                        ins = mm(wide[i].t[:, half, 0:HALF], W["wqkv1"][:, i * P:(i + 1) * P], xs(b, half * HALF, HALF))
                    filled(wide[i], ins, ("A1qk", b, i))
                for q in range(3):
                    ring = accs[q % 2]
                    opened(ring)
                    for j in range(4):
                        t, side = divmod(4 * q + j, 2)
                        o = ring.t[0:96, j * P:(j + 1) * P]
                        mm(o, xT[:, b, t * P + 96 * side:t * P + 96 * side + 96], W["wqkv1"][:, 2 * P:3 * P], True, False)
                        ins = mm(o, ones[:, 0:96], W["bv1"][:, :], False, True)
                    filled(ring, ins, ("A1v", b, q))
                taken(wide[0])
                taken(wide[1])
                taken(accs[0])
                taken(accs[1])

                def scores1(t, i):
                    opened(wide[i])
                    for j in range(4):
                        hd = 4 * i + j
                        ins = mm(wide[i].t[:, j // 2, (j % 2) * WIN:(j % 2 + 1) * WIN],
                                 qm[:, hd, t * P:(t + 1) * P], k1[:, t * P:t * P + WIN])
                    filled(wide[i], ins, ("S1", b, t, i))

                def turn1(t, q):
                    ring = turn[q % 2]
                    opened(ring)
                    for j in range(4):
                        hd, side = divmod(4 * q + j, 2)
                        ins = pe.transpose(ring.t[0:96, j * P:(j + 1) * P],
                                           s1[:, t % 3, hd, 96 * side:96 * side + 96], ident[:, :])
                    filled(ring, ins, ("T1", b, t, q))

                def values1(t):
                    moved("T1", b, t, 2)
                    moved("T1", b, t, 3)
                    opened(accs[0])
                    for hd in range(H1):
                        for side in range(2):
                            ins = mm(accs[0].t[:, hd * DH1:(hd + 1) * DH1], pT1[0:96, t % 2, 2 * hd + side, :],
                                     v1[0:96, t, side, hd * DH1:(hd + 1) * DH1], side == 0, side == 1)
                    filled(accs[0], ins, ("O1", b, t))

                def out_turn1(t):
                    moved("O1", b, t)
                    opened(accs[1])
                    filled(accs[1], pe.transpose(accs[1].t[:, 0:P], o1[:, :], ident[:, :]), ("OT1", b, t))

                def out_proj1(t):
                    moved("OT1", b, t)
                    opened(accs[1])
                    mm(accs[1].t[:, 0:P], oT1[:, :], W["wp1"][:, :], True, False)
                    filled(accs[1], mm(accs[1].t[:, 0:P], ones[:, :], W["bp1"][:, :], False, True), ("Y1", b, t))

                for s in range(NT + 5):
                    if s < NT:
                        scores1(s, 0)
                    if 2 <= s < NT + 2:
                        pe.wait_ge(probs_ready, b * NT + s - 1)
                        turn1(s - 2, 0)
                        turn1(s - 2, 1)
                    if 4 <= s < NT + 4:
                        out_turn1(s - 4)
                    if s < NT:
                        scores1(s, 1)
                    if 2 <= s < NT + 2:
                        turn1(s - 2, 2)
                        turn1(s - 2, 3)
                    if 3 <= s < NT + 3:
                        values1(s - 3)
                    if 4 <= s < NT + 4:
                        out_proj1(s - 4)

            for b in range(B):
                norm_turn("F1", b)
            mixture("L1", 8, 3)

            pe.wait_ge(loaded["attn2"], n_loads["attn2"])
            opened(accs[0])
            for c in range(16):
                ins = mm(accs[0].t[:, 0:P], W["wvT2"][:, c, :], W["wo2"][:, c, :], c == 0, c == 15)
            filled(accs[0], ins, ("wvo",))
            opened(accs[1])
            for c in range(16):
                ins = mm(accs[1].t[0:1, 0:P], W["bv2"][:, c:c + 1], W["wo2"][:, c, :], c == 0, c == 15)
            filled(accs[1], ins, ("bvo",))
            taken(accs[0])
            taken(accs[1])
            for b in range(B):
                norm_turn("A2", b)
                for i in range(2):
                    opened(wide[i])
                    for half in range(2):
                        ins = mm(wide[i].t[:, half, 0:HALF], W["wqk2"][:, i * P:(i + 1) * P], xs(b, half * HALF, HALF))
                    filled(wide[i], ins, ("A2qk", b, i))
                for half in range(2):
                    opened(accs[half])
                    for j in range(3):
                        o = accs[half].t[:, j * P:(j + 1) * P]
                        mm(o, xs(b, (3 * half + j) * P, P), wvo, True, False)
                        ins = mm(o, ones[:, :], bvo[0:1, :], False, True)
                    filled(accs[half], ins, ("A2v", b, half))
                for ring in wide + accs:
                    taken(ring)

                def scores2(t):
                    for i in range(2):
                        opened(wide[i])
                        for half in range(2):
                            ins = mm(wide[i].t[:, half, 0:SC], qk2[64 * i:64 * i + 64, 0, t * P:(t + 1) * P],
                                     qk2[64 * i:64 * i + 64, 1, half * SC:(half + 1) * SC])
                        filled(wide[i], ins, ("S2", b, t, i))

                def values2(t):
                    moved("T2", b, t, 0)
                    moved("T2", b, t, 1)
                    opened(accs[t % 2])
                    for k in range(NT):
                        mm(accs[t % 2].t[:, 0:P], pT2[:, t % 2, k, :], v2[:, k, :], k == 0, False)
                    filled(accs[t % 2], mm(accs[t % 2].t[:, 0:P], ones[:, :], W["bo2"][:, :], False, True),
                           ("O2", b, t))

                for s in range(NT + 3):
                    if s < NT:
                        scores2(s)
                    if s >= 3:
                        values2(s - 3)
                    if 2 <= s < NT + 2:
                        from_dve()
                        turn_rows(d2[:, s % 2, :], ("T2", b, s - 2))

            pe.wait_ge(loaded["mix2"], n_loads["mix2"])
            for b in range(B):
                norm_turn("F2", b)
            router("L2", W["rw2"], W["rb2"], 16)
            mixture("L2", 16, 8)
            gate_bias("L2", 16, W["b2_2"])

            pe.wait_ge(loaded["attn3"], n_loads["attn3"])
            for b in range(B):
                norm_turn("A3", b)
                opened(wide[0])
                for half in range(2):
                    ins = mm(wide[0].t[:, half, 0:HALF], W["wqk3"][:, :], xs(b, half * HALF, HALF))
                filled(wide[0], ins, ("A3u", b))
                for half in range(2):
                    opened(accs[half])
                    for j in range(3):
                        o = accs[half].t[:, j * P:(j + 1) * P]
                        mm(o, xs(b, (3 * half + j) * P, P), W["wv3"][:, :], True, False)
                        ins = mm(o, ones[:, :], W["bv3"][:, :], False, True)
                    filled(accs[half], ins, ("A3v", b, half))
                for ring in [wide[0]] + accs:
                    taken(ring)

                def scores3(t):
                    ring, n = wide[t % 2], (t + 1) * P
                    opened(ring)
                    for half in range(2):
                        w = min(HALF, n - half * HALF)
                        if w > 0:
                            ins = mm(ring.t[:, half, 0:w], uT3[:, t * P:(t + 1) * P], xs(b, half * HALF, w))
                    filled(ring, ins, ("S3", b, t))

                def values3(t):
                    moved("T3", b, t, 0)
                    if t >= 3:
                        moved("T3", b, t, 1)
                    opened(accs[t % 2])
                    for k in range(t + 1):
                        ins = mm(accs[t % 2].t[:, 0:P], pT3[:, t % 2, k, :], v3[:, k, :], k == 0, k == t)
                    filled(accs[t % 2], ins, ("O3", b, t))

                for s in range(NT + 3):
                    if s < NT:
                        scores3(s)
                    if s >= 3:
                        values3(s - 3)
                    if 2 <= s < NT + 2:
                        pe.wait_ge(probs_ready, NTT + b * NT + s - 1)
                        turn_rows(p3[:, (s - 2) % 3, :], ("T3", b, s - 2), s - 1)

            pe.wait_ge(loaded["mix3"], n_loads["mix3"])
            for b in range(B):
                norm_turn("F3", b)
            for b in range(B):
                ring = wide[b % 2]
                opened(ring)
                for half in range(2):
                    for k in range(3):
                        ins = mm(ring.t[:, half, 0:HALF], W["rc1"][:, k, :], xs(b, half * HALF + k - 1, HALF), k == 0, k == 2)
                filled(ring, ins, ("rc1", b))
            taken(wide[0])
            taken(wide[1])
            opened(accs[0])
            for g in range(NTT):
                b, t = divmod(g, NT)
                o = accs[0].t[:, g * 10:(g + 1) * 10]
                for k in range(3):
                    mm(o, rcT[:, b, HALO + t * P + k - 1:HALO + t * P + k - 1 + P], W["rc2"][:, k, :], k == 0, False)
                ins = mm(o, ones[:, :], W["rcb2"][:, :], False, True)
            filled(accs[0], ins, ("L3", "logits"))

            def shared_up(g):
                b, half = divmod(g, 2)
                for pair in range(2):
                    opened(wide[pair])
                    for f in range(2):
                        c = 2 * pair + f
                        for k in range(9):
                            ins = mm(wide[pair].t[:, f, 0:HALF], W["sh1"][:, k, c * P:(c + 1) * P],
                                     xs(b, half * HALF + k - 4, HALF), k == 0, k == 8)
                    filled(wide[pair], ins, ("sh", g, pair))

            def shared_down(g):
                moved("sh", g, 0)
                moved("sh", g, 1)
                ring = accs[(g + 1) % 2]
                opened(ring)
                for j in range(3):
                    o = ring.t[:, j * P:(j + 1) * P]
                    for c in range(NF):
                        mm(o, hid[:, g % 2, c, j * P:(j + 1) * P], W["sh2"][:, c, :], c == 0, False)
                    ins = mm(o, ones[:, :], W["shb2"][:, :], False, True)
                filled(ring, ins, ("shy", g))

            for g in range(9):
                if g < 8:
                    shared_up(g)
                if g >= 1:
                    shared_down(g - 1)
            mixture("L3", 10, 8)
            gate_bias("L3", 10, W["b2_3"])

        @block.sync
        def _(sp):
            for g, dst, src in load_list:
                if g == "mix1":
                    sp.wait_ge(tables_clear, 1)
                sp.dma_start(dst, src).then_inc(loaded[g], 16)
            n = 0
            for layer, n_e, _ in MIXES:
                for e in range(n_e):
                    if n >= SLOTS:
                        sp.wait_ge(*fill_of["expert", n - SLOTS])
                    sp.dma_start(w1[:, n % SLOTS, :], a[layer + "w1"][e]).then_inc(experts_in[n % SLOTS], 16)
                    sp.dma_start(w2[:, n % SLOTS, :, :], a[layer + "w2"][e].rearrange("(c p) n -> p c n", p=P))\
                      .then_inc(experts_in[n % SLOTS], 16)
                    n += 1
            for b in range(B):
                sp.wait_ge(stage_done, 9)
                sp.dma_start(out[b, 0:(NT - 1) * P, :].rearrange("(j p) d -> p j d", p=P),
                             h[:, b * NT:b * NT + NT - 1, :]).then_inc(out_done, 16)
                sp.dma_start(out[b, (NT - 1) * P:T, :], h[0:LAST, b * NT + NT - 1, :]).then_inc(out_done, 16)
            sp.wait_ge(out_done, 32 * B)

        @block.gpsimd
        def _(pl):
            n = [0]

            def step(ins):
                n[0] += 1
                ins.then_inc(pool_step, 1)
                pl.wait_ge(pool_step, n[0])

            step(pl.memset(ident[:, :], 0.0))
            step(pl.affine_select(out=ident[:, :], in_=ident[:, :], compare_op=ALU.not_equal, fill=1.0,
                                  base=0, pattern=[[-1, P]], channel_multiplier=1))
            step(pl.iota(iota_i[:, :], pattern=[[1, 16]], base=0, channel_multiplier=0))
            step(pl.memset(ones[:, :], 1.0))
            step(pl.memset(nhalf[:, :], -0.5))
            pl.memset(ew[:, :, :], 0.0)
            pl.memset(ei[:, :, :], 0).then_inc(tables_clear, 1)
            step(pl.memset(xT[:, :, :], 0.0))
            pl.memset(h[:, :, :], 0.0).then_inc(consts_ready, 1)

            rn = [0]

            def rsqrt():
                rn[0] += 1
                pl.wait_ge(var_ready, rn[0])
                pl.tensor_tensor(rstd[:, :], ve[:, :], nhalf[:, :], ALU.pow).then_inc(rstd_ready, 1)

            for _ in range(1 + 2 * B):
                rsqrt()
            pl.wait_ge(stage_done, 3)
            step(pl.memset(k1[:, :], 0.0))
            step(pl.memset(hmask[:, :], DH1 ** -0.5))
            step(pl.affine_select(out=hmask[:, :], in_=hmask[:, :], compare_op=ALU.is_ge, fill=0.0,
                                  base=0, pattern=[[-DH1, H1]], channel_multiplier=1))
            step(pl.affine_select(out=hmask[:, :], in_=hmask[:, :], compare_op=ALU.is_ge, fill=0.0,
                                  base=DH1 - 1, pattern=[[DH1, H1]], channel_multiplier=-1))
            step(pl.memset(wmask[:, :, :], 0.0))
            step(pl.affine_select(out=wmask[:, :, :], in_=wmask[:, :, :], compare_op=ALU.is_ge, fill=NEG,
                                  base=0, pattern=[[0, 3], [1, WIN]], channel_multiplier=-1))
            step(pl.affine_select(out=wmask[:, :, :], in_=wmask[:, :, :], compare_op=ALU.is_ge, fill=NEG,
                                  base=64, pattern=[[0, 3], [-1, WIN]], channel_multiplier=1))
            step(pl.memset(wmask[:, 0, 0:32], NEG))
            pl.memset(wmask[:, 2, LAST + 32:WIN], NEG).then_inc(consts_ready, 1)
            for _ in range(4 * B):
                rsqrt()
            pl.wait_ge(stage_done, 7)
            step(pl.iota(rel[:, :], pattern=[[1, TP]], base=-(NT - 1) * P, channel_multiplier=-1,
                         allow_small_or_imprecise_dtypes=True))
            step(pl.tensor_scalar(rel[:, :], rel[:, :], 0.5, None, ALU.mult))
            pl.affine_select(out=rel[:, :], in_=rel[:, :], compare_op=ALU.is_ge, fill=NEG,
                             base=(NT - 1) * P, pattern=[[-1, TP]], channel_multiplier=1).then_inc(consts_ready, 1)
            for _ in range(2 * B):
                rsqrt()
            pl.wait_ge(stage_done, 8)
            pl.memset(rcT[:, :, :], 0.0).then_inc(consts_ready, 1)
            for _ in range(B):
                rsqrt()


        @block.scalar
        def _(act):
            max_n = [0]

            def evac(ring, key, dst, src, func=ACT.Copy, last=True, **kw):
                act.wait_ge(*fill_of[key])
                ins = act.activation(dst, src, func, **kw)
                if last:
                    ins.then_inc(ring.free, 1)

            def norm_turn(stage, b):
                for half in range(2):
                    n = HALF if half == 0 else T - HALF
                    evac(turn[half], (stage, "norm", b, half),
                         xT[:, b, HALO + half * HALF:HALO + half * HALF + n], turn[half].t[:, 0:n])

            def halves(x):
                return x.rearrange("p (a c) -> p a c", a=2)

            def flat(x):
                return x.rearrange("p a c -> p (a c)")

            def from_max():
                max_n[0] += 1
                act.wait_ge(max_ready, max_n[0])

            act.wait_ge(loaded["tok"], n_loads["tok"])
            for b in range(B):
                evac(wide[b % 2], ("tok", b), halves(yT[:, b, 0:T]), wide[b % 2].t[:, :, 0:SC],
                     ACT.Relu, bias=W["tokv"][:, 0:1])
            act.wait_ge(consts_ready, 1)
            for b in range(B):
                evac(turn[0], ("tokT", b, 0), flat(h[:, b * NT:b * NT + 3, :]), turn[0].t[:, 0:HALF])

            for b in range(B):
                norm_turn("A0", b)
                for c in range(NF):
                    evac(wide[c % 2], ("A0q", b, c), halves(qT[:, c, :]), wide[c % 2].t[:, :, 0:HALF],
                         scale=DH0 ** -0.5)
                N = NT * H0
                for s in range(N + 6):
                    if s < N:
                        from_max()
                        t, hd = divmod(s, H0)
                        evac(wide[s % 2], ("S0", b, s), halves(p0[:, s % 3, 0:T]), wide[s % 2].t[:, :, 0:SC],
                             ACT.Exp, bias=nm[:, t % 2, hd:hd + 1], accum_out=ssum[:, t % 2, hd:hd + 1])
                    if s >= 4 and (s - 4) % H0 == H0 - 1:
                        evac(accs[1], ("OT0", b, (s - 4) // H0), flat(oT0[:, :, :]), accs[1].t[:, :])
                    if 2 <= s < N + 2:
                        u = s - 2
                        evac(turn[0], ("T0", b, u, 0), flat(pT0[:, u % 2, 0:3, :]), turn[0].t[:, 0:HALF])

            def gate_rows(stage, n_e):
                for q in range(0, NTT // 4):
                    evac(turn[q % 2], (stage, "gT", q), gT[0:n_e, 4 * q * P:(4 * q + 4) * P],
                         turn[q % 2].t[0:n_e, :])

            def softmax_exp(src):
                from_max()
                act.activation(src, src, ACT.Exp).then_inc(exp_ready, 1)

            def mixture(stage, n_e, n_g, bias):
                for i in range(n_e * n_g):
                    e, g = divmod(i, n_g)
                    for c in range(NF):
                        kw = {} if bias is None else {"bias": bias[:, e, c:c + 1]}
                        evac(wide[c // 2], (stage, "up", e, g, c // 2), hid[:, i % 2, c, :],
                             wide[c // 2].t[:, c % 2, 0:HALF], ACT.Gelu, last=c % 2 == 1, **kw)

            act.wait_ge(loaded["mix0"], n_loads["mix0"])
            for b in range(B):
                norm_turn("F0", b)
            softmax_exp(ex[:, :, 0:8])
            act.wait_ge(stage_done, 2)
            mixture("L0", 8, 8, W["b1_0"])
            gate_rows("L0", 8)

            act.wait_ge(loaded["attn1"], n_loads["attn1"])
            act.wait_ge(consts_ready, 2)
            for b in range(B):
                norm_turn("A1", b)
                evac(wide[1], ("A1qk", b, 1), k1[:, HALO:HALO + HALF], wide[1].t[:, 0, 0:HALF],
                     ACT.Identity, last=False, bias=W["bqk1"][:, 1:2])
                evac(wide[1], ("A1qk", b, 1), k1[:, HALO + HALF:HALO + TP], wide[1].t[:, 1, 0:HALF],
                     ACT.Identity, bias=W["bqk1"][:, 1:2])
                for q in range(3):
                    evac(accs[q % 2], ("A1v", b, q), v1[0:96, 2 * q:2 * q + 2, :, :].rearrange("p a s c -> p (a s c)"),
                         accs[q % 2].t[0:96, :])
                for s in range(NT + 5):
                    if 2 <= s < NT + 2:
                        for q in (0, 2):
                            evac(turn[0], ("T1", b, s - 2, q), flat(pT1[0:96, s % 2, 4 * q:4 * q + 4, :]),
                                 turn[0].t[0:96, :])
                    if 4 <= s < NT + 4:
                        evac(accs[1], ("OT1", b, s - 4), oT1[:, :], accs[1].t[:, 0:P])
                    if s < NT:
                        from_max()
                        for hd in range(H1):
                            ins = act.activation(s1[:, s % 3, hd, :], s1[:, s % 3, hd, :], ACT.Exp,
                                                 bias=nm[:, s % 2, hd:hd + 1], accum_out=ssum[:, s % 2, hd:hd + 1])
                        ins.then_inc(probs_ready, 1)

            for b in range(B):
                norm_turn("F1", b)
            act.wait_ge(stage_done, 4)
            mixture("L1", 8, 3, None)

            act.wait_ge(loaded["attn2"], n_loads["attn2"])
            act.wait_ge(stage_done, 5)
            evac(accs[0], ("wvo",), wvo[:, :], accs[0].t[:, 0:P])
            evac(accs[1], ("bvo",), bvo[0:1, :], accs[1].t[0:1, 0:P])
            from_max()
            act.activation(lamv[:, 0:2], lamv[:, 0:2], ACT.Exp).then_inc(exp_ready, 1)
            for b in range(B):
                norm_turn("A2", b)
                evac(wide[1], ("A2qk", b, 1), halves(qk2[:, 1, :]), wide[1].t[:, :, 0:HALF],
                     ACT.Identity, bias=W["bqk2"][:, 1:2])
                evac(accs[0], ("A2v", b, 0), flat(v2[:, 0:3, :]), accs[0].t[:, 0:HALF])
                for s in range(NT + 2):
                    if s < NT:
                        for i in range(2):
                            from_max()
                            evac(wide[i], ("S2", b, s, i), halves(p2[:, 2 * (s % 2) + i, 0:T]), wide[i].t[:, :, 0:SC],
                                 ACT.Exp, bias=nm[:, s % 2, i:i + 1], accum_out=ssum[:, s % 2, i:i + 1])
                    if s >= 2:
                        u = s - 2
                        evac(turn[0], ("T2", b, u, 0), flat(pT2[:, u % 2, 0:3, :]), turn[0].t[:, 0:HALF])

            act.wait_ge(loaded["mix2"], n_loads["mix2"])
            for b in range(B):
                norm_turn("F2", b)
            softmax_exp(ex[:, :, 0:16])
            act.wait_ge(stage_done, 6)
            mixture("L2", 16, 8, W["b1_2"])
            gate_rows("L2", 16)

            act.wait_ge(stage_done, 7)
            for b in range(B):
                norm_turn("A3", b)
                evac(wide[0], ("A3u", b), halves(uT3[:, :]), wide[0].t[:, :, 0:HALF])
                evac(accs[0], ("A3v", b, 0), flat(v3[:, 0:3, :]), accs[0].t[:, 0:HALF])
                for s in range(NT + 2):
                    if s < NT:
                        from_max()
                        n = (s + 1) * P
                        act.activation(p3[:, s % 3, 0:n], s3[:, s % 2, 0:n], ACT.Exp, bias=nm[:, s % 2, 0:1],
                                       accum_out=ssum[:, s % 2, 0:1]).then_inc(probs_ready, 1)
                    if s >= 2:
                        u = s - 2
                        n = min(3, u + 1)
                        evac(turn[0], ("T3", b, u, 0), flat(pT3[:, u % 2, 0:n, :]), turn[0].t[:, 0:n * P])

            act.wait_ge(loaded["mix3"], n_loads["mix3"])
            for b in range(B):
                norm_turn("F3", b)
            act.wait_ge(stage_done, 8)
            act.wait_ge(consts_ready, 4)
            for b in range(B):
                for half in range(2):
                    n = HALF if half == 0 else T - HALF
                    evac(wide[b % 2], ("rc1", b), rcT[:, b, HALO + half * HALF:HALO + half * HALF + n],
                         wide[b % 2].t[:, half, 0:n], ACT.Gelu, last=half == 1, bias=W["rcb1"][:, 0:1])
            softmax_exp(gw[:, :, 1])
            for g in range(8):
                for c in range(NF):
                    evac(wide[c // 2], ("sh", g, c // 2), hid[:, g % 2, c, :], wide[c // 2].t[:, c % 2, 0:HALF],
                         ACT.Silu, last=c % 2 == 1, bias=W["shb1"][:, c:c + 1])
            for i in range(10 * 8):
                e, g = divmod(i, 8)
                for pair in range(2):
                    act.wait_ge(*fill_of["L3", "up", e, g, pair])
                    if i >= 1:
                        act.wait_ge(elu_ready, 2 * (i - 1) + pair + 1)
                    for f in range(2):
                        c = 2 * pair + f
                        ins = act.activation(e3[:, c, :], wide[pair].t[:, f, 0:HALF], ACT.Exp,
                                             bias=W["b1_3"][:, e, c:c + 1])
                    ins.then_inc(exp_ready, 1)
            gate_rows("L3", 10)

        @block.vector
        def _(dve):
            steps, v_c, var_c, exp_c = [0], [0], [0], [0]

            def step(ins):
                steps[0] += 1
                ins.then_inc(v_step, 1)

            def settle():
                dve.wait_ge(v_step, steps[0])

            def then(ins):
                step(ins)
                settle()

            def to_pe(ins):
                v_c[0] += 1
                ins.then_inc(v_to_pe, 1)

            def settle_pe():
                dve.wait_ge(v_to_pe, v_c[0])

            def see(*key):
                dve.wait_ge(*fill_of[key])

            def moved(*key):
                dve.wait_ge(*free_of[key])

            def from_exp():
                exp_c[0] += 1
                dve.wait_ge(exp_ready, exp_c[0])

            def halves(x):
                return x.rearrange("p (a c) -> p a c", a=2)

            def flat(x):
                return x.rearrange("p a c -> p (a c)")

            def over(x, shape):
                return x.unsqueeze(len(shape) - 1).to_broadcast(shape)

            def rsqrt_var():
                var_c[0] += 1
                dve.wait_ge(rstd_ready, var_c[0])

            def norm(b, src=None, dst=None):
                src = h if src is None else src
                for t in range(NT):
                    ins = dve.bn_stats(st[:, t, :], src[:, b * NT + t, :])
                then(ins)
                for t in range(NT):
                    ins = dve.bn_aggr(mv[:, t, :], st[:, t, :])
                then(ins)
                dve.tensor_scalar(ve[:, :], mv[:, :, 1], EPS, None, ALU.add).then_inc(var_ready, 1)
                rsqrt_var()
                for t in range(NT):
                    ins = dve.tensor_scalar((xn if dst is None else dst)[:, b * NT + t, :], src[:, b * NT + t, :],
                                            mv[:, t, 0:1], rstd[:, t:t + 1], ALU.subtract, ALU.mult)
                    if dst is None and t % 3 == 2:
                        ins.then_inc(xn_ready, 1)
                if dst is not None:
                    then(ins)

            def add_tiles(acc, g, n, ring, key, src):
                see(*key)
                dve.tensor_tensor(acc[:, g:g + n, :], src, acc[:, g:g + n, :], ALU.add).then_inc(ring.free, 1)

            dve.wait_ge(consts_ready, 1)
            dve.memset(ve[:, :], 1.0)
            dve.memset(yT[:, :, T:TP], 0.0)
            step(dve.tensor_copy(iota[:, :], iota_i[:, :]))
            dve.wait_ge(loaded["tok"], n_loads["tok"])
            for b in range(B):
                moved("tok", b)
                for half in range(2):
                    ins = dve.bn_stats(st0[:, 2 * b + half, :], yT[:, b, half * SC:(half + 1) * SC])
            then(ins)
            then(dve.bn_aggr(mv0[:, :], flat(st0[:, :, :])))
            dve.tensor_scalar(ve[:, 0:1], mv0[:, 1:2], EPS, None, ALU.add).then_inc(var_ready, 1)
            rsqrt_var()
            then(dve.tensor_tensor(sc0[:, 0:1], rstd[:, 0:1], W["tokv"][:, 1:2], ALU.mult))
            then(dve.tensor_tensor(sc0[:, 1:2], mv0[:, 0:1], sc0[:, 0:1], ALU.mult))
            then(dve.tensor_tensor(sc0[:, 2:3], W["tokv"][:, 2:3], sc0[:, 1:2], ALU.subtract))
            to_pe(dve.tensor_scalar(yT[:, :, 0:T], yT[:, :, 0:T], sc0[:, 0:1], sc0[:, 2:3], ALU.mult, ALU.add))
            for b in range(B):
                see("tokT", b, 1)
                dve.tensor_copy(flat(h[:, b * NT + 3:b * NT + 6, :]), turn[1].t[:, 0:HALF]).then_inc(turn[1].free, 1)
            for b in range(B):
                for half in range(2):
                    moved("tokT", b, half)
            dve.memset(p0[:, :, T:TP], 0.0).then_inc(stage_done, 1)

            for b in range(B):
                norm(b)
                for c in range(NF):
                    see("A0k", b, c)
                    dve.tensor_copy(halves(kT[:, c, :]), wide[c % 2].t[:, :, 0:HALF]).then_inc(wide[c % 2].free, 1)
                for c in range(3):
                    see("A0v", b, c)
                    dve.tensor_copy(v0[:, 2 * c:2 * c + 2, :], wide[c % 2].t[:, :, :]).then_inc(wide[c % 2].free, 1)
                N = NT * H0
                for s in range(N + 6):
                    if s < N:
                        t, hd = divmod(s, H0)
                        see("S0", b, s)
                        dve.tensor_reduce(nm[:, t % 2, hd:hd + 1], wide[s % 2].t[:, :, 0:SC], AX.XY, ALU.max,
                                          negate=True).then_inc(max_ready, 1)
                    if 3 <= s < N + 3 and (s - 3) % H0 == H0 - 1:
                        t = (s - 3) // H0
                        moved("S0", b, s - 3)
                        moved("S0", b, s - 4)
                        then(dve.reciprocal(rs[:, t % 2, :], ssum[:, t % 2, :]))
                        see("O0", b, t)
                        dve.tensor_tensor(o0.rearrange("p (a c) -> p a c", a=H0),
                                          accs[0].t[:, :].rearrange("p (a c) -> p a c", a=H0),
                                          over(rs[:, t % 2, :], [P, H0, DH0]), ALU.mult).then_inc(accs[0].free, 1)
                    if s >= 5 and (s - 5) % H0 == H0 - 1:
                        t = (s - 5) // H0
                        add_tiles(h, b * NT + t, 1, accs[1], ("Y0", b, t), accs[1].t[:, 0:P].unsqueeze(1))
                    if 2 <= s < N + 2:
                        u = s - 2
                        see("T0", b, u, 1)
                        dve.tensor_copy(flat(pT0[:, u % 2, 3:6, :]), turn[1].t[:, 0:HALF]).then_inc(turn[1].free, 1)
            moved("Y0", B - 1, NT - 1)
            dve.memset(nm[:, :, :], 0.0).then_inc(stage_done, 1)

            def top(stage, n_e, tiles=NTT):
                see(stage, "logits")
                dve.tensor_copy(lg[:, :, 0:n_e], accs[0].t[:, 0:NTT * n_e].rearrange("p (a c) -> p a c", a=NTT))\
                   .then_inc(accs[0].free, 1)
                moved(stage, "logits")
                for g in range(NTT):
                    ins = dve.max(m8[:, g, :], lg[:, g, 0:n_e])
                then(ins)

            def find(n_e):
                for g in range(NTT):
                    ins = dve.max_index(i8[:, g, :], m8[:, g, :], lg[:, g, 0:n_e])
                then(ins)
                then(dve.tensor_copy(i8f[:, :, :], i8[:, :, :]))

            def one_hot(dst, index, n_e, n=NTT):
                return dve.tensor_tensor(dst[:, 0:n, 0:n_e], iota[:, 0:n_e].unsqueeze(1).to_broadcast([P, n, n_e]),
                                         over(index, [P, n, n_e]), ALU.is_equal)

            def times(dst, x, col, n_e, n=NTT):
                return dve.tensor_tensor(dst[:, 0:n, 0:n_e], x[:, 0:n, 0:n_e], over(col, [P, n, n_e]), ALU.mult)

            def route_softmax(stage, n_e, k):
                top(stage, n_e)
                dve.tensor_tensor(ex[:, :, 0:n_e], lg[:, :, 0:n_e], over(m8[:, :, 0], [P, NTT, n_e]), ALU.subtract)\
                   .then_inc(max_ready, 1)
                find(n_e)
                from_exp()
                then(dve.tensor_reduce(gw[:, :, 0], ex[:, :, 0:n_e], AX.X, ALU.add))
                step(dve.reciprocal(gw[:, :, 1], gw[:, :, 0]))
                then(one_hot(gates, i8f[:, :, 0], n_e))
                if k == 2:
                    then(one_hot(oh, i8f[:, :, 1], n_e))
                    then(dve.tensor_tensor(gates[:, :, 0:n_e], gates[:, :, 0:n_e], oh[:, :, 0:n_e], ALU.add))
                then(dve.tensor_tensor(gates[:, :, 0:n_e], gates[:, :, 0:n_e], ex[:, :, 0:n_e], ALU.mult))
                to_pe(times(gates, gates, gw[:, :, 1], n_e))
                settle_pe()

            def gated(acc, stage, i, e, g):
                ring = accs[i % 2]
                see(stage, "down", e, g)
                for j in range(3):
                    tile = 3 * g + j
                    ins = dve.scalar_tensor_tensor(out=acc[:, tile, :], in0=ring.t[:, j * P:(j + 1) * P],
                                                   scalar=gates[:, tile, e:e + 1], in1=acc[:, tile, :],
                                                   op0=ALU.mult, op1=ALU.add)
                ins.then_inc(ring.free, 1)

            def gate_bias(acc, stage):
                for q in range(NTT // 4):
                    add_tiles(acc, 4 * q, 4, accs[q % 2], (stage, "gb", q),
                              accs[q % 2].t[:, :].rearrange("p (a c) -> p a c", a=4))
                moved(stage, "gb", NTT // 4 - 2)
                moved(stage, "gb", NTT // 4 - 1)

            for b in range(B):
                norm(b)
            route_softmax("L0", 8, 1)
            for i in range(8 * 8):
                gated(h, "L0", i, *divmod(i, 8))
            gate_bias(h, "L0")
            dve.memset(nm[:, :, :], 0.0).then_inc(stage_done, 1)

            dve.wait_ge(loaded["attn1"], n_loads["attn1"])
            dve.wait_ge(consts_ready, 2)
            for b in range(B):
                norm(b)
                see("A1qk", b, 0)
                for hd in range(H1):
                    ins = dve.tensor_scalar(halves(qm[:, hd, :]), wide[0].t[:, :, 0:HALF], W["bqk1"][:, 0:1],
                                            hmask[:, hd:hd + 1], ALU.add, ALU.mult)
                ins.then_inc(wide[0].free, 1)
                def turned(t, q):
                    see("T1", b, t, q)
                    dve.tensor_copy(flat(pT1[0:96, t % 2, 4 * q:4 * q + 4, :]), turn[1].t[0:96, :])\
                       .then_inc(turn[1].free, 1)

                for s in range(NT + 5):
                    if 2 <= s < NT + 2:
                        dve.wait_ge(probs_ready, b * NT + s - 1)
                        then(dve.reciprocal(rs1[:, (s - 2) % 4, :], ssum[:, s % 2, :]))
                    if s < NT:
                        mask = wmask[:, 0 if s == 0 else 2 if s == NT - 1 else 1, :]
                        for i in range(2):
                            if i == 1 and s >= 2:
                                turned(s - 2, 1)
                            see("S1", b, s, i)
                            for j in range(2):
                                ins = dve.tensor_tensor(
                                    s1[:, s % 3, 4 * i + 2 * j:4 * i + 2 * j + 2, :],
                                    wide[i].t[:, j, 0:HALF].rearrange("p (a c) -> p a c", a=2),
                                    mask.unsqueeze(1).to_broadcast([P, 2, WIN]), ALU.add)
                            ins.then_inc(wide[i].free, 1)
                        moved("S1", b, s, 0)
                        moved("S1", b, s, 1)
                        dve.tensor_reduce(nm[:, s % 2, :], s1[:, s % 3, :, :], AX.X, ALU.max, negate=True)\
                           .then_inc(max_ready, 1)
                    if NT <= s < NT + 2:
                        turned(s - 2, 1)
                    if 2 <= s < NT + 2:
                        turned(s - 2, 3)
                    if 3 <= s < NT + 3:
                        t = s - 3
                        see("O1", b, t)
                        dve.tensor_tensor(o1.rearrange("p (a c) -> p a c", a=H1),
                                          accs[0].t[:, 0:P].rearrange("p (a c) -> p a c", a=H1),
                                          over(rs1[:, t % 4, :], [P, H1, DH1]), ALU.mult).then_inc(accs[0].free, 1)
                    if 4 <= s < NT + 4:
                        t = s - 4
                        add_tiles(h, b * NT + t, 1, accs[1], ("Y1", b, t), accs[1].t[:, 0:P].unsqueeze(1))
            moved("Y1", B - 1, NT - 1)
            dve.memset(nm[:, :, :], 0.0).then_inc(stage_done, 1)

            for b in range(B):
                norm(b)
            dve.wait_ge(loaded["mix1"], n_loads["mix1"])
            then(dve.tensor_copy(eif[:, :, :], ei[:, :, :]))
            step(one_hot(gates, eif[:, :, 0], 8, 9))
            then(one_hot(oh, eif[:, :, 1], 8, 9))
            step(times(gates, gates, ew[:, :, 0], 8, 9))
            then(times(oh, oh, ew[:, :, 1], 8, 9))
            then(dve.tensor_tensor(gates[:, 0:9, 0:8], gates[:, 0:9, 0:8], oh[:, 0:9, 0:8], ALU.add))
            for i in range(8 * 3):
                gated(h, "L1", i, *divmod(i, 3))
            moved("L1", "down", 7, 1)
            moved("L1", "down", 7, 2)
            dve.memset(nm[:, :, :], 0.0).then_inc(stage_done, 1)

            dve.wait_ge(loaded["attn2"], n_loads["attn2"])
            dve.memset(d2[:, :, T:TP], 0.0)
            for i in range(2):
                ins = dve.tensor_tensor(W["lam"][:, 2 * i, :], W["lam"][:, 2 * i, :], W["lam"][:, 2 * i + 1, :], ALU.mult)
            then(ins)
            dve.tensor_reduce(lamv[:, 0:2], W["lam"][:, 0:4:2, :], AX.X, ALU.add).then_inc(max_ready, 1)
            from_exp()
            then(dve.tensor_tensor(lamv[:, 2:3], lamv[:, 1:2], lamv[:, 0:1], ALU.subtract))
            then(dve.tensor_scalar(lamv[:, 3:4], lamv[:, 2:3], -(0.8 - 0.6 * math.exp(-0.3 * 0)), None, ALU.add))
            for b in range(B):
                norm(b)
                see("A2qk", b, 0)
                dve.tensor_scalar(halves(qk2[:, 0, :]), wide[0].t[:, :, 0:HALF], W["bqk2"][:, 0:1], 0.25,
                                  ALU.add, ALU.mult).then_inc(wide[0].free, 1)
                see("A2v", b, 1)
                dve.tensor_copy(flat(v2[:, 3:6, :]), accs[1].t[:, 0:HALF]).then_inc(accs[1].free, 1)
                for s in range(NT + 3):
                    if s < NT:
                        for i in range(2):
                            see("S2", b, s, i)
                            dve.tensor_reduce(nm[:, s % 2, i:i + 1], wide[i].t[:, :, 0:SC], AX.XY, ALU.max,
                                              negate=True).then_inc(max_ready, 1)
                    if 1 <= s < NT + 1:
                        t = s - 1
                        moved("S2", b, t, 0)
                        moved("S2", b, t, 1)
                        then(dve.reciprocal(rs[:, t % 2, 0:2], ssum[:, t % 2, 0:2]))
                        then(dve.tensor_tensor(rs[:, t % 2, 2:3], rs[:, t % 2, 1:2], lamv[:, 3:4], ALU.mult))
                        then(dve.tensor_scalar(p2[:, 2 * (t % 2) + 1, 0:T], p2[:, 2 * (t % 2) + 1, 0:T],
                                               rs[:, t % 2, 2:3], None, ALU.mult))
                        to_pe(dve.scalar_tensor_tensor(out=d2[:, t % 2, 0:T], in0=p2[:, 2 * (t % 2), 0:T],
                                                       scalar=rs[:, t % 2, 0:1], in1=p2[:, 2 * (t % 2) + 1, 0:T],
                                                       op0=ALU.mult, op1=ALU.add))
                    if s >= 3:
                        t = s - 3
                        add_tiles(h, b * NT + t, 1, accs[t % 2], ("O2", b, t), accs[t % 2].t[:, 0:P].unsqueeze(1))
                    if 2 <= s < NT + 2:
                        t = s - 2
                        see("T2", b, t, 1)
                        dve.tensor_copy(flat(pT2[:, t % 2, 3:6, :]), turn[1].t[:, 0:HALF]).then_inc(turn[1].free, 1)
            moved("O2", B - 1, NT - 2)
            moved("O2", B - 1, NT - 1)
            dve.memset(nm[:, :, :], 0.0).then_inc(stage_done, 1)

            for b in range(B):
                norm(b)
            route_softmax("L2", 16, 2)
            for i in range(16 * 8):
                gated(h, "L2", i, *divmod(i, 8))
            gate_bias(h, "L2")
            dve.memset(nm[:, :, :], 0.0).then_inc(stage_done, 1)

            dve.wait_ge(consts_ready, 3)
            for b in range(B):
                norm(b)
                see("A3v", b, 1)
                dve.tensor_copy(flat(v3[:, 3:6, :]), accs[1].t[:, 0:HALF]).then_inc(accs[1].free, 1)
                for s in range(NT + 3):
                    if 2 <= s < NT + 2:
                        dve.wait_ge(probs_ready, NTT + b * NT + s - 1)
                        then(dve.reciprocal(rs1[:, (s - 2) % 4, 0:1], ssum[:, s % 2, 0:1]))
                    if s < NT:
                        see("S3", b, s)
                        if b * NT + s >= 2:
                            dve.wait_ge(probs_ready, NTT + b * NT + s - 1)
                        n, off = (s + 1) * P, (NT - 1 - s) * P
                        for half in range(2):
                            lo, hi = half * HALF, min((half + 1) * HALF, n)
                            if lo < hi:
                                ins = dve.scalar_tensor_tensor(
                                    out=s3[:, s % 2, lo:hi], in0=wide[s % 2].t[:, half, 0:hi - lo], scalar=P ** -0.5,
                                    in1=rel[:, off + lo:off + hi], op0=ALU.mult, op1=ALU.add)
                        ins.then_inc(wide[s % 2].free, 1)
                        moved("S3", b, s)
                        dve.tensor_reduce(nm[:, s % 2, 0:1], s3[:, s % 2, 0:n], AX.X, ALU.max, negate=True)\
                           .then_inc(max_ready, 1)
                    if s >= 3:
                        t = s - 3
                        see("O3", b, t)
                        dve.scalar_tensor_tensor(out=h[:, b * NT + t, :], in0=accs[t % 2].t[:, 0:P],
                                                 scalar=rs1[:, t % 4, 0:1], in1=h[:, b * NT + t, :],
                                                 op0=ALU.mult, op1=ALU.add).then_inc(accs[t % 2].free, 1)
                    if 5 <= s < NT + 2:
                        t = s - 2
                        see("T3", b, t, 1)
                        dve.tensor_copy(flat(pT3[:, t % 2, 3:t + 1, :]), turn[1].t[:, 0:(t - 2) * P])\
                           .then_inc(turn[1].free, 1)
            moved("O3", B - 1, NT - 2)
            moved("O3", B - 1, NT - 1)
            dve.memset(nm[:, :, :], 0.0).then_inc(stage_done, 1)

            dve.wait_ge(loaded["mix3"], n_loads["mix3"])
            for b in range(B):
                norm(b)
            step(dve.tensor_scalar(b1m[:, :, :], W["b1_3"][:, :, :], -1.0, None, ALU.add))
            top("L3", 10)
            dve.tensor_tensor(gw[:, :, 1], m8[:, :, 1], m8[:, :, 0], ALU.subtract).then_inc(max_ready, 1)
            find(10)
            from_exp()
            then(dve.tensor_scalar(gw[:, :, 0], gw[:, :, 1], 1.0, None, ALU.add))
            then(dve.reciprocal(gw[:, :, 0], gw[:, :, 0]))
            step(dve.tensor_tensor(gw[:, :, 1], gw[:, :, 1], gw[:, :, 0], ALU.mult))
            step(one_hot(gates, i8f[:, :, 0], 10))
            then(one_hot(oh, i8f[:, :, 1], 10))
            step(times(gates, gates, gw[:, :, 0], 10))
            then(times(oh, oh, gw[:, :, 1], 10))
            to_pe(dve.tensor_tensor(gates[:, :, 0:10], gates[:, :, 0:10], oh[:, :, 0:10], ALU.add))
            settle_pe()
            for g in range(8):
                add_tiles(xn, 3 * g, 3, accs[(g + 1) % 2], ("shy", g),
                          accs[(g + 1) % 2].t[:, 0:HALF].rearrange("p (a c) -> p a c", a=3))
            for i in range(10 * 8 + 1):
                if i < 80:
                    e, g = divmod(i, 8)
                    for pair in range(2):
                        from_exp()
                        for f in range(2):
                            c = 2 * pair + f
                            ins = dve.tensor_scalar(r3[:, c, :], wide[pair].t[:, f, 0:HALF], b1m[:, e, c:c + 1], -1.0,
                                                    ALU.add, ALU.max)
                        ins.then_inc(wide[pair].free, 1)
                        moved("L3", "up", e, g, pair)
                        c = 2 * pair
                        dve.scalar_tensor_tensor(out=flat(hid[:, i % 2, c:c + 2, :]), in0=flat(e3[:, c:c + 2, :]),
                                                 scalar=1.0, in1=flat(r3[:, c:c + 2, :]), op0=ALU.min,
                                                 op1=ALU.add).then_inc(elu_ready, 1)
                if i >= 1:
                    gated(xn, "L3", i - 1, *divmod(i - 1, 8))
            gate_bias(xn, "L3")
            for b in range(B):
                norm(b, xn, zt)
                z = zt[:, b * NT:(b + 1) * NT, :]
                then(dve.tensor_tensor(z, z, W["lng"][:, :].unsqueeze(1).to_broadcast([P, NT, P]), ALU.mult))
                then(dve.tensor_tensor(z, z, W["lnb"][:, :].unsqueeze(1).to_broadcast([P, NT, P]), ALU.add))
                ins = dve.tensor_tensor(h[:, b * NT:(b + 1) * NT, :], h[:, b * NT:(b + 1) * NT, :], z, ALU.add)
            ins.then_inc(stage_done, 1)


def kernel(**inputs):
    import numpy as _np
    import concourse.bacc as _bacc
    from concourse import mybir as _mybir
    from concourse.bass_utils import run_bass_kernel_spmd as _run

    x = {k: _np.asarray(v) for k, v in inputs.items()}

    def cols(v, n=1):
        return v.reshape(n, -1).T

    qkv = x["L1_attn_b_qkv"]
    lay = {
        "x": x["x"].transpose(0, 2, 1),
        "tokW": x["L0_tok_W"].T,
        "tokv": _np.stack([x["L0_tok_b"], x["L0_tok_gamma"], x["L0_tok_beta"]], axis=1),
        "wq": x["L0_attn_w_q"], "wk": x["L0_attn_w_k"], "wv": x["L0_attn_w_v"],
        "wo": x["L0_attn_w_out"].reshape(4, 128, 128).transpose(1, 0, 2),
        "bo": x["L0_attn_b_out"][None],
        "Ws0": x["L0_ffn_Ws"], "bs0": x["L0_ffn_bs"][None],
        "b1_0": x["L0_ffn_b1"].reshape(8, 4, 128).transpose(2, 0, 1), "b2_0": x["L0_ffn_b2"],
        "L0w1": x["L0_ffn_W1"], "L0w2": x["L0_ffn_W2"],
        "wqkv1": x["L1_attn_W_qkv"], "bqk1": cols(qkv[:256], 2), "bv1": qkv[None, 256:],
        "wp1": x["L1_attn_W_proj"], "bp1": x["L1_attn_b_proj"][None],
        "ei": x["L1_ffn_expert_indices"], "ew": x["L1_ffn_expert_weights"],
        "L1w1": x["L1_ffn_w1"], "L1w2": x["L1_ffn_w2"],
        "wqk2": x["L2_attn_Wqkv"], "bqk2": cols(x["L2_attn_bqkv"], 2),
        "wvT2": x["L2_attn_Wv"].T.reshape(16, 128, 128).transpose(1, 0, 2),
        "bv2": cols(x["L2_attn_bv"], 16),
        "wo2": x["L2_attn_Wo"].reshape(16, 128, 128).transpose(1, 0, 2),
        "bo2": x["L2_attn_bo"][None],
        "lam": _np.stack([x["L2_attn_lq1"], x["L2_attn_lk1"], x["L2_attn_lq2"], x["L2_attn_lk2"]]),
        "rw2": x["L2_ffn_router_w"].T, "rb2": x["L2_ffn_router_b"][None],
        "b1_2": x["L2_ffn_b1"].reshape(16, 4, 128).transpose(2, 0, 1), "b2_2": x["L2_ffn_b2"],
        "L2w1": x["L2_ffn_w1"].transpose(0, 2, 1), "L2w2": x["L2_ffn_w2"].transpose(0, 2, 1),
        "wqk3": x["L3_attn_W_qk"], "wv3": x["L3_attn_W_v"].T, "bv3": x["L3_attn_b_v"][None],
        "rc1": x["L3_ffn_rc_w1"].transpose(1, 2, 0), "rcb1": cols(x["L3_ffn_rc_b1"]),
        "rc2": x["L3_ffn_rc_w2"].transpose(1, 2, 0), "rcb2": x["L3_ffn_rc_b2"][None],
        "sh1": x["L3_ffn_sh_w1"].transpose(1, 2, 0), "shb1": cols(x["L3_ffn_sh_b1"], 4),
        "sh2": x["L3_ffn_sh_w2"][:, :, 0].T.reshape(4, 128, 128).transpose(1, 0, 2),
        "shb2": x["L3_ffn_sh_b2"][None],
        "b1_3": x["L3_ffn_e_b1"].reshape(10, 4, 128).transpose(2, 0, 1), "b2_3": x["L3_ffn_e_b2"],
        "L3w1": x["L3_ffn_e_w1"], "L3w2": x["L3_ffn_e_w2"],
        "lng": x["L3_ffn_ln_g"], "lnb": x["L3_ffn_ln_b"],
    }
    nc = _bacc.Bacc("TRN2", target_bir_lowering=False, num_devices=1)
    arrays, aps = {}, {}
    for name, v in lay.items():
        v = _np.ascontiguousarray(v)
        arrays[f"in_{name}"] = v
        aps[name] = nc.dram_tensor(f"in_{name}", v.shape, _mybir.dt.from_np(v.dtype), kind="ExternalInput").ap()
    out = nc.dram_tensor("out", (B, T, P), _mybir.dt.float32, kind="ExternalOutput").ap()
    build(nc, aps, out)
    r = _run(nc, [arrays], core_ids=[0])
    return r.results[0]["out"]
```

```python
import math
from contextlib import ExitStack

import concourse.bass as bass
from concourse import mybir

F32 = mybir.dt.float32
I32 = mybir.dt.int32
U32 = mybir.dt.uint32
ALU = mybir.AluOpType
ACT = mybir.ActivationFunctionType
AX = mybir.AxisListType

P = 128
B, T_IN, D_IN, CTX = 4, 750, 23, 5
T = T_IN - CTX + 1
NT = 6
TP = NT * P
NTT = B * NT
LAST = T - (NT - 1) * P
HALF = 3 * P
SC = T // 2
HALO = 32
XW = HALO + TP + HALO
H0, DH0 = 8, 64
H1, DH1, WIN = 8, 16, 192
NF = 4
AREA = 24 * 1024
EW = 1024
EPS = 1e-5
NEG = -1e30


class Mix:

    def __init__(self, name, experts, k, tiles, tokens):
        self.name, self.experts, self.k, self.tiles = name, experts, k, tiles
        self.blocks = (k * tokens + (P - 1) * experts) // P
        self.base = AREA - experts * EW


MIXES = [Mix("L0", 8, 1, NTT, B * T), Mix("L1", 8, 2, 9, 1024),
         Mix("L2", 16, 2, NTT, B * T), Mix("L3", 10, 2, NTT, B * T)]
MAXB = max(m.blocks for m in MIXES)
XG = 4


class Ring:

    def __init__(self, nc, ctx, name, shape):
        self.t = ctx.enter_context(nc.psum_tensor(name, shape, F32))
        self.full = ctx.enter_context(nc.semaphore(name + "_full"))
        self.free = ctx.enter_context(nc.semaphore(name + "_free"))
        self.fills = 0


def build(nc, a, xs_dram, ys_dram, out):
    ctx = ExitStack()
    with ctx:
        def sb(name, shape, dt=F32):
            return ctx.enter_context(nc.sbuf_tensor(name, shape, dt))

        def sem(name):
            return ctx.enter_context(nc.semaphore(name))

        wide = [Ring(nc, ctx, f"wide{i}", [P, 2, 512]) for i in range(2)]
        turn = [Ring(nc, ctx, f"turn{i}", [P, 512]) for i in range(2)]
        accs = [Ring(nc, ctx, f"accs{i}", [P, 512]) for i in range(2)]

        h = sb("h", [P, NTT, P])
        xn = sb("xn", [P, NTT, P])
        xT = sb("xT", [P, B, XW])
        ident = sb("ident", [P, P])
        onesq = sb("onesq", [P, P])
        ones = onesq[0:1, :]
        before = sb("before", [P, P])
        lane = sb("lane", [P, P])
        row = sb("row", [P, 1])
        tok_id = sb("tok_id", [P, NTT])
        real = sb("real", [P, 2, NTT])
        pad_off = sb("pad_off", [P, 2, NTT])
        nhalf = sb("nhalf", [P, NT])

        WSHAPES = {
            "tokW": [CTX * D_IN, P], "tokv": [P, 3],
            "wq": [P, H0 * DH0], "wk": [P, H0 * DH0], "wv": [P, H0 * DH0], "wo": [P, NF, P],
            "bo": [1, P],
            "Ws0": [P, 8], "bs0": [1, 8], "b2_0": [8, P],
            "wqkv1": [P, 3 * P], "bqk1": [P, 2], "bv1": [1, P], "wp1": [P, P], "bp1": [1, P],
            "wqk2": [P, 2 * P], "bqk2": [P, 2], "wvT2": [P, 16, P], "bv2": [P, 16],
            "wo2": [P, 16, P], "bo2": [1, P], "lam": [P, 4, 16],
            "rw2": [P, 16], "rb2": [1, 16], "b2_2": [16, P],
            "wqk3": [P, P], "wv3": [P, P], "bv3": [1, P],
            "rc1": [P, 3, P], "rcb1": [P, 1], "rc2": [P, 3, 10], "rcb2": [1, 10],
            "sh1": [P, 9, 4 * P], "shb1": [P, NF], "sh2": [P, NF, P], "shb2": [1, P],
            "b2_3": [10, P], "lng": [P, P], "lnb": [P, P],
        }
        W = {k: sb("w_" + k, s) for k, s in WSHAPES.items()}

        shared = sb("shared", [P, AREA])
        used = [0]

        def part(n, *dims):
            v = shared[:, used[0]:used[0] + n]
            used[0] += n
            assert used[0] <= AREA
            if len(dims) == 2:
                v = v.rearrange("p (a b) -> p a b", a=dims[0])
            if len(dims) == 3:
                v = v.rearrange("p (a b c) -> p a b c", a=dims[0], b=dims[1])
            return v

        st = sb("st", [P, NT, 6])
        mv = sb("mv", [P, NT, 2])
        ve = sb("ve", [P, NT])
        rstd = sb("rstd", [P, NT])
        nm = sb("nm", [P, 2, 8])
        ssum = sb("ssum", [P, 2, 8])
        rs = sb("rs", [P, 2, 8])
        rs1 = sb("rs1", [P, 4, 8])
        lg = sb("lg", [P, NTT, 16])
        ex = sb("ex", [P, NTT, 16])
        oneh = sb("oneh", [P, 2, NTT, 16])
        gates = sb("gates", [P, NTT, 16])
        m8 = sb("m8", [P, NTT, 8])
        i8 = sb("i8", [P, NTT, 8], U32)
        i8f = sb("i8f", [P, NTT, 8])
        gw = sb("gw", [P, NTT, 2])
        ei = sb("ei", [P, 9, 2], I32)
        eif = sb("eif", [P, 9, 2])
        pos_i = sb("pos_i", [P, 2, NTT], I32)
        ew = sb("ew", [P, 9, 2])
        lamv = sb("lamv", [P, 4])

        patches, yT = part(B * T, B, T), part(B * TP, B, TP)
        st0, mv0, sc0 = part(48, 8, 6), part(2), part(8)
        used[0] = 0
        qT, kT = part(4 * TP, 4, TP), part(4 * TP, 4, TP)
        v0 = part(NT * 512, NT, 512)
        p0 = part(3 * TP, 3, TP)
        pT0 = part(2 * TP, 2, NT, P)
        o0, oT0 = part(512), part(512, NF, P)
        used[0] = 0
        qm = part(H1 * TP, H1, TP)
        k1 = part(XW)
        v1 = part(NT * 2 * P, NT, 2, P)
        s1 = part(3 * H1 * WIN).rearrange("p (s a b) -> p s a b", s=3, a=H1)
        pT1 = part(4 * H1 * P, 2, 2 * H1, P)
        o1, oT1 = part(P), part(P)
        wmask, hmask = part(3 * WIN, 3, WIN), part(H1)
        used[0] = 0
        qk2 = part(2 * TP, 2, TP)
        v2 = part(TP, NT, P)
        p2 = part(4 * TP, 4, TP)
        d2 = part(2 * TP, 2, TP)
        pT2 = part(2 * TP, 2, NT, P)
        wvo, bvo = part(P), part(P)
        used[0] = 0
        uT3, v3 = part(TP), part(TP, NT, P)
        s3, p3 = part(2 * TP, 2, TP), part(3 * TP, 3, TP)
        pT3 = part(2 * TP, 2, NT, P)
        rel = part(TP)
        used[0] = 0
        b1T = part(4 * P)
        slot_hot, blk_hot = part(2 * NT * P, 2, NT, P), part(2 * NT * MAXB, 2, NT, MAXB)
        used[0] -= 2 * NT * (P + MAXB)
        w1c = part(2 * 4 * P, 2, 4 * P)
        e3, r3 = part(2 * NF * P, 2, NF, P), part(NF * P, NF, P)
        ge_end = slot_hot.rearrange("p a b c -> p (a b c)")[:, 0:MAXB * 16]
        sent, pre = part(NTT * 16), part(NTT * 16)
        used[0] -= 2 * NTT * 16
        yo = part(XG * P, XG, P)
        used[0] += 2 * NTT * 16 - XG * P
        ysent = part(2 * NTT * 16)
        used[0] -= 2 * NTT * 16
        gT = part(2 * 4 * P, 2, 4 * P)
        bsum, bpre, bb = part(4 * 16, 4, 16), part(5 * 16, 5, 16), part(4 * 16, 4, 16)
        scan = part(2 * 32, 2, 32)
        nblk, bstart, blk_e = part(16), part(16), part(MAXB)
        pos, slot_f, blk_f = part(2 * NTT), part(2 * NTT), part(2 * NTT)
        bias = part(NF * MAXB, NF, MAXB)
        biasm = part(NF * MAXB, NF, MAXB)
        xg, xgT = part(XG * P, XG, P), part(2 * P, 2, P)
        hidb = part(3 * NF * P, 3, NF, P)
        assert used[0] <= MIXES[2].base, used[0]
        used[0] -= 3 * NF * P
        hid = part(2 * NF * HALF, 2, NF, HALF)
        rcT = part(B * XW, B, XW)
        assert used[0] <= MIXES[3].base, used[0]
        nblk_i, slot_i, blk_i = sb("nblk_i", [P, 16], I32), sb("slot_i", [P, 2 * NTT], I32), sb("blk_i", [P, 2 * NTT], I32)
        blk_e_i = sb("blk_e_i", [P, MAXB], I32)
        idx = sb("idx", [P, MAXB], I32)
        used[0] = AREA - 2 * NTT * P
        yg = part(2 * NTT * P, 2, NTT, P)
        zt = yg[:, 0]

        loaded = {k: sem("ld_" + k) for k in
                  ("patch", "tok", "attn0", "mix0", "attn1", "mix1", "attn2", "mix2", "attn3", "mix3")}
        experts_in = {m.name: sem("experts_in_" + m.name) for m in MIXES}
        b1_in = {k: sem("b1_in_" + k) for k in ("L0", "L2", "L3")}
        xs_out = sem("xs_out")
        xg_in = [sem(f"xg_in{i}") for i in range(XG)]
        ys_out = [sem(f"ys_out{i}") for i in range(XG)]
        yg_in = {(m.name, b): sem(f"yg_in_{m.name}_{b}") for m in MIXES for b in range(B)}
        combined = sem("combined")
        idx_ready = sem("idx_ready")
        gates_ready = sem("gates_ready")
        table_used = sem("table_used")
        w1_ready = sem("w1_ready")
        final_ready = sem("final_ready")
        consts_ready = sem("consts_ready")
        pool_step = sem("pool_step")
        rstd_ready = sem("rstd_ready")
        var_ready = sem("var_ready")
        xn_ready = sem("xn_ready")
        v_step = sem("v_step")
        v_to_pe = sem("v_to_pe")
        probs_ready = sem("probs_ready")
        elu_ready = sem("elu_ready")
        max_ready = sem("max_ready")
        exp_ready = sem("exp_ready")
        tables_clear = sem("tables_clear")
        stage_done = sem("stage_done")
        out_done = sem("out_done")

        fill_of = {}
        free_of = {}

        def group(dst, loads):
            return [(dst, o, i) for o, i in loads]

        load_list = (
            group("patch", [(patches[k * D_IN:(k + 1) * D_IN, :, :],
                             a["x"].rearrange("b d t -> d b t")[:, :, k:k + T]) for k in range(CTX)])
            + group("tok", [(W[k][:, :], a[k]) for k in ("tokW", "tokv")])
            + group("attn0", [(W[k][:], a[k]) for k in ("wq", "wk", "wv", "wo", "bo")])
            + group("mix0", [(W[k][:], a[k]) for k in ("Ws0", "bs0", "b2_0")])
            + group("attn1", [(W[k][:], a[k]) for k in ("wqkv1", "bqk1", "bv1", "wp1", "bp1")])
            + group("attn2", [(W[k][:], a[k]) for k in
                              ("wqk2", "bqk2", "wvT2", "bv2", "wo2", "bo2")]
                    + [(W["lam"][:], a["lam"].partition_broadcast(P))])
            + group("mix2", [(W[k][:], a[k]) for k in ("rw2", "rb2", "b2_2")])
            + group("attn3", [(W[k][:], a[k]) for k in ("wqk3", "wv3", "bv3")])
            + group("mix3", [(W[k][:], a[k]) for k in
                             ("rc1", "rcb1", "rc2", "rcb2", "sh1", "shb1", "sh2", "shb2", "b2_3")]
                    + [(W[k][:], a[k].partition_broadcast(P)) for k in ("lng", "lnb")])
        )
        N1 = a["ei"].shape[0]
        for dst, src in ((ei, a["ei"]), (ew, a["ew"])):
            load_list += group("mix1", [
                (dst[:, 0:5, :], src[0:640].rearrange("(j p) k -> p j k", p=P)),
                (dst[0:LAST, 5, :], src[640:T]),
                (dst[:, 6:8, :], src[T:T + 256].rearrange("(j p) k -> p j k", p=P)),
                (dst[0:N1 - T - 256, 8, :], src[T + 256:N1])])

        def weights(m):
            return shared[:, m.base:AREA].rearrange("p (e n) -> p e n", e=m.experts)

        def batch_tiles(m, b):
            return range(b * NT, min((b + 1) * NT, m.tiles))

        def chunks(m):
            return [(k, list(batch_tiles(m, b))) for k in range(m.k) for b in range(B) if len(batch_tiles(m, b))]

        n_loads = {k: 16 * sum(g == k for g, _, _ in load_list) for k in loaded}

        block = ctx.enter_context(nc.Block())

        @block.tensor
        def _(pe):
            v_n, xn_n = [0], [0]

            def opened(ring):
                if ring.fills:
                    pe.wait_ge(ring.free, ring.fills)

            def filled(ring, ins, key=None):
                ins.then_inc(ring.full, 1)
                ring.fills += 1
                fill_of[key] = (ring.full, ring.fills)
                free_of[key] = (ring.free, ring.fills)

            def taken(ring):
                pe.wait_ge(ring.free, ring.fills)

            def moved(*key):
                pe.wait_ge(*free_of[key])

            def from_dve():
                v_n[0] += 1
                pe.wait_ge(v_to_pe, v_n[0])

            def rows(t):
                return LAST if t == NT - 1 else P

            def mm(o, l, r, start=True, stop=True):
                return pe.matmul(o, l, r, start=start, stop=stop)

            def norm_turn(stage, b):
                for half in range(2):
                    xn_n[0] += 1
                    pe.wait_ge(xn_ready, xn_n[0])
                    opened(turn[half])
                    for j in range(3):
                        ins = pe.transpose(turn[half].t[:, j * P:(j + 1) * P],
                                           xn[:, b * NT + 3 * half + j, :], ident[:, :])
                    filled(turn[half], ins, (stage, "norm", b, half))
                for half in range(2):
                    taken(turn[half])

            def xs(b, t0, n):
                return xT[:, b, HALO + t0:HALO + t0 + n]

            def turn_rows(src, key, n=NT):
                for half in range(2):
                    tiles = range(3 * half, min(3 * half + 3, n))
                    if not len(tiles):
                        continue
                    opened(turn[half])
                    for j in tiles:
                        ins = pe.transpose(turn[half].t[:, (j - 3 * half) * P:(j - 3 * half + 1) * P],
                                           src[:, j * P:(j + 1) * P], ident[:, :])
                    filled(turn[half], ins, key + (half,))

            pe.wait_ge(loaded["patch"], n_loads["patch"])
            pe.wait_ge(loaded["tok"], n_loads["tok"])
            for b in range(B):
                ring = wide[b % 2]
                opened(ring)
                for half in range(2):
                    ins = mm(ring.t[:, half, 0:SC], W["tokW"][:, :], patches[0:CTX * D_IN, b, half * SC:(half + 1) * SC])
                filled(ring, ins, ("tok", b))
            pe.wait_ge(consts_ready, 1)
            from_dve()
            for b in range(B):
                turn_rows(yT[:, b, :], ("tokT", b))

            pe.wait_ge(loaded["attn0"], n_loads["attn0"])
            for b in range(B):
                norm_turn("A0", b)
                n = 0
                for nm_, w in (("q", "wq"), ("k", "wk")):
                    for c in range(NF):
                        ring = wide[n % 2]
                        opened(ring)
                        for half in range(2):
                            ins = mm(ring.t[:, half, 0:HALF], W[w][:, c * P:(c + 1) * P], xs(b, half * HALF, HALF))
                        filled(ring, ins, ("A0" + nm_, b, c))
                        n += 1
                for c in range(3):
                    ring = wide[n % 2]
                    opened(ring)
                    for half in range(2):
                        ins = mm(ring.t[:, half, :], xs(b, (2 * c + half) * P, P), W["wv"][:, :])
                    filled(ring, ins, ("A0v", b, c))
                    n += 1
                taken(wide[0])
                taken(wide[1])
                N = NT * H0

                def scores(u):
                    t, hd = divmod(u, H0)
                    ring, r0 = wide[u % 2], DH0 * (hd % 2)
                    opened(ring)
                    for half in range(2):
                        ins = mm(ring.t[:, half, 0:SC], qT[r0:r0 + DH0, hd // 2, t * P:(t + 1) * P],
                                 kT[r0:r0 + DH0, hd // 2, half * SC:(half + 1) * SC])
                    filled(ring, ins, ("S0", b, u))

                def values(u):
                    t, hd = divmod(u, H0)
                    moved("T0", b, u, 0)
                    moved("T0", b, u, 1)
                    if hd == 0:
                        opened(accs[0])
                    for k in range(NT):
                        ins = mm(accs[0].t[:, hd * DH0:(hd + 1) * DH0], pT0[:, u % 2, k, :],
                                 v0[:, k, hd * DH0:(hd + 1) * DH0], k == 0, k == NT - 1)
                    if hd == H0 - 1:
                        filled(accs[0], ins, ("O0", b, t))

                def out_turn(t):
                    moved("O0", b, t)
                    opened(accs[1])
                    for c in range(NF):
                        ins = pe.transpose(accs[1].t[:, c * P:(c + 1) * P], o0[:, c * P:(c + 1) * P], ident[:, :])
                    filled(accs[1], ins, ("OT0", b, t))

                def out_proj(t):
                    moved("OT0", b, t)
                    opened(accs[1])
                    for c in range(NF):
                        mm(accs[1].t[:, 0:P], oT0[:, c, :], W["wo"][:, c, :], c == 0, False)
                    filled(accs[1], mm(accs[1].t[:, 0:P], ones[:, :], W["bo"][:, :], False, True), ("Y0", b, t))

                for s in range(N + 6):
                    if s < N:
                        scores(s)
                    if 3 <= s < N + 3:
                        values(s - 3)
                    if s >= 4 and (s - 4) % H0 == H0 - 1:
                        out_turn((s - 4) // H0)
                    if s >= 5 and (s - 5) % H0 == H0 - 1:
                        out_proj((s - 5) // H0)
                    if 2 <= s < N + 2:
                        moved("S0", b, s - 2)
                        turn_rows(p0[:, (s - 2) % 3, :], ("T0", b, s - 2))

            chunk_n, w1_n, idx_n = [0], [0], [0]
            xg_n = [0] * XG

            def router(stage, w, bias, n_e):
                opened(accs[0])
                for g in range(NTT):
                    b, t = divmod(g, NT)
                    o = accs[0].t[:, g * n_e:(g + 1) * n_e]
                    mm(o, xs(b, t * P, P), w[:, :], True, False)
                    ins = mm(o, ones[:, :], bias[:, :], False, True)
                filled(accs[0], ins, (stage, "logits"))

            def ranks(m):
                from_dve()
                opened(wide[0])
                mm(wide[0].t[:, 0, 0:NTT * m.experts], before[:, :], sent[:, 0:NTT * m.experts])
                filled(wide[0], mm(wide[0].t[:, 1, 0:NTT * m.experts], onesq[:, :], sent[:, 0:NTT * m.experts]),
                       (m.name, "ranks"))

            def block_bias(m):
                from_dve()
                pe.wait_ge(b1_in[m.name], 16)
                opened(accs[0])
                for c in range(NF):
                    ins = mm(accs[0].t[:, c * m.blocks:(c + 1) * m.blocks], b1T[0:m.experts, c * P:(c + 1) * P],
                             blk_e[0:m.experts, 0:m.blocks])
                filled(accs[0], ins, (m.name, "bias"))

            def invert(m):
                opened(accs[1])
                todo = chunks(m)
                for i, (k, tiles) in enumerate(todo):
                    from_dve()
                    for j in range(len(tiles)):
                        last = i == len(todo) - 1 and j == len(tiles) - 1
                        ins = mm(accs[1].t[:, 0:m.blocks], slot_hot[:, i % 2, j, :], blk_hot[:, i % 2, j, 0:m.blocks],
                                 i == 0 and j == 0, last)
                    if i < len(todo) - 1:
                        ins.then_inc(table_used, 1)
                filled(accs[1], ins, (m.name, "idx"))

            def gate_bias(m, b2):
                pe.wait_ge(gates_ready, {"L0": 1, "L2": 2, "L3": 3}[m.name])
                for q in range(NTT // 4 + 1):
                    if q < NTT // 4:
                        ring = turn[q % 2]
                        opened(ring)
                        for j in range(4):
                            ins = pe.transpose(ring.t[0:m.experts, j * P:(j + 1) * P],
                                               gates[:, 4 * q + j, 0:m.experts], ident[:, :])
                        filled(ring, ins, (m.name, "gT", q))
                    if q >= 1:
                        moved(m.name, "gT", q - 1)
                        ring = accs[(q - 1) % 2]
                        opened(ring)
                        for j in range(4):
                            ins = mm(ring.t[:, j * P:(j + 1) * P], gT[0:m.experts, (q - 1) % 2, j * P:(j + 1) * P], b2[:, :])
                        filled(ring, ins, (m.name, "gb", q - 1))

            def expert_blocks(m):
                w = weights(m)
                idx_n[0] += 1
                pe.wait_ge(idx_ready, idx_n[0])
                pe.wait_ge(experts_in[m.name], 32 * m.experts)
                expert = {}

                def rows_in(j):
                    xg_n[j % XG] += 1
                    pe.wait_ge(xg_in[j % XG], 16 * xg_n[j % XG])
                    opened(turn[j % 2])
                    filled(turn[j % 2], pe.transpose(turn[j % 2].t[:, 0:P], xg[:, j % XG, :], ident[:, :]),
                           (m.name, "xt", j))

                def up(j):
                    moved(m.name, "xt", j)
                    w1_n[0] += 1
                    pe.wait_ge(w1_ready, w1_n[0])
                    opened(wide[j % 2])
                    for c in range(NF):
                        ins = mm(wide[j % 2].t[:, 0, c * P:(c + 1) * P], w1c[:, j % 2, c * P:(c + 1) * P], xgT[:, j % 2, :])
                    filled(wide[j % 2], ins, (m.name, "up", j))

                def down(j):
                    if m.name == "L3":
                        pe.wait_ge(elu_ready, j + 1)
                    else:
                        moved(m.name, "up", j)
                    opened(accs[j % 2])
                    for c in range(NF):
                        ins = mm(accs[j % 2].t[:, 0:P], hidb[:, j % 3, c, :],
                                 w[:, bass.ds(expert[j], 1), 4 * P + c * P:4 * P + (c + 1) * P], c == 0, c == NF - 1)
                    filled(accs[j % 2], ins, (m.name, "down", j))

                for s in range(m.blocks + 3):
                    if s < m.blocks:
                        rows_in(s)
                    if 1 <= s < m.blocks + 1:
                        up(s - 1)
                    if s >= 3:
                        down(s - 3)
                    if 2 <= s < m.blocks + 2:
                        expert[s - 2] = pe.value_load(blk_e_i[0:1, s - 2:s - 1], min_val=0, max_val=m.experts - 1)

            pe.wait_ge(loaded["mix0"], n_loads["mix0"])
            for b in range(B):
                norm_turn("F0", b)
            router("L0", W["Ws0"], W["bs0"], 8)
            ranks(MIXES[0])
            block_bias(MIXES[0])
            invert(MIXES[0])
            gate_bias(MIXES[0], W["b2_0"])
            expert_blocks(MIXES[0])

            pe.wait_ge(loaded["attn1"], n_loads["attn1"])
            for b in range(B):
                norm_turn("A1", b)
                for i in range(2):
                    opened(wide[i])
                    for half in range(2):
                        ins = mm(wide[i].t[:, half, 0:HALF], W["wqkv1"][:, i * P:(i + 1) * P], xs(b, half * HALF, HALF))
                    filled(wide[i], ins, ("A1qk", b, i))
                for q in range(3):
                    ring = accs[q % 2]
                    opened(ring)
                    for j in range(4):
                        t, side = divmod(4 * q + j, 2)
                        o = ring.t[0:96, j * P:(j + 1) * P]
                        mm(o, xT[:, b, t * P + 96 * side:t * P + 96 * side + 96], W["wqkv1"][:, 2 * P:3 * P], True, False)
                        ins = mm(o, ones[:, 0:96], W["bv1"][:, :], False, True)
                    filled(ring, ins, ("A1v", b, q))
                taken(wide[0])
                taken(wide[1])
                taken(accs[0])
                taken(accs[1])

                def scores1(t, i):
                    opened(wide[i])
                    for j in range(4):
                        hd = 4 * i + j
                        ins = mm(wide[i].t[:, j // 2, (j % 2) * WIN:(j % 2 + 1) * WIN],
                                 qm[:, hd, t * P:(t + 1) * P], k1[:, t * P:t * P + WIN])
                    filled(wide[i], ins, ("S1", b, t, i))

                def turn1(t, q):
                    ring = turn[q % 2]
                    opened(ring)
                    for j in range(4):
                        hd, side = divmod(4 * q + j, 2)
                        ins = pe.transpose(ring.t[0:96, j * P:(j + 1) * P],
                                           s1[:, t % 3, hd, 96 * side:96 * side + 96], ident[:, :])
                    filled(ring, ins, ("T1", b, t, q))

                def values1(t):
                    moved("T1", b, t, 2)
                    moved("T1", b, t, 3)
                    opened(accs[0])
                    for hd in range(H1):
                        for side in range(2):
                            ins = mm(accs[0].t[:, hd * DH1:(hd + 1) * DH1], pT1[0:96, t % 2, 2 * hd + side, :],
                                     v1[0:96, t, side, hd * DH1:(hd + 1) * DH1], side == 0, side == 1)
                    filled(accs[0], ins, ("O1", b, t))

                def out_turn1(t):
                    moved("O1", b, t)
                    opened(accs[1])
                    filled(accs[1], pe.transpose(accs[1].t[:, 0:P], o1[:, :], ident[:, :]), ("OT1", b, t))

                def out_proj1(t):
                    moved("OT1", b, t)
                    opened(accs[1])
                    mm(accs[1].t[:, 0:P], oT1[:, :], W["wp1"][:, :], True, False)
                    filled(accs[1], mm(accs[1].t[:, 0:P], ones[:, :], W["bp1"][:, :], False, True), ("Y1", b, t))

                for s in range(NT + 5):
                    if s < NT:
                        scores1(s, 0)
                    if 2 <= s < NT + 2:
                        pe.wait_ge(probs_ready, b * NT + s - 1)
                        turn1(s - 2, 0)
                        turn1(s - 2, 1)
                    if 4 <= s < NT + 4:
                        out_turn1(s - 4)
                    if s < NT:
                        scores1(s, 1)
                    if 2 <= s < NT + 2:
                        turn1(s - 2, 2)
                        turn1(s - 2, 3)
                    if 3 <= s < NT + 3:
                        values1(s - 3)
                    if 4 <= s < NT + 4:
                        out_proj1(s - 4)

            for b in range(B):
                norm_turn("F1", b)
            ranks(MIXES[1])
            invert(MIXES[1])
            expert_blocks(MIXES[1])

            pe.wait_ge(loaded["attn2"], n_loads["attn2"])
            opened(accs[0])
            for c in range(16):
                ins = mm(accs[0].t[:, 0:P], W["wvT2"][:, c, :], W["wo2"][:, c, :], c == 0, c == 15)
            filled(accs[0], ins, ("wvo",))
            opened(accs[1])
            for c in range(16):
                ins = mm(accs[1].t[0:1, 0:P], W["bv2"][:, c:c + 1], W["wo2"][:, c, :], c == 0, c == 15)
            filled(accs[1], ins, ("bvo",))
            taken(accs[0])
            taken(accs[1])
            for b in range(B):
                norm_turn("A2", b)
                for i in range(2):
                    opened(wide[i])
                    for half in range(2):
                        ins = mm(wide[i].t[:, half, 0:HALF], W["wqk2"][:, i * P:(i + 1) * P], xs(b, half * HALF, HALF))
                    filled(wide[i], ins, ("A2qk", b, i))
                for half in range(2):
                    opened(accs[half])
                    for j in range(3):
                        o = accs[half].t[:, j * P:(j + 1) * P]
                        mm(o, xs(b, (3 * half + j) * P, P), wvo, True, False)
                        ins = mm(o, ones[:, :], bvo[0:1, :], False, True)
                    filled(accs[half], ins, ("A2v", b, half))
                for ring in wide + accs:
                    taken(ring)

                def scores2(t):
                    for i in range(2):
                        opened(wide[i])
                        for half in range(2):
                            ins = mm(wide[i].t[:, half, 0:SC], qk2[64 * i:64 * i + 64, 0, t * P:(t + 1) * P],
                                     qk2[64 * i:64 * i + 64, 1, half * SC:(half + 1) * SC])
                        filled(wide[i], ins, ("S2", b, t, i))

                def values2(t):
                    moved("T2", b, t, 0)
                    moved("T2", b, t, 1)
                    opened(accs[t % 2])
                    for k in range(NT):
                        mm(accs[t % 2].t[:, 0:P], pT2[:, t % 2, k, :], v2[:, k, :], k == 0, False)
                    filled(accs[t % 2], mm(accs[t % 2].t[:, 0:P], ones[:, :], W["bo2"][:, :], False, True),
                           ("O2", b, t))

                for s in range(NT + 3):
                    if s < NT:
                        scores2(s)
                    if s >= 3:
                        values2(s - 3)
                    if 2 <= s < NT + 2:
                        from_dve()
                        turn_rows(d2[:, s % 2, :], ("T2", b, s - 2))

            pe.wait_ge(loaded["mix2"], n_loads["mix2"])
            for b in range(B):
                norm_turn("F2", b)
            router("L2", W["rw2"], W["rb2"], 16)
            ranks(MIXES[2])
            block_bias(MIXES[2])
            invert(MIXES[2])
            gate_bias(MIXES[2], W["b2_2"])
            expert_blocks(MIXES[2])

            pe.wait_ge(loaded["attn3"], n_loads["attn3"])
            for b in range(B):
                norm_turn("A3", b)
                opened(wide[0])
                for half in range(2):
                    ins = mm(wide[0].t[:, half, 0:HALF], W["wqk3"][:, :], xs(b, half * HALF, HALF))
                filled(wide[0], ins, ("A3u", b))
                for half in range(2):
                    opened(accs[half])
                    for j in range(3):
                        o = accs[half].t[:, j * P:(j + 1) * P]
                        mm(o, xs(b, (3 * half + j) * P, P), W["wv3"][:, :], True, False)
                        ins = mm(o, ones[:, :], W["bv3"][:, :], False, True)
                    filled(accs[half], ins, ("A3v", b, half))
                for ring in [wide[0]] + accs:
                    taken(ring)

                def scores3(t):
                    ring, n = wide[t % 2], (t + 1) * P
                    opened(ring)
                    for half in range(2):
                        w = min(HALF, n - half * HALF)
                        if w > 0:
                            ins = mm(ring.t[:, half, 0:w], uT3[:, t * P:(t + 1) * P], xs(b, half * HALF, w))
                    filled(ring, ins, ("S3", b, t))

                def values3(t):
                    moved("T3", b, t, 0)
                    if t >= 3:
                        moved("T3", b, t, 1)
                    opened(accs[t % 2])
                    for k in range(t + 1):
                        ins = mm(accs[t % 2].t[:, 0:P], pT3[:, t % 2, k, :], v3[:, k, :], k == 0, k == t)
                    filled(accs[t % 2], ins, ("O3", b, t))

                for s in range(NT + 3):
                    if s < NT:
                        scores3(s)
                    if s >= 3:
                        values3(s - 3)
                    if 2 <= s < NT + 2:
                        pe.wait_ge(probs_ready, NTT + b * NT + s - 1)
                        turn_rows(p3[:, (s - 2) % 3, :], ("T3", b, s - 2), s - 1)

            pe.wait_ge(loaded["mix3"], n_loads["mix3"])
            for b in range(B):
                norm_turn("F3", b)
            for b in range(B):
                ring = wide[b % 2]
                opened(ring)
                for half in range(2):
                    for k in range(3):
                        ins = mm(ring.t[:, half, 0:HALF], W["rc1"][:, k, :], xs(b, half * HALF + k - 1, HALF), k == 0, k == 2)
                filled(ring, ins, ("rc1", b))
            taken(wide[0])
            taken(wide[1])
            opened(accs[0])
            for g in range(NTT):
                b, t = divmod(g, NT)
                o = accs[0].t[:, g * 10:(g + 1) * 10]
                for k in range(3):
                    mm(o, rcT[:, b, HALO + t * P + k - 1:HALO + t * P + k - 1 + P], W["rc2"][:, k, :], k == 0, False)
                ins = mm(o, ones[:, :], W["rcb2"][:, :], False, True)
            filled(accs[0], ins, ("L3", "logits"))

            def shared_up(g):
                b, half = divmod(g, 2)
                for pair in range(2):
                    opened(wide[pair])
                    for f in range(2):
                        c = 2 * pair + f
                        for k in range(9):
                            ins = mm(wide[pair].t[:, f, 0:HALF], W["sh1"][:, k, c * P:(c + 1) * P],
                                     xs(b, half * HALF + k - 4, HALF), k == 0, k == 8)
                    filled(wide[pair], ins, ("sh", g, pair))

            def shared_down(g):
                moved("sh", g, 0)
                moved("sh", g, 1)
                ring = accs[(g + 1) % 2]
                opened(ring)
                for j in range(3):
                    o = ring.t[:, j * P:(j + 1) * P]
                    for c in range(NF):
                        mm(o, hid[:, g % 2, c, j * P:(j + 1) * P], W["sh2"][:, c, :], c == 0, False)
                    ins = mm(o, ones[:, :], W["shb2"][:, :], False, True)
                filled(ring, ins, ("shy", g))

            shared_up(0)
            ranks(MIXES[3])
            shared_up(1)
            shared_down(0)
            block_bias(MIXES[3])
            invert(MIXES[3])
            for g in (2, 3, 4):
                if g < 4:
                    shared_up(g)
                shared_down(g - 1)
            gate_bias(MIXES[3], W["b2_3"])
            expert_blocks(MIXES[3])
            for g in (4, 5, 6, 7, 8):
                if g < 8:
                    shared_up(g)
                if g > 4:
                    shared_down(g - 1)

        @block.sync
        def _(sp):
            for g, dst, src in load_list:
                if g == "mix1":
                    sp.wait_ge(tables_clear, 1)
                sp.dma_start(dst, src).then_inc(loaded[g], 16)
            ys_n = [0] * XG
            xn_n = 0
            norms = 4

            def experts(m, which):
                for e in which:
                    o = weights(m)[:, e, :]
                    sp.dma_start(o[:, 0:4 * P], a[m.name + "w1"][e]).then_inc(experts_in[m.name], 16)
                    sp.dma_start(o[:, 4 * P:].rearrange("p (c n) -> p c n", c=NF),
                                 a[m.name + "w2"][e].rearrange("(c p) n -> p c n", p=P))\
                      .then_inc(experts_in[m.name], 16)

            experts(MIXES[0], range(8))
            late = {"L0": 0, "L1": 2, "L2": 1, "L3": 0}
            for i, m in enumerate(MIXES):
                if i:
                    sp.wait_ge(combined, sum(p.k * p.tiles for p in MIXES[:i]))
                    experts(m, range(late[m.name], m.experts))
                for b in range(B):
                    sp.wait_ge(xn_ready, 2 * (norms + b + 1))
                    if b == 0:
                        experts(m, range(late[m.name]))
                        if m.name in b1_in:
                            sp.dma_start(b1T[0:m.experts, :], a[m.name + "b1"]).then_inc(b1_in[m.name], 16)
                    sp.dma_start(xs_dram[b * TP:(b + 1) * TP, :].rearrange("(j p) d -> p j d", p=P),
                                 xn[:, b * NT:(b + 1) * NT, :]).then_inc(xs_out, 16)
                norms += 8
                for j in range(m.blocks):
                    sp.wait_ge(*free_of[m.name, "down", j])
                    sp.dma_start(ys_dram[j * P:(j + 1) * P, :], yo[:, j % XG, :]).then_inc(ys_out[j % XG], 16)
            for b in range(B):
                sp.wait_ge(final_ready, b + 1)
                sp.dma_start(out[b, 0:(NT - 1) * P, :].rearrange("(j p) d -> p j d", p=P),
                             h[:, b * NT:b * NT + NT - 1, :]).then_inc(out_done, 16)
                sp.dma_start(out[b, (NT - 1) * P:T, :], h[0:LAST, b * NT + NT - 1, :]).then_inc(out_done, 16)
            sp.wait_ge(out_done, 32 * B)

        @block.gpsimd
        def _(pl):
            n = [0]

            def step(ins):
                n[0] += 1
                ins.then_inc(pool_step, 1)
                pl.wait_ge(pool_step, n[0])

            step(pl.memset(ident[:, :], 0.0))
            step(pl.affine_select(out=ident[:, :], in_=ident[:, :], compare_op=ALU.not_equal, fill=1.0,
                                  base=0, pattern=[[-1, P]], channel_multiplier=1))
            step(pl.memset(onesq[:, :], 1.0))
            step(pl.memset(nhalf[:, :], -0.5))
            pl.memset(ew[:, :, :], 0.0)
            pl.memset(ei[:, :, :], 0).then_inc(tables_clear, 1)
            step(pl.memset(xT[:, :, :], 0.0))
            pl.memset(h[:, :, :], 0.0).then_inc(consts_ready, 1)

            def numbers(dst, pattern, channel_multiplier):
                step(pl.iota(dst, pattern=pattern, base=0, channel_multiplier=channel_multiplier,
                             allow_small_or_imprecise_dtypes=True))

            numbers(lane[:, :], [[1, P]], 0)
            numbers(row[:, :], [[0, 1]], 1)
            numbers(tok_id[:, :], [[P, NTT]], 1)
            step(pl.memset(before[:, :], 1.0))
            step(pl.affine_select(out=before[:, :], in_=before[:, :], compare_op=ALU.is_gt, fill=0.0,
                                  base=0, pattern=[[1, P]], channel_multiplier=-1))
            step(pl.memset(real[:, 0, :], 1.0))
            step(pl.memset(real[:, 1, :], 0.0))
            for b in range(B):
                o = real[:, 0, b * NT + NT - 1:(b + 1) * NT]
                step(pl.affine_select(out=o, in_=o, compare_op=ALU.is_gt, fill=0.0,
                                      base=LAST, pattern=[[0, 1]], channel_multiplier=-1))
            step(pl.tensor_copy(real[:, 1, 0:9], real[:, 0, 0:9]))
            o = real[:, 1, 8:9]
            step(pl.affine_select(out=o, in_=o, compare_op=ALU.is_gt, fill=0.0,
                                  base=N1 - T - 2 * P, pattern=[[0, 1]], channel_multiplier=-1))
            pl.tensor_scalar(pad_off[:, :, :], real[:, :, :], -1000.0, 1000.0, ALU.mult, ALU.add)\
              .then_inc(consts_ready, 1)

            xg_n, xg_all = [0] * XG, [0]
            rn = [0]

            def gather_blocks(m):
                xg_all[0] += 1
                pl.wait_ge(xs_out, 64 * xg_all[0])
                pl.wait_ge(idx_ready, xg_all[0])
                for j in range(m.blocks):
                    if j >= XG:
                        pl.wait_ge(*fill_of[m.name, "xt", j - XG])
                    pl.indirect_dma_start(xg[:, j % XG, :], None, xs_dram,
                                          bass.IndirectOffsetOnAxis(ap=idx[:, j:j + 1].bitcast(U32), axis=0),
                                          bounds_check=B * TP - 1, oob_is_err=False).then_inc(xg_in[j % XG], 16)

            ys_n = [0] * XG

            def results_out(m):
                for i in range(XG):
                    ys_n[i] += len(range(i, m.blocks, XG))
                    pl.wait_ge(ys_out[i], 16 * ys_n[i])

            def gather_results(m, b):
                for k in range(m.k):
                    for g in batch_tiles(m, b):
                        pl.indirect_dma_start(yg[:, k, g, :], None, ys_dram[0:m.blocks * P, :],
                                              bass.IndirectOffsetOnAxis(ap=pos_i[:, k, g:g + 1].bitcast(U32), axis=0),
                                              bounds_check=m.blocks * P - 1, oob_is_err=False)\
                          .then_inc(yg_in[m.name, b], 16)

            def rsqrt():
                rn[0] += 1
                pl.wait_ge(var_ready, rn[0])
                pl.tensor_tensor(rstd[:, :], ve[:, :], nhalf[:, :], ALU.pow).then_inc(rstd_ready, 1)

            def gathers_and_norms(m):
                results_out(m)
                gather_results(m, 0)
                rsqrt()
                gather_results(m, 1)
                gather_results(m, 2)
                rsqrt()
                gather_results(m, 3)
                rsqrt()
                rsqrt()

            for _ in range(1 + 2 * B):
                rsqrt()
            gather_blocks(MIXES[0])
            pl.wait_ge(stage_done, 3)
            step(pl.memset(k1[:, :], 0.0))
            step(pl.memset(hmask[:, :], DH1 ** -0.5))
            step(pl.affine_select(out=hmask[:, :], in_=hmask[:, :], compare_op=ALU.is_ge, fill=0.0,
                                  base=0, pattern=[[-DH1, H1]], channel_multiplier=1))
            step(pl.affine_select(out=hmask[:, :], in_=hmask[:, :], compare_op=ALU.is_ge, fill=0.0,
                                  base=DH1 - 1, pattern=[[DH1, H1]], channel_multiplier=-1))
            step(pl.memset(wmask[:, :, :], 0.0))
            step(pl.affine_select(out=wmask[:, :, :], in_=wmask[:, :, :], compare_op=ALU.is_ge, fill=NEG,
                                  base=0, pattern=[[0, 3], [1, WIN]], channel_multiplier=-1))
            step(pl.affine_select(out=wmask[:, :, :], in_=wmask[:, :, :], compare_op=ALU.is_ge, fill=NEG,
                                  base=64, pattern=[[0, 3], [-1, WIN]], channel_multiplier=1))
            step(pl.memset(wmask[:, 0, 0:32], NEG))
            pl.memset(wmask[:, 2, LAST + 32:WIN], NEG).then_inc(consts_ready, 1)
            gathers_and_norms(MIXES[0])
            for _ in range(B):
                rsqrt()
            gather_blocks(MIXES[1])
            gathers_and_norms(MIXES[1])
            for _ in range(B):
                rsqrt()
            gather_blocks(MIXES[2])
            pl.wait_ge(stage_done, 7)
            step(pl.iota(rel[:, :], pattern=[[1, TP]], base=-(NT - 1) * P, channel_multiplier=-1,
                         allow_small_or_imprecise_dtypes=True))
            step(pl.tensor_scalar(rel[:, :], rel[:, :], 0.5, None, ALU.mult))
            pl.affine_select(out=rel[:, :], in_=rel[:, :], compare_op=ALU.is_ge, fill=NEG,
                             base=(NT - 1) * P, pattern=[[-1, TP]], channel_multiplier=1).then_inc(consts_ready, 1)
            gathers_and_norms(MIXES[2])
            pl.wait_ge(stage_done, 8)
            pl.memset(rcT[:, :, :], 0.0).then_inc(consts_ready, 1)
            for _ in range(B):
                rsqrt()
            gather_blocks(MIXES[3])
            results_out(MIXES[3])
            for b in range(B):
                gather_results(MIXES[3], b)
                rsqrt()

        @block.scalar
        def _(act):
            max_n = [0]

            def evac(ring, key, dst, src, func=ACT.Copy, last=True, **kw):
                act.wait_ge(*fill_of[key])
                ins = act.activation(dst, src, func, **kw)
                if last:
                    ins.then_inc(ring.free, 1)

            def norm_turn(stage, b):
                for half in range(2):
                    n = HALF if half == 0 else T - HALF
                    evac(turn[half], (stage, "norm", b, half),
                         xT[:, b, HALO + half * HALF:HALO + half * HALF + n], turn[half].t[:, 0:n])

            def halves(x):
                return x.rearrange("p (a c) -> p a c", a=2)

            def flat(x):
                return x.rearrange("p a c -> p (a c)")

            def from_max():
                max_n[0] += 1
                act.wait_ge(max_ready, max_n[0])

            act.wait_ge(loaded["tok"], n_loads["tok"])
            for b in range(B):
                evac(wide[b % 2], ("tok", b), halves(yT[:, b, 0:T]), wide[b % 2].t[:, :, 0:SC],
                     ACT.Relu, bias=W["tokv"][:, 0:1])
            act.wait_ge(consts_ready, 1)
            for b in range(B):
                evac(turn[0], ("tokT", b, 0), flat(h[:, b * NT:b * NT + 3, :]), turn[0].t[:, 0:HALF])

            for b in range(B):
                norm_turn("A0", b)
                for c in range(NF):
                    evac(wide[c % 2], ("A0q", b, c), halves(qT[:, c, :]), wide[c % 2].t[:, :, 0:HALF],
                         scale=DH0 ** -0.5)
                N = NT * H0
                for s in range(N + 6):
                    if s < N:
                        from_max()
                        t, hd = divmod(s, H0)
                        evac(wide[s % 2], ("S0", b, s), halves(p0[:, s % 3, 0:T]), wide[s % 2].t[:, :, 0:SC],
                             ACT.Exp, bias=nm[:, t % 2, hd:hd + 1], accum_out=ssum[:, t % 2, hd:hd + 1])
                    if s >= 4 and (s - 4) % H0 == H0 - 1:
                        evac(accs[1], ("OT0", b, (s - 4) // H0), flat(oT0[:, :, :]), accs[1].t[:, :])
                    if 2 <= s < N + 2:
                        u = s - 2
                        evac(turn[0], ("T0", b, u, 0), flat(pT0[:, u % 2, 0:3, :]), turn[0].t[:, 0:HALF])

            def gate_rows(m):
                for q in range(0, NTT // 4):
                    if q >= 2:
                        act.wait_ge(*fill_of[m.name, "gb", q - 2])
                    evac(turn[q % 2], (m.name, "gT", q), gT[0:m.experts, q % 2, :], turn[q % 2].t[0:m.experts, :])

            def softmax_exp(src):
                from_max()
                act.activation(src, src, ACT.Exp).then_inc(exp_ready, 1)

            def expert_blocks(m):
                for j in range(m.blocks):
                    if j >= 3:
                        act.wait_ge(*fill_of[m.name, "down", j - 3])
                    if m.name == "L1":
                        evac(wide[j % 2], (m.name, "up", j), flat(hidb[:, j % 3, :, :]), wide[j % 2].t[:, 0, :], ACT.Gelu)
                        continue
                    for c in range(NF):
                        evac(wide[j % 2], (m.name, "up", j), hidb[:, j % 3, c, :],
                             wide[j % 2].t[:, 0, c * P:(c + 1) * P], ACT.Gelu, last=c == NF - 1,
                             bias=bias[:, c, j:j + 1])

            act.wait_ge(loaded["mix0"], n_loads["mix0"])
            for b in range(B):
                norm_turn("F0", b)
            softmax_exp(ex[:, :, 0:8])
            act.wait_ge(stage_done, 2)
            gate_rows(MIXES[0])
            act.wait_ge(idx_ready, 1)
            expert_blocks(MIXES[0])

            act.wait_ge(loaded["attn1"], n_loads["attn1"])
            act.wait_ge(consts_ready, 3)
            for b in range(B):
                norm_turn("A1", b)
                evac(wide[1], ("A1qk", b, 1), k1[:, HALO:HALO + HALF], wide[1].t[:, 0, 0:HALF],
                     ACT.Identity, last=False, bias=W["bqk1"][:, 1:2])
                evac(wide[1], ("A1qk", b, 1), k1[:, HALO + HALF:HALO + TP], wide[1].t[:, 1, 0:HALF],
                     ACT.Identity, bias=W["bqk1"][:, 1:2])
                for q in range(3):
                    evac(accs[q % 2], ("A1v", b, q), v1[0:96, 2 * q:2 * q + 2, :, :].rearrange("p a s c -> p (a s c)"),
                         accs[q % 2].t[0:96, :])
                for s in range(NT + 5):
                    if 2 <= s < NT + 2:
                        for q in (0, 2):
                            evac(turn[0], ("T1", b, s - 2, q), flat(pT1[0:96, s % 2, 4 * q:4 * q + 4, :]),
                                 turn[0].t[0:96, :])
                    if 4 <= s < NT + 4:
                        evac(accs[1], ("OT1", b, s - 4), oT1[:, :], accs[1].t[:, 0:P])
                    if s < NT:
                        from_max()
                        for hd in range(H1):
                            ins = act.activation(s1[:, s % 3, hd, :], s1[:, s % 3, hd, :], ACT.Exp,
                                                 bias=nm[:, s % 2, hd:hd + 1], accum_out=ssum[:, s % 2, hd:hd + 1])
                        ins.then_inc(probs_ready, 1)

            for b in range(B):
                norm_turn("F1", b)
            act.wait_ge(stage_done, 4)
            expert_blocks(MIXES[1])

            act.wait_ge(loaded["attn2"], n_loads["attn2"])
            act.wait_ge(stage_done, 5)
            evac(accs[0], ("wvo",), wvo[:, :], accs[0].t[:, 0:P])
            evac(accs[1], ("bvo",), bvo[0:1, :], accs[1].t[0:1, 0:P])
            from_max()
            act.activation(lamv[:, 0:2], lamv[:, 0:2], ACT.Exp).then_inc(exp_ready, 1)
            for b in range(B):
                norm_turn("A2", b)
                evac(wide[1], ("A2qk", b, 1), halves(qk2[:, 1, :]), wide[1].t[:, :, 0:HALF],
                     ACT.Identity, bias=W["bqk2"][:, 1:2])
                evac(accs[0], ("A2v", b, 0), flat(v2[:, 0:3, :]), accs[0].t[:, 0:HALF])
                for s in range(NT + 2):
                    if s < NT:
                        for i in range(2):
                            from_max()
                            evac(wide[i], ("S2", b, s, i), halves(p2[:, 2 * (s % 2) + i, 0:T]), wide[i].t[:, :, 0:SC],
                                 ACT.Exp, bias=nm[:, s % 2, i:i + 1], accum_out=ssum[:, s % 2, i:i + 1])
                    if s >= 2:
                        u = s - 2
                        evac(turn[0], ("T2", b, u, 0), flat(pT2[:, u % 2, 0:3, :]), turn[0].t[:, 0:HALF])

            act.wait_ge(loaded["mix2"], n_loads["mix2"])
            for b in range(B):
                norm_turn("F2", b)
            softmax_exp(ex[:, :, 0:16])
            act.wait_ge(stage_done, 6)
            gate_rows(MIXES[2])
            act.wait_ge(idx_ready, 3)
            expert_blocks(MIXES[2])

            act.wait_ge(stage_done, 7)
            for b in range(B):
                norm_turn("A3", b)
                evac(wide[0], ("A3u", b), halves(uT3[:, :]), wide[0].t[:, :, 0:HALF])
                evac(accs[0], ("A3v", b, 0), flat(v3[:, 0:3, :]), accs[0].t[:, 0:HALF])
                for s in range(NT + 2):
                    if s < NT:
                        from_max()
                        n = (s + 1) * P
                        act.activation(p3[:, s % 3, 0:n], s3[:, s % 2, 0:n], ACT.Exp, bias=nm[:, s % 2, 0:1],
                                       accum_out=ssum[:, s % 2, 0:1]).then_inc(probs_ready, 1)
                    if s >= 2:
                        u = s - 2
                        n = min(3, u + 1)
                        evac(turn[0], ("T3", b, u, 0), flat(pT3[:, u % 2, 0:n, :]), turn[0].t[:, 0:n * P])

            act.wait_ge(loaded["mix3"], n_loads["mix3"])
            for b in range(B):
                norm_turn("F3", b)
            act.wait_ge(stage_done, 8)
            act.wait_ge(consts_ready, 5)
            for b in range(B):
                for half in range(2):
                    n = HALF if half == 0 else T - HALF
                    evac(wide[b % 2], ("rc1", b), rcT[:, b, HALO + half * HALF:HALO + half * HALF + n],
                         wide[b % 2].t[:, half, 0:n], ACT.Gelu, last=half == 1, bias=W["rcb1"][:, 0:1])
            softmax_exp(gw[:, :, 1])

            def shared_rows(g):
                for c in range(NF):
                    evac(wide[c // 2], ("sh", g, c // 2), hid[:, g % 2, c, :], wide[c // 2].t[:, c % 2, 0:HALF],
                         ACT.Silu, last=c % 2 == 1, bias=W["shb1"][:, c:c + 1])

            for g in range(4):
                shared_rows(g)
            gate_rows(MIXES[3])
            act.wait_ge(idx_ready, 4)
            for j in range(MIXES[3].blocks):
                act.wait_ge(*fill_of["L3", "up", j])
                if j >= 2:
                    act.wait_ge(elu_ready, j - 1)
                for c in range(NF):
                    ins = act.activation(e3[:, j % 2, c, :], wide[j % 2].t[:, 0, c * P:(c + 1) * P], ACT.Exp,
                                         bias=bias[:, c, j:j + 1])
                ins.then_inc(exp_ready, 1)
            for g in range(4, 8):
                shared_rows(g)

        @block.vector
        def _(dve):
            steps, v_c, var_c, exp_c = [0], [0], [0], [0]

            def step(ins):
                steps[0] += 1
                ins.then_inc(v_step, 1)

            def settle():
                dve.wait_ge(v_step, steps[0])

            def then(ins):
                step(ins)
                settle()

            def to_pe(ins):
                v_c[0] += 1
                ins.then_inc(v_to_pe, 1)

            def settle_pe():
                dve.wait_ge(v_to_pe, v_c[0])

            def see(*key):
                dve.wait_ge(*fill_of[key])

            def moved(*key):
                dve.wait_ge(*free_of[key])

            def from_exp():
                exp_c[0] += 1
                dve.wait_ge(exp_ready, exp_c[0])

            def halves(x):
                return x.rearrange("p (a c) -> p a c", a=2)

            def flat(x):
                return x.rearrange("p a c -> p (a c)")

            def over(x, shape):
                return x.unsqueeze(len(shape) - 1).to_broadcast(shape)

            def rsqrt_var():
                var_c[0] += 1
                dve.wait_ge(rstd_ready, var_c[0])

            def norm(b, src=None, dst=None):
                src = h if src is None else src
                for t in range(NT):
                    ins = dve.bn_stats(st[:, t, :], src[:, b * NT + t, :])
                then(ins)
                for t in range(NT):
                    ins = dve.bn_aggr(mv[:, t, :], st[:, t, :])
                then(ins)
                dve.tensor_scalar(ve[:, :], mv[:, :, 1], EPS, None, ALU.add).then_inc(var_ready, 1)
                rsqrt_var()
                for t in range(NT):
                    ins = dve.tensor_scalar((xn if dst is None else dst)[:, b * NT + t, :], src[:, b * NT + t, :],
                                            mv[:, t, 0:1], rstd[:, t:t + 1], ALU.subtract, ALU.mult)
                    if dst is None and t % 3 == 2:
                        ins.then_inc(xn_ready, 1)
                if dst is not None:
                    then(ins)

            def add_tiles(acc, g, n, ring, key, src):
                see(*key)
                dve.tensor_tensor(acc[:, g:g + n, :], src, acc[:, g:g + n, :], ALU.add).then_inc(ring.free, 1)

            dve.wait_ge(consts_ready, 1)
            dve.memset(ve[:, :], 1.0)
            dve.memset(yT[:, :, T:TP], 0.0)
            dve.wait_ge(loaded["tok"], n_loads["tok"])
            for b in range(B):
                moved("tok", b)
                for half in range(2):
                    ins = dve.bn_stats(st0[:, 2 * b + half, :], yT[:, b, half * SC:(half + 1) * SC])
            then(ins)
            then(dve.bn_aggr(mv0[:, :], flat(st0[:, :, :])))
            dve.tensor_scalar(ve[:, 0:1], mv0[:, 1:2], EPS, None, ALU.add).then_inc(var_ready, 1)
            rsqrt_var()
            then(dve.tensor_tensor(sc0[:, 0:1], rstd[:, 0:1], W["tokv"][:, 1:2], ALU.mult))
            then(dve.tensor_tensor(sc0[:, 1:2], mv0[:, 0:1], sc0[:, 0:1], ALU.mult))
            then(dve.tensor_tensor(sc0[:, 2:3], W["tokv"][:, 2:3], sc0[:, 1:2], ALU.subtract))
            to_pe(dve.tensor_scalar(yT[:, :, 0:T], yT[:, :, 0:T], sc0[:, 0:1], sc0[:, 2:3], ALU.mult, ALU.add))
            for b in range(B):
                see("tokT", b, 1)
                dve.tensor_copy(flat(h[:, b * NT + 3:b * NT + 6, :]), turn[1].t[:, 0:HALF]).then_inc(turn[1].free, 1)
            for b in range(B):
                for half in range(2):
                    moved("tokT", b, half)
            dve.memset(p0[:, :, T:TP], 0.0).then_inc(stage_done, 1)

            for b in range(B):
                norm(b)
                for c in range(NF):
                    see("A0k", b, c)
                    dve.tensor_copy(halves(kT[:, c, :]), wide[c % 2].t[:, :, 0:HALF]).then_inc(wide[c % 2].free, 1)
                for c in range(3):
                    see("A0v", b, c)
                    dve.tensor_copy(v0[:, 2 * c:2 * c + 2, :], wide[c % 2].t[:, :, :]).then_inc(wide[c % 2].free, 1)
                N = NT * H0
                for s in range(N + 6):
                    if s < N:
                        t, hd = divmod(s, H0)
                        see("S0", b, s)
                        dve.tensor_reduce(nm[:, t % 2, hd:hd + 1], wide[s % 2].t[:, :, 0:SC], AX.XY, ALU.max,
                                          negate=True).then_inc(max_ready, 1)
                    if 3 <= s < N + 3 and (s - 3) % H0 == H0 - 1:
                        t = (s - 3) // H0
                        moved("S0", b, s - 3)
                        moved("S0", b, s - 4)
                        then(dve.reciprocal(rs[:, t % 2, :], ssum[:, t % 2, :]))
                        see("O0", b, t)
                        dve.tensor_tensor(o0.rearrange("p (a c) -> p a c", a=H0),
                                          accs[0].t[:, :].rearrange("p (a c) -> p a c", a=H0),
                                          over(rs[:, t % 2, :], [P, H0, DH0]), ALU.mult).then_inc(accs[0].free, 1)
                    if s >= 5 and (s - 5) % H0 == H0 - 1:
                        t = (s - 5) // H0
                        add_tiles(h, b * NT + t, 1, accs[1], ("Y0", b, t), accs[1].t[:, 0:P].unsqueeze(1))
                    if 2 <= s < N + 2:
                        u = s - 2
                        see("T0", b, u, 1)
                        dve.tensor_copy(flat(pT0[:, u % 2, 3:6, :]), turn[1].t[:, 0:HALF]).then_inc(turn[1].free, 1)
            moved("Y0", B - 1, NT - 1)
            dve.memset(nm[:, :, :], 0.0).then_inc(stage_done, 1)

            def top(stage, n_e, tiles=NTT):
                see(stage, "logits")
                dve.tensor_copy(lg[:, :, 0:n_e], accs[0].t[:, 0:NTT * n_e].rearrange("p (a c) -> p a c", a=NTT))\
                   .then_inc(accs[0].free, 1)
                moved(stage, "logits")
                for g in range(NTT):
                    ins = dve.max(m8[:, g, :], lg[:, g, 0:n_e])
                then(ins)

            def find(n_e):
                for g in range(NTT):
                    ins = dve.max_index(i8[:, g, :], m8[:, g, :], lg[:, g, 0:n_e])
                then(ins)
                then(dve.tensor_copy(i8f[:, :, :], i8[:, :, :]))

            def one_hot(dst, index, n_e, n=NTT):
                return dve.tensor_tensor(dst[:, 0:n, 0:n_e], lane[:, 0:n_e].unsqueeze(1).to_broadcast([P, n, n_e]),
                                         over(index, [P, n, n_e]), ALU.is_equal)

            def times(dst, x, col, n_e, n=NTT):
                return dve.tensor_tensor(dst[:, 0:n, 0:n_e], x[:, 0:n, 0:n_e], over(col, [P, n, n_e]), ALU.mult)

            idx_n, table_n, w1_n, comb_n = [0], [0], [0], [0]

            def by_expert(x, E):
                return x[:, 0:NTT * E].rearrange("p (g e) -> p g e", e=E)

            def choose(m):
                E = m.experts
                for k in range(m.k):
                    step(one_hot(oneh[:, k], i8f[:, :, k], E))
                settle()
                both = oneh[:, 0, :, 0:E]
                if m.k == 2:
                    then(dve.tensor_tensor(by_expert(sent, E), oneh[:, 0, :, 0:E], oneh[:, 1, :, 0:E], ALU.add))
                    both = by_expert(sent, E)
                to_pe(dve.tensor_tensor(by_expert(sent, E), both, over(real[:, 0, :], [P, NTT, E]), ALU.mult))

            def softmax_gates(m):
                E = m.experts
                from_exp()
                then(dve.tensor_reduce(gw[:, :, 0], ex[:, :, 0:E], AX.X, ALU.add))
                step(dve.reciprocal(gw[:, :, 1], gw[:, :, 0]))
                both = oneh[:, 0, :, 0:E]
                if m.k == 2:
                    then(dve.tensor_tensor(gates[:, :, 0:E], oneh[:, 0, :, 0:E], oneh[:, 1, :, 0:E], ALU.add))
                    both = gates[:, :, 0:E]
                then(dve.tensor_tensor(gates[:, :, 0:E], both, ex[:, :, 0:E], ALU.mult))
                times(gates, gates, gw[:, :, 1], E).then_inc(gates_ready, 1)

            def gate_of_choice(m, n):
                E = m.experts
                dve.wait_ge(gates_ready, n)
                for k in range(m.k):
                    then(dve.tensor_tensor(ex[:, :, 0:E], oneh[:, k, :, 0:E], gates[:, :, 0:E], ALU.mult))
                    then(dve.tensor_reduce(gw[:, :, k], ex[:, :, 0:E], AX.X, ALU.add))

            def slots(m):
                E, layer1 = m.experts, int(m.name == "L1")
                tot = wide[0].t[:, 1, 0:NTT * E].rearrange("p (b t e) -> p b t e", b=B, t=NT)
                pre4 = pre[:, 0:NTT * E].rearrange("p (b t e) -> p b t e", b=B, t=NT)
                for z in (pre4[:, :, 0, :], bpre[:, 0, 0:E], scan[:, 0, 0:16], scan[:, 1, 0:16]):
                    ins = dve.memset(z, 0.0)
                then(ins)
                see(m.name, "ranks")
                for t in range(NT - 1):
                    then(dve.tensor_tensor(pre4[:, :, t + 1, :], pre4[:, :, t, :], tot[:, :, t, :], ALU.add))
                then(dve.tensor_tensor(bsum[:, :, 0:E], pre4[:, :, NT - 1, :], tot[:, :, NT - 1, :], ALU.add))
                for b in range(B):
                    then(dve.tensor_tensor(bpre[:, b + 1, 0:E], bpre[:, b, 0:E], bsum[:, b, 0:E], ALU.add))
                then(dve.tensor_scalar(nblk_i[:, 0:E], bpre[:, B, 0:E], float(P - 1), None, ALU.add))
                then(dve.tensor_scalar(nblk_i[:, 0:E], nblk_i[:, 0:E], 7, None, ALU.logical_shift_right))
                step(dve.tensor_copy(nblk[:, 0:E], nblk_i[:, 0:E]))
                then(dve.tensor_copy(scan[:, 0, 16:16 + E], nblk_i[:, 0:E]))
                i = 0
                for sh in (1, 2, 4, 8):
                    then(dve.tensor_tensor(scan[:, 1 - i, 16:16 + E], scan[:, i, 16:16 + E],
                                           scan[:, i, 16 - sh:16 - sh + E], ALU.add))
                    i = 1 - i
                end = scan[:, i, 16:16 + E]
                then(dve.tensor_tensor(bstart[:, 0:E], end, nblk[:, 0:E], ALU.subtract))
                then(dve.scalar_tensor_tensor(out=bb[:, :, 0:E], in0=bstart[:, 0:E].unsqueeze(1).to_broadcast([P, B, E]),
                                              scalar=float(P), in1=bpre[:, 0:B, 0:E], op0=ALU.mult, op1=ALU.add))
                for b in range(B):
                    ins = dve.tensor_tensor(pre4[:, b], pre4[:, b], bb[:, b, 0:E].unsqueeze(1).to_broadcast([P, NT, E]),
                                            ALU.add)
                then(ins)
                dve.tensor_tensor(pre[:, 0:NTT * E], pre[:, 0:NTT * E], wide[0].t[:, 0, 0:NTT * E], ALU.add)\
                   .then_inc(wide[0].free, 1)
                moved(m.name, "ranks")
                K, n = m.k, 2 * NTT if m.k == 2 else NTT
                for k in range(K):
                    ins = dve.tensor_tensor(by_expert(ysent[:, k * NTT * 16:(k + 1) * NTT * 16], E), oneh[:, k, :, 0:E],
                                            by_expert(pre, E), ALU.mult)
                then(ins)
                for k in range(K):
                    ins = dve.tensor_reduce(pos[:, k * NTT:(k + 1) * NTT],
                                            by_expert(ysent[:, k * NTT * 16:(k + 1) * NTT * 16], E), AX.X, ALU.add)
                then(ins)
                if layer1:
                    then(dve.tensor_tensor(eif[:, :, 0], eif[:, :, 0], eif[:, :, 1], ALU.is_equal))
                    then(dve.tensor_tensor(pos[:, NTT:NTT + 9], pos[:, NTT:NTT + 9], eif[:, :, 0], ALU.add))
                for k in range(K):
                    ins = dve.tensor_tensor(pos_i[:, k, :], pos[:, k * NTT:(k + 1) * NTT], real[:, layer1, :], ALU.mult)
                then(ins)
                flat_i = flat(pos_i[:, :, :])[:, 0:n]
                step(dve.tensor_scalar(blk_i[:, 0:n], flat_i, 7, None, ALU.logical_shift_right))
                then(dve.tensor_scalar(slot_i[:, 0:n], flat_i, P - 1, None, ALU.bitwise_and))
                step(dve.tensor_copy(slot_f[:, 0:n], slot_i[:, 0:n]))
                for k in range(K):
                    ins = dve.tensor_tensor(blk_f[:, k * NTT:(k + 1) * NTT], blk_i[:, k * NTT:(k + 1) * NTT],
                                            pad_off[:, layer1, :], ALU.add)
                then(ins)
                g = ge_end[:, 0:m.blocks * E].rearrange("p (j e) -> p j e", e=E)
                then(dve.tensor_tensor(g, over(lane[:, 0:m.blocks], [P, m.blocks, E]),
                                       end.unsqueeze(1).to_broadcast([P, m.blocks, E]), ALU.is_ge))
                then(dve.tensor_reduce(blk_e[:, 0:m.blocks], g, AX.X, ALU.add))
                then(dve.tensor_scalar(blk_e[:, 0:m.blocks], blk_e[:, 0:m.blocks], float(E - 1), None, ALU.min))
                then(dve.tensor_copy(blk_e_i[:, 0:m.blocks], blk_e[:, 0:m.blocks]))
                if m.name != "L1":
                    to_pe(dve.tensor_scalar(blk_e[:, 0:m.blocks], blk_e[:, 0:m.blocks], row[:, 0:1], None, ALU.is_equal))

            def invert(m):
                todo = chunks(m)
                for i, (k, tiles) in enumerate(todo):
                    n, c0 = len(tiles), k * NTT + tiles[0]
                    if i >= 2:
                        dve.wait_ge(table_used, table_n[0] + i - 1)
                    dve.tensor_tensor(slot_hot[:, i % 2, 0:n, :], lane[:, :].unsqueeze(1).to_broadcast([P, n, P]),
                                      over(slot_f[:, c0:c0 + n], [P, n, P]), ALU.is_equal)
                    o = blk_hot[:, i % 2, 0:n, 0:m.blocks]
                    then(dve.tensor_tensor(o, lane[:, 0:m.blocks].unsqueeze(1).to_broadcast([P, n, m.blocks]),
                                           over(blk_f[:, c0:c0 + n], [P, n, m.blocks]), ALU.is_equal))
                    to_pe(dve.tensor_tensor(o, o, over(tok_id[:, tiles[0]:tiles[0] + n], [P, n, m.blocks]), ALU.mult))
                table_n[0] += len(todo) - 1
                if m.name != "L1":
                    see(m.name, "bias")
                    dve.tensor_copy(bias[:, :, 0:m.blocks],
                                    accs[0].t[:, 0:NF * m.blocks].rearrange("p (c j) -> p c j", c=NF))\
                       .then_inc(accs[0].free, 1)
                if m.name == "L3":
                    moved(m.name, "bias")
                    step(dve.tensor_scalar(biasm[:, :, 0:m.blocks], bias[:, :, 0:m.blocks], -1.0, None, ALU.add))
                see(m.name, "idx")
                dve.tensor_copy(idx[:, 0:m.blocks], accs[1].t[:, 0:m.blocks]).then_inc(accs[1].free, 1)
                moved(m.name, "idx")
                dve.memset(nm[:, :, :], 0.0).then_inc(idx_ready, 1)
                idx_n[0] += 1

            ys_n = [0] * XG

            def expert_blocks(m):
                w = weights(m)
                dve.wait_ge(idx_ready, idx_n[0])
                dve.wait_ge(experts_in[m.name], 32 * m.experts)
                for s in range(m.blocks + 3):
                    if s < m.blocks:
                        e = dve.value_load(blk_e_i[0:1, s:s + 1], min_val=0, max_val=m.experts - 1)
                        if s >= 2:
                            see(m.name, "up", s - 2)
                        dve.tensor_copy(w1c[:, s % 2, :], w[:, bass.ds(e, 1), 0:4 * P].rearrange("p a c -> p (a c)"))\
                           .then_inc(w1_ready, 1)
                        see(m.name, "xt", s)
                        dve.tensor_copy(xgT[:, s % 2, :], turn[s % 2].t[:, 0:P]).then_inc(turn[s % 2].free, 1)
                    if m.name == "L3" and 1 <= s < m.blocks + 1:
                        j = s - 1
                        from_exp()
                        if j >= 1:
                            dve.wait_ge(elu_ready, j)
                        for c in range(NF):
                            ins = dve.tensor_scalar(r3[:, c, :], wide[j % 2].t[:, 0, c * P:(c + 1) * P],
                                                    biasm[:, c, j:j + 1], -1.0, ALU.add, ALU.max)
                        ins.then_inc(wide[j % 2].free, 1)
                        moved(m.name, "up", j)
                        if j >= 3:
                            see(m.name, "down", j - 3)
                        dve.scalar_tensor_tensor(out=flat(hidb[:, j % 3, :, :]), in0=flat(e3[:, j % 2, :, :]),
                                                 scalar=1.0, in1=flat(r3[:, :, :]), op0=ALU.min,
                                                 op1=ALU.add).then_inc(elu_ready, 1)
                    if s >= 3:
                        j = s - 3
                        see(m.name, "down", j)
                        if ys_n[j % XG]:
                            dve.wait_ge(ys_out[j % XG], 16 * ys_n[j % XG])
                        ys_n[j % XG] += 1
                        dve.tensor_copy(yo[:, j % XG, :], accs[j % 2].t[:, 0:P]).then_inc(accs[j % 2].free, 1)
                moved(m.name, "down", m.blocks - 2)
                moved(m.name, "down", m.blocks - 1)

            def combine(m, b, acc, weight):
                tiles = batch_tiles(m, b)
                if not len(tiles):
                    return
                dve.wait_ge(yg_in[m.name, b], 16 * m.k * len(tiles))
                for k in range(m.k):
                    for g in tiles:
                        if k == 1:
                            dve.wait_ge(combined, comb_n[0] + 1 - len(tiles))
                        dve.scalar_tensor_tensor(out=acc[:, g, :], in0=yg[:, k, g, :], scalar=weight[:, g, k:k + 1],
                                                 in1=acc[:, g, :], op0=ALU.mult, op1=ALU.add).then_inc(combined, 1)
                        comb_n[0] += 1
                dve.wait_ge(combined, comb_n[0])

            def gate_bias(acc, stage):
                for q in range(NTT // 4):
                    add_tiles(acc, 4 * q, 4, accs[q % 2], (stage, "gb", q),
                              accs[q % 2].t[:, :].rearrange("p (a c) -> p a c", a=4))
                moved(stage, "gb", NTT // 4 - 2)
                moved(stage, "gb", NTT // 4 - 1)

            for b in range(B):
                norm(b)
            def route(m, n):
                E = m.experts
                top(m.name, E)
                dve.tensor_tensor(ex[:, :, 0:E], lg[:, :, 0:E], over(m8[:, :, 0], [P, NTT, E]), ALU.subtract)\
                   .then_inc(max_ready, 1)
                find(E)
                choose(m)
                softmax_gates(m)
                slots(m)
                invert(m)
                gate_of_choice(m, n)
                settle()
                gate_bias(h, m.name)
                expert_blocks(m)

            route(MIXES[0], 1)
            dve.memset(nm[:, :, :], 0.0).then_inc(stage_done, 1)

            dve.wait_ge(loaded["attn1"], n_loads["attn1"])
            dve.wait_ge(consts_ready, 3)
            for b in range(B):
                combine(MIXES[0], b, h, gw)
                norm(b)
                see("A1qk", b, 0)
                for hd in range(H1):
                    ins = dve.tensor_scalar(halves(qm[:, hd, :]), wide[0].t[:, :, 0:HALF], W["bqk1"][:, 0:1],
                                            hmask[:, hd:hd + 1], ALU.add, ALU.mult)
                ins.then_inc(wide[0].free, 1)
                def turned(t, q):
                    see("T1", b, t, q)
                    dve.tensor_copy(flat(pT1[0:96, t % 2, 4 * q:4 * q + 4, :]), turn[1].t[0:96, :])\
                       .then_inc(turn[1].free, 1)

                for s in range(NT + 5):
                    if 2 <= s < NT + 2:
                        dve.wait_ge(probs_ready, b * NT + s - 1)
                        then(dve.reciprocal(rs1[:, (s - 2) % 4, :], ssum[:, s % 2, :]))
                    if s < NT:
                        mask = wmask[:, 0 if s == 0 else 2 if s == NT - 1 else 1, :]
                        for i in range(2):
                            if i == 1 and s >= 2:
                                turned(s - 2, 1)
                            see("S1", b, s, i)
                            for j in range(2):
                                ins = dve.tensor_tensor(
                                    s1[:, s % 3, 4 * i + 2 * j:4 * i + 2 * j + 2, :],
                                    wide[i].t[:, j, 0:HALF].rearrange("p (a c) -> p a c", a=2),
                                    mask.unsqueeze(1).to_broadcast([P, 2, WIN]), ALU.add)
                            ins.then_inc(wide[i].free, 1)
                        moved("S1", b, s, 0)
                        moved("S1", b, s, 1)
                        dve.tensor_reduce(nm[:, s % 2, :], s1[:, s % 3, :, :], AX.X, ALU.max, negate=True)\
                           .then_inc(max_ready, 1)
                    if NT <= s < NT + 2:
                        turned(s - 2, 1)
                    if 2 <= s < NT + 2:
                        turned(s - 2, 3)
                    if 3 <= s < NT + 3:
                        t = s - 3
                        see("O1", b, t)
                        dve.tensor_tensor(o1.rearrange("p (a c) -> p a c", a=H1),
                                          accs[0].t[:, 0:P].rearrange("p (a c) -> p a c", a=H1),
                                          over(rs1[:, t % 4, :], [P, H1, DH1]), ALU.mult).then_inc(accs[0].free, 1)
                    if 4 <= s < NT + 4:
                        t = s - 4
                        add_tiles(h, b * NT + t, 1, accs[1], ("Y1", b, t), accs[1].t[:, 0:P].unsqueeze(1))
            moved("Y1", B - 1, NT - 1)
            dve.memset(nm[:, :, :], 0.0).then_inc(stage_done, 1)

            for b in range(B):
                norm(b)
            dve.wait_ge(loaded["mix1"], n_loads["mix1"])
            then(dve.tensor_copy(eif[:, :, :], ei[:, :, :]))
            step(dve.memset(oneh[:, :, :, :], 0.0))
            then(dve.memset(sent[:, :], 0.0))
            for k in range(2):
                then(one_hot(oneh[:, k], eif[:, :, k], 8, 9))
            then(dve.tensor_tensor(by_expert(sent, 8)[:, 0:9], oneh[:, 0, 0:9, 0:8], oneh[:, 1, 0:9, 0:8], ALU.add))
            to_pe(dve.tensor_tensor(by_expert(sent, 8)[:, 0:9], by_expert(sent, 8)[:, 0:9],
                                    over(real[:, 1, 0:9], [P, 9, 8]), ALU.mult))
            slots(MIXES[1])
            invert(MIXES[1])
            expert_blocks(MIXES[1])
            dve.memset(nm[:, :, :], 0.0).then_inc(stage_done, 1)

            dve.wait_ge(loaded["attn2"], n_loads["attn2"])
            dve.memset(d2[:, :, T:TP], 0.0)
            for i in range(2):
                ins = dve.tensor_tensor(W["lam"][:, 2 * i, :], W["lam"][:, 2 * i, :], W["lam"][:, 2 * i + 1, :], ALU.mult)
            then(ins)
            dve.tensor_reduce(lamv[:, 0:2], W["lam"][:, 0:4:2, :], AX.X, ALU.add).then_inc(max_ready, 1)
            from_exp()
            then(dve.tensor_tensor(lamv[:, 2:3], lamv[:, 1:2], lamv[:, 0:1], ALU.subtract))
            then(dve.tensor_scalar(lamv[:, 3:4], lamv[:, 2:3], -(0.8 - 0.6 * math.exp(-0.3 * 0)), None, ALU.add))
            for b in range(B):
                combine(MIXES[1], b, h, ew)
                norm(b)
                see("A2qk", b, 0)
                dve.tensor_scalar(halves(qk2[:, 0, :]), wide[0].t[:, :, 0:HALF], W["bqk2"][:, 0:1], 0.25,
                                  ALU.add, ALU.mult).then_inc(wide[0].free, 1)
                see("A2v", b, 1)
                dve.tensor_copy(flat(v2[:, 3:6, :]), accs[1].t[:, 0:HALF]).then_inc(accs[1].free, 1)
                for s in range(NT + 3):
                    if s < NT:
                        for i in range(2):
                            see("S2", b, s, i)
                            dve.tensor_reduce(nm[:, s % 2, i:i + 1], wide[i].t[:, :, 0:SC], AX.XY, ALU.max,
                                              negate=True).then_inc(max_ready, 1)
                    if 1 <= s < NT + 1:
                        t = s - 1
                        moved("S2", b, t, 0)
                        moved("S2", b, t, 1)
                        then(dve.reciprocal(rs[:, t % 2, 0:2], ssum[:, t % 2, 0:2]))
                        then(dve.tensor_tensor(rs[:, t % 2, 2:3], rs[:, t % 2, 1:2], lamv[:, 3:4], ALU.mult))
                        then(dve.tensor_scalar(p2[:, 2 * (t % 2) + 1, 0:T], p2[:, 2 * (t % 2) + 1, 0:T],
                                               rs[:, t % 2, 2:3], None, ALU.mult))
                        to_pe(dve.scalar_tensor_tensor(out=d2[:, t % 2, 0:T], in0=p2[:, 2 * (t % 2), 0:T],
                                                       scalar=rs[:, t % 2, 0:1], in1=p2[:, 2 * (t % 2) + 1, 0:T],
                                                       op0=ALU.mult, op1=ALU.add))
                    if s >= 3:
                        t = s - 3
                        add_tiles(h, b * NT + t, 1, accs[t % 2], ("O2", b, t), accs[t % 2].t[:, 0:P].unsqueeze(1))
                    if 2 <= s < NT + 2:
                        t = s - 2
                        see("T2", b, t, 1)
                        dve.tensor_copy(flat(pT2[:, t % 2, 3:6, :]), turn[1].t[:, 0:HALF]).then_inc(turn[1].free, 1)
            moved("O2", B - 1, NT - 2)
            moved("O2", B - 1, NT - 1)
            dve.memset(nm[:, :, :], 0.0).then_inc(stage_done, 1)

            for b in range(B):
                norm(b)
            route(MIXES[2], 2)
            dve.memset(nm[:, :, :], 0.0).then_inc(stage_done, 1)

            dve.wait_ge(consts_ready, 4)
            for b in range(B):
                combine(MIXES[2], b, h, gw)
                norm(b)
                see("A3v", b, 1)
                dve.tensor_copy(flat(v3[:, 3:6, :]), accs[1].t[:, 0:HALF]).then_inc(accs[1].free, 1)
                for s in range(NT + 3):
                    if 2 <= s < NT + 2:
                        dve.wait_ge(probs_ready, NTT + b * NT + s - 1)
                        then(dve.reciprocal(rs1[:, (s - 2) % 4, 0:1], ssum[:, s % 2, 0:1]))
                    if s < NT:
                        see("S3", b, s)
                        if b * NT + s >= 2:
                            dve.wait_ge(probs_ready, NTT + b * NT + s - 1)
                        n, off = (s + 1) * P, (NT - 1 - s) * P
                        for half in range(2):
                            lo, hi = half * HALF, min((half + 1) * HALF, n)
                            if lo < hi:
                                ins = dve.scalar_tensor_tensor(
                                    out=s3[:, s % 2, lo:hi], in0=wide[s % 2].t[:, half, 0:hi - lo], scalar=P ** -0.5,
                                    in1=rel[:, off + lo:off + hi], op0=ALU.mult, op1=ALU.add)
                        ins.then_inc(wide[s % 2].free, 1)
                        moved("S3", b, s)
                        dve.tensor_reduce(nm[:, s % 2, 0:1], s3[:, s % 2, 0:n], AX.X, ALU.max, negate=True)\
                           .then_inc(max_ready, 1)
                    if s >= 3:
                        t = s - 3
                        see("O3", b, t)
                        dve.scalar_tensor_tensor(out=h[:, b * NT + t, :], in0=accs[t % 2].t[:, 0:P],
                                                 scalar=rs1[:, t % 4, 0:1], in1=h[:, b * NT + t, :],
                                                 op0=ALU.mult, op1=ALU.add).then_inc(accs[t % 2].free, 1)
                    if 5 <= s < NT + 2:
                        t = s - 2
                        see("T3", b, t, 1)
                        dve.tensor_copy(flat(pT3[:, t % 2, 3:t + 1, :]), turn[1].t[:, 0:(t - 2) * P])\
                           .then_inc(turn[1].free, 1)
            moved("O3", B - 1, NT - 2)
            moved("O3", B - 1, NT - 1)
            dve.memset(nm[:, :, :], 0.0).then_inc(stage_done, 1)

            dve.wait_ge(loaded["mix3"], n_loads["mix3"])
            for b in range(B):
                norm(b)
            m = MIXES[3]
            top("L3", 10)
            dve.tensor_tensor(gw[:, :, 1], m8[:, :, 1], m8[:, :, 0], ALU.subtract).then_inc(max_ready, 1)
            find(10)
            choose(m)
            from_exp()
            then(dve.tensor_scalar(gw[:, :, 0], gw[:, :, 1], 1.0, None, ALU.add))
            then(dve.reciprocal(gw[:, :, 0], gw[:, :, 0]))
            then(dve.tensor_tensor(gw[:, :, 1], gw[:, :, 1], gw[:, :, 0], ALU.mult))
            step(times(gates, oneh[:, 0], gw[:, :, 0], 10))
            then(times(ex, oneh[:, 1], gw[:, :, 1], 10))
            dve.tensor_tensor(gates[:, :, 0:10], gates[:, :, 0:10], ex[:, :, 0:10], ALU.add).then_inc(gates_ready, 1)
            slots(m)
            dve.wait_ge(xs_out, 64 * len(MIXES))

            def shared_sum(g):
                add_tiles(xn, 3 * g, 3, accs[(g + 1) % 2], ("shy", g),
                          accs[(g + 1) % 2].t[:, 0:HALF].rearrange("p (a c) -> p a c", a=3))

            shared_sum(0)
            invert(m)
            for g in range(1, 4):
                shared_sum(g)
            for g in range(4):
                moved("shy", g)
            gate_bias(xn, "L3")
            expert_blocks(m)
            for b in range(B):
                if b >= 2:
                    for g in (2 * b, 2 * b + 1):
                        shared_sum(g)
                    for g in (2 * b, 2 * b + 1):
                        moved("shy", g)
                combine(m, b, xn, gw)
                norm(b, xn, zt)
                z = zt[:, b * NT:(b + 1) * NT, :]
                then(dve.tensor_tensor(z, z, W["lng"][:, :].unsqueeze(1).to_broadcast([P, NT, P]), ALU.mult))
                then(dve.tensor_tensor(z, z, W["lnb"][:, :].unsqueeze(1).to_broadcast([P, NT, P]), ALU.add))
                dve.tensor_tensor(h[:, b * NT:(b + 1) * NT, :], h[:, b * NT:(b + 1) * NT, :], z, ALU.add)\
                   .then_inc(final_ready, 1)


def kernel(**inputs):
    import numpy as _np
    import concourse.bacc as _bacc
    from concourse import mybir as _mybir
    from concourse.bass_utils import run_bass_kernel_spmd as _run

    x = {k: _np.asarray(v) for k, v in inputs.items()}

    def cols(v, n=1):
        return v.reshape(n, -1).T

    qkv = x["L1_attn_b_qkv"]
    lay = {
        "x": x["x"].transpose(0, 2, 1),
        "tokW": x["L0_tok_W"].T,
        "tokv": _np.stack([x["L0_tok_b"], x["L0_tok_gamma"], x["L0_tok_beta"]], axis=1),
        "wq": x["L0_attn_w_q"], "wk": x["L0_attn_w_k"], "wv": x["L0_attn_w_v"],
        "wo": x["L0_attn_w_out"].reshape(4, 128, 128).transpose(1, 0, 2),
        "bo": x["L0_attn_b_out"][None],
        "Ws0": x["L0_ffn_Ws"], "bs0": x["L0_ffn_bs"][None],
        "L0b1": x["L0_ffn_b1"], "b2_0": x["L0_ffn_b2"],
        "L0w1": x["L0_ffn_W1"], "L0w2": x["L0_ffn_W2"],
        "wqkv1": x["L1_attn_W_qkv"], "bqk1": cols(qkv[:256], 2), "bv1": qkv[None, 256:],
        "wp1": x["L1_attn_W_proj"], "bp1": x["L1_attn_b_proj"][None],
        "ei": x["L1_ffn_expert_indices"], "ew": x["L1_ffn_expert_weights"],
        "L1w1": x["L1_ffn_w1"], "L1w2": x["L1_ffn_w2"],
        "wqk2": x["L2_attn_Wqkv"], "bqk2": cols(x["L2_attn_bqkv"], 2),
        "wvT2": x["L2_attn_Wv"].T.reshape(16, 128, 128).transpose(1, 0, 2),
        "bv2": cols(x["L2_attn_bv"], 16),
        "wo2": x["L2_attn_Wo"].reshape(16, 128, 128).transpose(1, 0, 2),
        "bo2": x["L2_attn_bo"][None],
        "lam": _np.stack([x["L2_attn_lq1"], x["L2_attn_lk1"], x["L2_attn_lq2"], x["L2_attn_lk2"]]),
        "rw2": x["L2_ffn_router_w"].T, "rb2": x["L2_ffn_router_b"][None],
        "L2b1": x["L2_ffn_b1"], "b2_2": x["L2_ffn_b2"],
        "L2w1": x["L2_ffn_w1"].transpose(0, 2, 1), "L2w2": x["L2_ffn_w2"].transpose(0, 2, 1),
        "wqk3": x["L3_attn_W_qk"], "wv3": x["L3_attn_W_v"].T, "bv3": x["L3_attn_b_v"][None],
        "rc1": x["L3_ffn_rc_w1"].transpose(1, 2, 0), "rcb1": cols(x["L3_ffn_rc_b1"]),
        "rc2": x["L3_ffn_rc_w2"].transpose(1, 2, 0), "rcb2": x["L3_ffn_rc_b2"][None],
        "sh1": x["L3_ffn_sh_w1"].transpose(1, 2, 0), "shb1": cols(x["L3_ffn_sh_b1"], 4),
        "sh2": x["L3_ffn_sh_w2"][:, :, 0].T.reshape(4, 128, 128).transpose(1, 0, 2),
        "shb2": x["L3_ffn_sh_b2"][None],
        "L3b1": x["L3_ffn_e_b1"], "b2_3": x["L3_ffn_e_b2"],
        "L3w1": x["L3_ffn_e_w1"], "L3w2": x["L3_ffn_e_w2"],
        "lng": x["L3_ffn_ln_g"], "lnb": x["L3_ffn_ln_b"],
    }
    nc = _bacc.Bacc("TRN2", target_bir_lowering=False, num_devices=1)
    arrays, aps = {}, {}
    for name, v in lay.items():
        v = _np.ascontiguousarray(v)
        arrays[f"in_{name}"] = v
        aps[name] = nc.dram_tensor(f"in_{name}", v.shape, _mybir.dt.from_np(v.dtype), kind="ExternalInput").ap()
    out = nc.dram_tensor("out", (B, T, P), _mybir.dt.float32, kind="ExternalOutput").ap()
    xs = nc.dram_tensor("xs", (B * TP, P), _mybir.dt.float32, kind="Internal").ap()
    ys = nc.dram_tensor("ys", (MAXB * P, P), _mybir.dt.float32, kind="Internal").ap()
    build(nc, aps, xs, ys, out)
    r = _run(nc, [arrays], core_ids=[0])
    return r.results[0]["out"]
```

```python
import math
from contextlib import ExitStack

import concourse.bass as bass
from concourse import mybir

F32 = mybir.dt.float32
F16 = mybir.dt.float16
BF16 = mybir.dt.bfloat16
I32 = mybir.dt.int32
U32 = mybir.dt.uint32
ALU = mybir.AluOpType
ACT = mybir.ActivationFunctionType
AX = mybir.AxisListType

P = 128
B, T_IN, D_IN, CTX = 4, 750, 23, 5
T = T_IN - CTX + 1
NT = 6
TP = NT * P
NTT = B * NT
LAST = T - (NT - 1) * P
HALF = 3 * P
SC = T // 2
HALO = 32
XW = HALO + TP + HALO
H0, DH0 = 8, 64
H1, DH1, WIN = 8, 16, 192
NF = 4
AREA = 24 * 1024
EW = 1024
EPS = 1e-5
NEG = -1e30


NORMS = []
for _l in range(4):
    NORMS.append((f"A{_l}", 0))
    for _b in range(B):
        if _b >= 1 and _l == 0:
            NORMS.append((f"F{_l}", _b - 1))
        if _b < B - 1:
            NORMS.append((f"A{_l}", _b + 1))
        if _b >= 1 and _l >= 1 and not (_l == 1 and _b - 1 > 1):
            NORMS.append((f"F{_l}", _b - 1))
    if _l != 1:
        NORMS.append((f"F{_l}", B - 1))


def norm_count(stage, b):
    return NORMS.index((stage, b)) + 1


V0_PARTS = [(0, 0), (0, 1), (1, 0), (0, 2), (1, 1), (2, 0), (1, 2), (2, 1), (2, 2)]
V0_RESTS = [(1, 0), (1, 1), (2, 0), (1, 2), (2, 1), (2, 2)]

SIDE = {"A0": ((6, 8, 10, 12, 14), (20, 22, 24))}
STREAM = {"A1": ((4, 5, 7), (1, 2, 4)), "A2": ((3, 4, 6, 7, 8), (1, 2, 4)), "A3": ((3, 4, 6), (2, 3, 4))}
PROJECT = NT - 1


def side_jobs(stage, b, s):
    jobs = []
    if stage in STREAM:
        steps_f, steps_a = STREAM[stage]
        todo = [(steps_a, stage, q, s - (q - 1) * NT) for q in range(1, B)]
        todo += [(steps_f, "F" + stage[1], q, s - (q + 1) * NT) for q in range(B - 1)]
    else:
        todo = [(SIDE[stage][0], "F" + stage[1], b - 1, s), (SIDE[stage][1], stage, b + 1, s)]
    for steps, what, q, at in todo:
        if (what, q) in NORMS and at in steps and 0 <= q and (what[0] == "A" or q < B - 1):
            jobs.append((steps.index(at), what, q))
    return jobs


class Mix:

    def __init__(self, name, experts, k, tiles, tokens):
        self.name, self.experts, self.k, self.tiles = name, experts, k, tiles
        self.blocks = (k * tokens + (P - 1) * experts) // P
        self.base = AREA - experts * EW


MIXES = [Mix("L0", 8, 1, NTT, B * T), Mix("L1", 8, 2, 9, 1024),
         Mix("L2", 16, 2, NTT, B * T), Mix("L3", 10, 2, NTT, B * T)]
MID = B * TP // 2
MAXB = max(m.blocks for m in MIXES)
GB = 4
XG = 4


class Ring:

    def __init__(self, nc, ctx, name, shape):
        self.t = ctx.enter_context(nc.psum_tensor(name, shape, F32))
        self.full = ctx.enter_context(nc.semaphore(name + "_full"))
        self.free = ctx.enter_context(nc.semaphore(name + "_free"))
        self.fills = 0


def build(nc, a, xs_dram, ys_dram, out):
    ctx = ExitStack()
    with ctx:
        def sb(name, shape, dt=F32):
            return ctx.enter_context(nc.sbuf_tensor(name, shape, dt))

        def sem(name):
            return ctx.enter_context(nc.semaphore(name))

        wide = [Ring(nc, ctx, f"wide{i}", [P, 2, 512]) for i in range(2)]
        turn = [Ring(nc, ctx, f"turn{i}", [P, 512]) for i in range(2)]
        accs = [Ring(nc, ctx, f"accs{i}", [P, 512]) for i in range(2)]

        h = sb("h", [P, NTT, P])
        xn = sb("xn", [P, NTT, P])
        xT = sb("xT", [P, B, XW])
        ident = sb("ident", [P, P])
        onesq = sb("onesq", [P, P])
        ones = onesq[0:1, :]
        ident16 = sb("ident16", [P, P], BF16)
        before = sb("before", [P, P])
        lane = sb("lane", [P, P])
        row = sb("row", [P, 1])
        tok_id = sb("tok_id", [P, NTT], F16)
        lane16 = sb("lane16", [P, P], F16)
        real = sb("real", [P, 2, NTT])
        pad_off = sb("pad_off", [P, 2, NTT])
        nhalf = sb("nhalf", [P, NT])

        WSHAPES = {
            "tokW": [CTX * D_IN, P], "tokv": [P, 3],
            "wq": [P, H0 * DH0], "wk": [P, H0 * DH0], "wv": [P, H0 * DH0], "wo": [P, NF, P],
            "bo": [1, P],
            "Ws0": [P, 8], "bs0": [8, 1], "b2_0": [8, P],
            "wqkv1": [P, 3 * P], "bqk1": [P, 2], "bv1": [1, P], "wp1": [P, P], "bp1": [1, P],
            "wqk2": [P, 2 * P], "bqk2": [P, 2], "wvT2": [P, 16, P], "bv2": [P, 16],
            "wo2": [P, 16, P], "bo2": [1, P], "lam": [P, 4, 16],
            "rw2": [P, 16], "rb2": [16, 1], "b2_2": [16, P],
            "wqk3": [P, P], "wv3": [P, P], "bv3": [1, P],
            "rc1": [P, 3, P], "rcb1": [P, 1], "rc2": [P, 3, 10], "rcb2": [10, 1],
            "sh1": [P, 9, 4 * P], "shb1": [P, NF], "sh2": [P, NF, P], "shb2": [1, P],
            "b2_3": [10, P], "lng": [P, P], "lnb": [P, P],
        }
        W = {k: sb("w_" + k, s) for k, s in WSHAPES.items()}

        shared = sb("shared", [P, AREA])
        used = [0]

        def part(n, *dims):
            v = shared[:, used[0]:used[0] + n]
            used[0] += n
            assert used[0] <= AREA
            if len(dims) == 2:
                v = v.rearrange("p (a b) -> p a b", a=dims[0])
            if len(dims) == 3:
                v = v.rearrange("p (a b c) -> p a b c", a=dims[0], b=dims[1])
            return v

        st = sb("st", [P, NT, 6])
        mv = sb("mv", [P, NT, 2])
        ve = sb("ve", [P, NT])
        rstd = sb("rstd", [P, NT])
        nm = sb("nm", [P, 2, 8])
        ssum = sb("ssum", [P, 2, 8])
        rs = sb("rs", [P, 2, 8])
        rs1 = sb("rs1", [P, 4, 8])
        lg = sb("lg", [P, NTT, 16])
        lgT = sb("lgT", [16, TP])
        ex = sb("ex", [P, NTT, 16])
        oneh = sb("oneh", [P, 2, NTT, 16])
        gates = sb("gates", [P, NTT, 16])
        m8 = sb("m8", [P, NTT, 8])
        i8 = sb("i8", [P, NTT, 8], U32)
        i8f = sb("i8f", [P, NTT, 8])
        gw = sb("gw", [P, NTT, 2])
        ei = sb("ei", [P, 9, 2], I32)
        eif = sb("eif", [P, 9, 2])
        pos_i = sb("pos_i", [P, 2, NTT], I32)
        ew = sb("ew", [P, 9, 2])
        lamv = sb("lamv", [P, 4])

        patches, yT = part(B * T, B, T), part(B * TP, B, TP)
        st0, mv0, sc0 = part(48, 8, 6), part(2), part(8)
        used[0] = 0
        qT, kT = part(4 * TP, 4, TP), part(4 * TP, 4, TP)
        v0 = part(NT * 512 * 3 // 2).bitcast(BF16).rearrange("p (t k c) -> p t k c", t=NT, k=3)
        p0 = part(3 * TP, 3, TP)
        pT0 = part(3 * TP // 2).bitcast(F16).rearrange("p (a b c) -> p a b c", a=3, b=NT)
        pT0r = part(3 * TP // 2).bitcast(F16).rearrange("p (a b c) -> p a b c", a=3, b=NT)
        used[0] += 56
        masks_at = used[0]
        hmask, bq8 = part(H1), part(H1)
        wmask2 = part(3 * WIN).bitcast(BF16).rearrange("p (m a c) -> p m a c", m=3, a=2)
        masks_end = used[0]
        assert masks_end <= MIXES[0].base
        o0, oT0 = part(512), part(512, NF, P)
        v0r = part(NT * 512, 3, 2, 512)
        used[0] = 2 * 4096
        wmask = part(3 * WIN, 3, WIN)
        used[0] = 0
        qm = part(H1 * TP, H1, TP)
        k1 = part(XW)
        v1 = [part(NT * 2 * P * 3 // 2).bitcast(BF16).rearrange("p (q s h k d) -> p q s h k d", q=3, s=4, h=H1, k=3)
              for _ in range(2)]
        v1r = part(3 * 4 * P, 3, 4 * P)
        pT1 = part(2 * H1 * P).bitcast(F16).rearrange("p (a b c) -> p a b c", a=2, b=2 * H1)
        assert used[0] <= masks_at
        used[0] = masks_end
        pT1r = part(2 * H1 * P).bitcast(F16).rearrange("p (a b c) -> p a b c", a=2, b=2 * H1)
        s1 = part(2 * H1 * WIN).rearrange("p (s a b) -> p s a b", s=2, a=H1)
        o1, oT1 = part(P), part(P)
        assert used[0] <= AREA - NTT * P
        used[0] = 0
        qk2 = part(4 * TP).rearrange("p (b a c) -> p b a c", b=2, a=2)
        v2 = part(2 * TP, 2, NT, P)
        p2 = part(4 * TP, 4, TP)
        d2 = part(2 * TP, 2, TP)
        pT2 = part(2 * TP, 2, NT, P)
        wvo, bvo = part(P), part(P)
        used[0] = 0
        uT3, v3 = part(2 * TP, 2, TP), part(2 * TP, 2, NT, P)
        s3, p3 = part(2 * TP, 2, TP), part(3 * TP, 3, TP)
        pT3 = part(2 * TP, 2, NT, P)
        rel = part(TP)
        used[0] = 0
        b1T = part(4 * P)
        slot_hot = part(NT * P).bitcast(F16).rearrange("p (a b c) -> p a b c", a=2, b=NT)
        blk_hot = part(NT * MAXB).bitcast(F16).rearrange("p (a b c) -> p a b c", a=2, b=NT)
        used[0] -= NT * (P + MAXB)
        w1c = part(2 * 4 * P, 2, 4 * P)
        e3, r3 = part(2 * NF * P, 2, NF, P), part(NF * P, NF, P)
        ge_end = shared[:, used[0] - 1536:used[0] - 1536 + MAXB * 16]
        sent, pre = part(NTT * 16), part(NTT * 16)
        used[0] -= 2 * NTT * 16
        yo = part(XG * P, XG, P)
        used[0] += 2 * NTT * 16 - XG * P
        ysent = part(2 * NTT * 16)
        used[0] -= 2 * NTT * 16
        gT = part(2 * 4 * P, 2, 4 * P)
        bsum, bpre, bb = part(4 * 16, 4, 16), part(5 * 16, 5, 16), part(4 * 16, 4, 16)
        scan = part(2 * 32, 2, 32)
        nblk, bstart, blk_e = part(16), part(16), part(MAXB)
        pos = part(2 * NTT)
        slot_f, blk_f = sb("slot_f", [P, 2 * NTT], F16), sb("blk_f", [P, 2 * NTT], F16)
        bias = part(NF * MAXB, NF, MAXB)
        biasm = part(NF * MAXB, NF, MAXB)
        xg, xgT = part(XG * P, XG, P), part(2 * P, 2, P)
        hidb = part(3 * NF * P, 3, NF, P)
        assert used[0] <= MIXES[2].base, used[0]
        used[0] -= 3 * NF * P
        hid = part(2 * NF * HALF, 2, NF, HALF)
        rcT = part(B * XW, B, XW)
        assert used[0] <= MIXES[3].base, used[0]
        nblk_i, slot_i, blk_i = sb("nblk_i", [P, 16], I32), sb("slot_i", [P, 2 * NTT], I32), sb("blk_i", [P, 2 * NTT], I32)
        blk_e_i = sb("blk_e_i", [P, MAXB], I32)
        idx = sb("idx", [P, MAXB], I32)
        used[0] = AREA - 2 * NTT * P
        yg = part(2 * NTT * P, 2, NTT, P)
        zt = yg[:, 0]

        loaded = {k: sem("ld_" + k) for k in
                  ("patch", "tok", "attn0", "mix0", "attn1", "mix1", "attn2", "mix2", "attn3", "mix3")}
        experts_in = {m.name: sem("experts_in_" + m.name) for m in MIXES}
        b1_in = {k: sem("b1_in_" + k) for k in ("L0", "L2", "L3")}
        xs_out = sem("xs_out")
        xg_in = [sem(f"xg_in{i}") for i in range(XG)]
        ys_out = [sem(f"ys_out{i}") for i in range(XG)]
        yg_in = {(m.name, b, k): sem(f"yg_in_{m.name}_{b}_{k}") for m in MIXES for b in range(B) for k in range(m.k)}
        combined = sem("combined")
        idx_ready = sem("idx_ready")
        gates_ready = sem("gates_ready")
        table_used = sem("table_used")
        w1_ready = sem("w1_ready")
        final_ready = sem("final_ready")
        consts_ready = sem("consts_ready")
        pool_step = sem("pool_step")
        rstd_ready = sem("rstd_ready")
        var_ready = sem("var_ready")
        xn_ready = sem("xn_ready")
        v_step = sem("v_step")
        v_to_pe = sem("v_to_pe")
        probs_ready = sem("probs_ready")
        elu_ready = sem("elu_ready")
        max_ready = sem("max_ready")
        exp_ready = sem("exp_ready")
        v0_part = sem("v0_part")
        v0_rest = sem("v0_rest")
        p0_ready = sem("p0_ready")
        parts_ready = sem("parts_ready")
        bq8_ready = sem("bq8_ready")
        heads_ready = sem("heads_ready")
        v1_ready = sem("v1_ready")
        tables_clear = sem("tables_clear")
        stage_done = sem("stage_done")
        out_done = sem("out_done")

        fill_of = {}
        parts_at = {}
        free_of = {}

        def group(dst, loads):
            return [(dst, o, i) for o, i in loads]

        load_list = (
            group("patch", [(patches[k * D_IN:(k + 1) * D_IN, :, :],
                             a["x"].rearrange("b d t -> d b t")[:, :, k:k + T]) for k in range(CTX)])
            + group("tok", [(W[k][:, :], a[k]) for k in ("tokW", "tokv")])
            + group("attn0", [(W[k][:], a[k]) for k in ("wq", "wk", "wv", "wo", "bo")])
            + group("mix0", [(W[k][:], a[k]) for k in ("Ws0", "bs0", "b2_0")])
            + group("attn1", [(W[k][:], a[k]) for k in ("wqkv1", "bqk1", "bv1", "wp1", "bp1")])
            + group("attn2", [(W[k][:], a[k]) for k in
                              ("wqk2", "bqk2", "wvT2", "bv2", "wo2", "bo2")]
                    + [(W["lam"][:], a["lam"].partition_broadcast(P))])
            + group("mix2", [(W[k][:], a[k]) for k in ("rw2", "rb2", "b2_2")])
            + group("attn3", [(W[k][:], a[k]) for k in ("wqk3", "wv3", "bv3")])
            + group("mix3", [(W[k][:], a[k]) for k in
                             ("rc1", "rcb1", "rc2", "rcb2", "sh1", "shb1", "sh2", "shb2", "b2_3")]
                    + [(W[k][:], a[k].partition_broadcast(P)) for k in ("lng", "lnb")])
        )
        N1 = a["ei"].shape[0]
        for dst, src in ((ei, a["ei"]), (ew, a["ew"])):
            load_list += group("mix1", [
                (dst[:, 0:5, :], src[0:640].rearrange("(j p) k -> p j k", p=P)),
                (dst[0:LAST, 5, :], src[640:T]),
                (dst[:, 6:8, :], src[T:T + 256].rearrange("(j p) k -> p j k", p=P)),
                (dst[0:N1 - T - 256, 8, :], src[T + 256:N1])])

        def weights(m):
            return shared[:, m.base:AREA].rearrange("p (e n) -> p e n", e=m.experts)

        seqs = [[b for b in range(B) if (f"F{i}", b) in NORMS] for i in range(len(MIXES))]

        def batch_tiles(m, b):
            return range(b * NT, min((b + 1) * NT, m.tiles))

        def chunks(m):
            return [(k, list(batch_tiles(m, b))) for k in range(m.k) for b in range(B) if len(batch_tiles(m, b))]

        n_loads = {k: 16 * sum(g == k for g, _, _ in load_list) for k in loaded}

        block = ctx.enter_context(nc.Block())

        @block.tensor
        def _(pe):
            v_n = [0]

            def opened(ring):
                if ring.fills:
                    pe.wait_ge(ring.free, ring.fills)

            def filled(ring, ins, key=None):
                ins.then_inc(ring.full, 1)
                ring.fills += 1
                fill_of[key] = (ring.full, ring.fills)
                free_of[key] = (ring.free, ring.fills)

            def taken(ring):
                pe.wait_ge(ring.free, ring.fills)

            def moved(*key):
                pe.wait_ge(*free_of[key])

            def from_dve():
                v_n[0] += 1
                pe.wait_ge(v_to_pe, v_n[0])

            def rows(t):
                return LAST if t == NT - 1 else P

            def mm(o, l, r, start=True, stop=True):
                return pe.matmul(o, l, r, start=start, stop=stop)

            def norm_turn(stage, b):
                for half in range(2):
                    pe.wait_ge(xn_ready, 2 * norm_count(stage, b) - 1 + half)
                    opened(turn[half])
                    for j in range(3):
                        ins = pe.transpose(turn[half].t[:, j * P:(j + 1) * P],
                                           xn[:, b * NT + 3 * half + j, :], ident[:, :])
                    filled(turn[half], ins, (stage, "norm", b, half))

            def turned(stage, b):
                for half in range(2):
                    moved(stage, "norm", b, half)

            def logits_in(stage, q):
                m = MIXES[int(stage[1])]
                turned(stage, q)
                for half in range(2):
                    opened(turn[half])
                    ins = mm(turn[half].t[0:m.experts, 0:HALF], W["Ws0" if m.name == "L0" else "rw2"][:, :],
                             xs(q, half * HALF, HALF))
                    filled(turn[half], ins, (stage, "lgT", q, half))

            def logits_turn(stage, q):
                m = MIXES[int(stage[1])]
                moved(stage, "lgT", q, 0)
                moved(stage, "lgT", q, 1)
                opened(turn[0])
                for t in range(NT):
                    ins = pe.transpose(turn[0].t[:, t * m.experts:(t + 1) * m.experts],
                                       lgT[0:m.experts, t * P:(t + 1) * P], ident[0:m.experts, 0:m.experts])
                filled(turn[0], ins, (stage, "lg", q))

            def side_turns(stage, b, s):
                for phase, what, q in side_jobs(stage, b, s):
                    if phase == 2:
                        norm_turn(what, q)
                    if phase == 3:
                        logits_in(what, q)
                    if phase == 4:
                        logits_turn(what, q)

            def xs(b, t0, n):
                return xT[:, b, HALO + t0:HALO + t0 + n]

            def turn_rows(src, key, n=NT):
                for half in range(2):
                    tiles = range(3 * half, min(3 * half + 3, n))
                    if not len(tiles):
                        continue
                    opened(turn[half])
                    for j in tiles:
                        ins = pe.transpose(turn[half].t[:, (j - 3 * half) * P:(j - 3 * half + 1) * P],
                                           src[:, j * P:(j + 1) * P], ident[:, :])
                    filled(turn[half], ins, key + (half,))

            pe.wait_ge(loaded["patch"], n_loads["patch"])
            pe.wait_ge(loaded["tok"], n_loads["tok"])
            for b in range(B):
                ring = wide[b % 2]
                opened(ring)
                for half in range(2):
                    ins = mm(ring.t[:, half, 0:SC], W["tokW"][:, :], patches[0:CTX * D_IN, b, half * SC:(half + 1) * SC])
                filled(ring, ins, ("tok", b))
            pe.wait_ge(consts_ready, 1)
            from_dve()
            for b in range(B):
                turn_rows(yT[:, b, :], ("tokT", b))

            pe.wait_ge(loaded["attn0"], n_loads["attn0"])
            pe.wait_ge(loaded["mix0"], n_loads["mix0"])
            for b in range(B):
                if b == 0:
                    norm_turn("A0", 0)
                turned("A0", b)
                n = 0
                for c in range(3):
                    ring = wide[n % 2]
                    opened(ring)
                    for half in range(2):
                        ins = mm(ring.t[:, half, :], xs(b, (2 * c + half) * P, P), W["wv"][:, :])
                    filled(ring, ins, ("A0v", b, c))
                    n += 1
                for nm_, w in (("q", "wq"), ("k", "wk")):
                    for c in range(NF):
                        ring = wide[n % 2]
                        opened(ring)
                        for half in range(2):
                            ins = mm(ring.t[:, half, 0:HALF], W[w][:, c * P:(c + 1) * P], xs(b, half * HALF, HALF))
                        filled(ring, ins, ("A0" + nm_, b, c))
                        n += 1
                taken(wide[0])
                taken(wide[1])
                N = NT * H0

                def scores(u):
                    t, hd = divmod(u, H0)
                    ring, r0 = wide[u % 2], DH0 * (hd % 2)
                    opened(ring)
                    for half in range(2):
                        ins = mm(ring.t[:, half, 0:SC], qT[r0:r0 + DH0, hd // 2, t * P:(t + 1) * P],
                                 kT[r0:r0 + DH0, hd // 2, half * SC:(half + 1) * SC])
                    filled(ring, ins, ("S0", b, u))

                def values(u):
                    t, hd = divmod(u, H0)
                    moved("T0", b, u, 0)
                    moved("T0", b, u, 1)
                    if hd == 0:
                        opened(accs[t % 2])
                    if u == 0:
                        pe.wait_ge(v0_part, len(V0_PARTS) * (b + 1))
                    for k in range(NT):
                        for x, i in ((pT0, 0), (pT0, 1), (pT0, 2), (pT0r, 0), (pT0r, 1)):
                            ins = mm(accs[t % 2].t[:, hd * DH0:(hd + 1) * DH0], x[:, u % 3, k, :],
                                     v0[:, k, i, hd * DH0:(hd + 1) * DH0], k == 0 and x is pT0 and i == 0,
                                     k == NT - 1 and x is pT0r and i == 1)
                    if hd == H0 - 1:
                        filled(accs[t % 2], ins, ("O0", b, t))

                def out_turn(t):
                    moved("O0", b, t)
                    opened(accs[t % 2])
                    for c in range(NF):
                        ins = pe.transpose(accs[t % 2].t[:, c * P:(c + 1) * P], o0[:, c * P:(c + 1) * P], ident[:, :])
                    filled(accs[t % 2], ins, ("OT0", b, t))

                def out_proj(t):
                    moved("OT0", b, t)
                    opened(accs[t % 2])
                    for c in range(NF):
                        mm(accs[t % 2].t[:, 0:P], oT0[:, c, :], W["wo"][:, c, :], c == 0, False)
                    filled(accs[t % 2], mm(accs[t % 2].t[:, 0:P], ones[:, :], W["bo"][:, :], False, True), ("Y0", b, t))

                for s in range(N + 7):
                    if s < N:
                        scores(s)
                    if 2 <= s < N + 2:
                        moved("S0", b, s - 2)
                        turn_rows(p0[:, (s - 2) % 3, :], ("T0", b, s - 2))
                    if s >= 5 and (s - 5) % H0 == H0 - 1:
                        out_turn((s - 5) // H0)
                    if s >= 6 and (s - 6) % H0 == H0 - 1:
                        out_proj((s - 6) // H0)
                    if 4 <= s < N + 4:
                        values(s - 4)
                    side_turns("A0", b, s)

            chunk_n, w1_n, idx_n = [0], [0], [0]
            xg_n = [0] * XG

            def ranks(m):
                from_dve()
                opened(wide[0])
                mm(wide[0].t[:, 0, 0:NTT * m.experts], before[:, :], sent[:, 0:NTT * m.experts])
                filled(wide[0], mm(wide[0].t[:, 1, 0:NTT * m.experts], onesq[:, :], sent[:, 0:NTT * m.experts]),
                       (m.name, "ranks"))

            def block_bias(m):
                from_dve()
                pe.wait_ge(b1_in[m.name], 16)
                opened(accs[0])
                for c in range(NF):
                    ins = mm(accs[0].t[:, c * m.blocks:(c + 1) * m.blocks], b1T[0:m.experts, c * P:(c + 1) * P],
                             blk_e[0:m.experts, 0:m.blocks])
                filled(accs[0], ins, (m.name, "bias"))

            def invert(m, beside=lambda i: None):
                opened(accs[1])
                todo = chunks(m)
                for i, (k, tiles) in enumerate(todo):
                    from_dve()
                    for j in range(len(tiles)):
                        last = i == len(todo) - 1 and j == len(tiles) - 1
                        ins = mm(accs[1].t[:, 0:m.blocks], slot_hot[:, i % 2, j, :], blk_hot[:, i % 2, j, 0:m.blocks],
                                 i == 0 and j == 0, last)
                    if i < len(todo) - 1:
                        ins.then_inc(table_used, 1)
                        beside(i)
                filled(accs[1], ins, (m.name, "idx"))

            def gate_bias(m, b2, s):
                q = s - GB
                if q == 0:
                    pe.wait_ge(gates_ready, {"L0": 1, "L2": 2, "L3": 3}[m.name])
                if 0 <= q < NTT // 4:
                    ring = turn[(s + 1) % 2]
                    opened(ring)
                    for j in range(4):
                        ins = pe.transpose(ring.t[0:m.experts, j * P:(j + 1) * P],
                                           gates[:, 4 * q + j, 0:m.experts], ident[:, :])
                    filled(ring, ins, (m.name, "gT", q))
                if 1 <= q < NTT // 4 + 1:
                    moved(m.name, "gT", q - 1)
                    ring = accs[s % 2]
                    opened(ring)
                    for j in range(4):
                        ins = mm(ring.t[:, j * P:(j + 1) * P], gT[0:m.experts, (q - 1) % 2, j * P:(j + 1) * P], b2[:, :])
                    filled(ring, ins, (m.name, "gb", q - 1))

            def expert_blocks(m, b2=None):
                w = weights(m)
                idx_n[0] += 1
                pe.wait_ge(idx_ready, idx_n[0])
                pe.wait_ge(experts_in[m.name], 32 * m.experts)
                expert = {}

                def rows_in(j):
                    xg_n[j % XG] += 1
                    pe.wait_ge(xg_in[j % XG], 16 * xg_n[j % XG])
                    opened(turn[j % 2])
                    filled(turn[j % 2], pe.transpose(turn[j % 2].t[:, 0:P], xg[:, j % XG, :], ident[:, :]),
                           (m.name, "xt", j))

                def up(j):
                    moved(m.name, "xt", j)
                    w1_n[0] += 1
                    pe.wait_ge(w1_ready, w1_n[0])
                    opened(wide[j % 2])
                    for c in range(NF):
                        ins = mm(wide[j % 2].t[:, 0, c * P:(c + 1) * P], w1c[:, j % 2, c * P:(c + 1) * P], xgT[:, j % 2, :])
                    filled(wide[j % 2], ins, (m.name, "up", j))

                def down(j):
                    if m.name == "L3":
                        pe.wait_ge(elu_ready, j + 1)
                    else:
                        moved(m.name, "up", j)
                    opened(accs[j % 2])
                    for c in range(NF):
                        ins = mm(accs[j % 2].t[:, 0:P], hidb[:, j % 3, c, :],
                                 w[:, bass.ds(expert[j], 1), 4 * P + c * P:4 * P + (c + 1) * P], c == 0, c == NF - 1)
                    filled(accs[j % 2], ins, (m.name, "down", j))

                for s in range(m.blocks + 3):
                    if s < m.blocks:
                        rows_in(s)
                    if 1 <= s < m.blocks + 1:
                        up(s - 1)
                    if s >= 3:
                        down(s - 3)
                    if b2 is not None:
                        gate_bias(m, b2, s)
                    if 2 <= s < m.blocks + 2:
                        expert[s - 2] = pe.value_load(blk_e_i[0:1, s - 2:s - 1], min_val=0, max_val=m.experts - 1)

            norm_turn("F0", B - 1)
            for b in range(B):
                turned("F0", b)
            logits_in("F0", B - 1)
            logits_turn("F0", B - 1)
            ranks(MIXES[0])
            block_bias(MIXES[0])
            invert(MIXES[0])
            expert_blocks(MIXES[0], W["b2_0"])

            pe.wait_ge(loaded["attn1"], n_loads["attn1"])
            pe.wait_ge(consts_ready, 4)

            def project1(b):
                turned("A1", b)
                for i in range(2):
                    opened(wide[i])
                    for half in range(2):
                        ins = mm(wide[i].t[:, half, 0:HALF], W["wqkv1"][:, i * P:(i + 1) * P], xs(b, half * HALF, HALF))
                    filled(wide[i], ins, ("A1qk", b, i))
                for q in range(3):
                    ring = accs[q % 2]
                    opened(ring)
                    for j in range(4):
                        t, side = divmod(4 * q + j, 2)
                        o = ring.t[0:96, j * P:(j + 1) * P]
                        mm(o, xT[:, b, t * P + 96 * side:t * P + 96 * side + 96], W["wqkv1"][:, 2 * P:3 * P], True, False)
                        ins = mm(o, ones[:, 0:96], W["bv1"][:, :], False, True)
                    filled(ring, ins, ("A1v", b, q))

            def scores1(b, t, i):
                if t == 0:
                    moved("A1qk", b, 0)
                    moved("A1qk", b, 1)
                opened(wide[i])
                for j in range(4):
                    hd = 4 * i + j
                    if j % 2 == 0:
                        mm(wide[i].t[:, j // 2, 0:2 * WIN], ident16[:, :],
                           wmask2[:, 0 if t == 0 else 2 if t == NT - 1 else 1, :, :].rearrange("p a c -> p (a c)"),
                           True, False)
                    ins = mm(wide[i].t[:, j // 2, (j % 2) * WIN:(j % 2 + 1) * WIN],
                             qm[:, hd, t * P:(t + 1) * P], k1[:, t * P:t * P + WIN], False, j % 2 == 1)
                filled(wide[i], ins, ("S1", b, t, i))

            def turn1(b, t, q):
                ring = turn[q % 2]
                opened(ring)
                for j in range(4):
                    hd, side = divmod(4 * q + j, 2)
                    ins = pe.transpose(ring.t[0:96, j * P:(j + 1) * P],
                                       s1[:, t % 2, hd, 96 * side:96 * side + 96], ident[:, :])
                filled(ring, ins, ("T1", b, t, q))

            def values1(b, t):
                moved("T1", b, t, 2)
                moved("T1", b, t, 3)
                if t == 0:
                    pe.wait_ge(v1_ready, b + 1)
                opened(accs[0])
                for hd in range(H1):
                    o = accs[0].t[:, 3 * hd * DH1:3 * (hd + 1) * DH1]
                    for side in range(2):
                        q, i = divmod(2 * t + side, 4)
                        v = v1[b % 2][0:96, q, i, hd, :, :].rearrange("p k d -> p (k d)")
                        mm(o, pT1[0:96, t % 2, 2 * hd + side, :], v, side == 0, False)
                        ins = mm(o[:, 0:2 * DH1], pT1r[0:96, t % 2, 2 * hd + side, :], v[:, 0:2 * DH1], False, side == 1)
                filled(accs[0], ins, ("O1", b, t))

            def out_turn1(b, t):
                moved("O1", b, t)
                opened(accs[1])
                filled(accs[1], pe.transpose(accs[1].t[:, 0:P], o1[:, :], ident[:, :]), ("OT1", b, t))

            def out_proj1(b, t):
                moved("OT1", b, t)
                opened(accs[1])
                mm(accs[1].t[:, 0:P], oT1[:, :], W["wp1"][:, :], True, False)
                filled(accs[1], mm(accs[1].t[:, 0:P], ones[:, :], W["bp1"][:, :], False, True), ("Y1", b, t))

            norm_turn("A1", 0)
            project1(0)
            for s in range(NTT + 4):
                side_turns("A1", None, s)
                if s < NTT:
                    scores1(*divmod(s, NT), 0)
                if 2 <= s < NTT + 2:
                    before_last = divmod(s - 2, NT)
                    moved("S1", *before_last, 0)
                    moved("S1", *before_last, 1)
                    turn1(*before_last, 0)
                    turn1(*before_last, 1)
                if s >= 4:
                    out_turn1(*divmod(s - 4, NT))
                if s < NTT:
                    scores1(*divmod(s, NT), 1)
                if 2 <= s < NTT + 2:
                    turn1(*before_last, 2)
                    turn1(*before_last, 3)
                if 3 <= s < NTT + 3:
                    values1(*divmod(s - 3, NT))
                if s >= 4:
                    out_proj1(*divmod(s - 4, NT))
                if s % NT == PROJECT and s < NTT - NT:
                    project1(s // NT + 1)

            for b in range(2):
                turned("F1", b)
            ranks(MIXES[1])
            invert(MIXES[1])
            expert_blocks(MIXES[1])

            pe.wait_ge(loaded["attn2"], n_loads["attn2"])
            pe.wait_ge(loaded["mix2"], n_loads["mix2"])
            opened(accs[0])
            for c in range(16):
                ins = mm(accs[0].t[:, 0:P], W["wvT2"][:, c, :], W["wo2"][:, c, :], c == 0, c == 15)
            filled(accs[0], ins, ("wvo",))
            opened(accs[1])
            for c in range(16):
                ins = mm(accs[1].t[0:1, 0:P], W["bv2"][:, c:c + 1], W["wo2"][:, c, :], c == 0, c == 15)
            filled(accs[1], ins, ("bvo",))
            taken(accs[0])
            taken(accs[1])
            def project2(b):
                turned("A2", b)
                for i in range(2):
                    opened(wide[i])
                    for half in range(2):
                        ins = mm(wide[i].t[:, half, 0:HALF], W["wqk2"][:, i * P:(i + 1) * P], xs(b, half * HALF, HALF))
                    filled(wide[i], ins, ("A2qk", b, i))
                for half in range(2):
                    opened(accs[half])
                    for j in range(3):
                        o = accs[half].t[:, j * P:(j + 1) * P]
                        mm(o, xs(b, (3 * half + j) * P, P), wvo, True, False)
                        ins = mm(o, ones[:, :], bvo[0:1, :], False, True)
                    filled(accs[half], ins, ("A2v", b, half))

            def scores2(b, t):
                if t == 0:
                    for i in range(2):
                        moved("A2qk", b, i)
                for i in range(2):
                    opened(wide[i])
                    for half in range(2):
                        ins = mm(wide[i].t[:, half, 0:SC], qk2[64 * i:64 * i + 64, b % 2, 0, t * P:(t + 1) * P],
                                 qk2[64 * i:64 * i + 64, b % 2, 1, half * SC:(half + 1) * SC])
                    filled(wide[i], ins, ("S2", b, t, i))

            def values2(b, t):
                if t == 0:
                    for half in range(2):
                        moved("A2v", b, half)
                moved("T2", b, t, 0)
                moved("T2", b, t, 1)
                opened(accs[t % 2])
                for k in range(NT):
                    mm(accs[t % 2].t[:, 0:P], pT2[:, t % 2, k, :], v2[:, b % 2, k, :], k == 0, False)
                filled(accs[t % 2], mm(accs[t % 2].t[:, 0:P], ones[:, :], W["bo2"][:, :], False, True),
                       ("O2", b, t))

            norm_turn("A2", 0)
            project2(0)
            for s in range(NTT + 3):
                if s < NTT:
                    scores2(*divmod(s, NT))
                if 2 <= s < NTT + 2:
                    from_dve()
                    turn_rows(d2[:, s % 2, :], ("T2", *divmod(s - 2, NT)))
                if s >= 3:
                    values2(*divmod(s - 3, NT))
                if s % NT == PROJECT and s < NTT - NT:
                    project2(s // NT + 1)
                side_turns("A2", None, s)

            norm_turn("F2", B - 1)
            for b in range(B):
                turned("F2", b)
            logits_in("F2", B - 1)
            logits_turn("F2", B - 1)
            ranks(MIXES[2])
            block_bias(MIXES[2])
            invert(MIXES[2])
            expert_blocks(MIXES[2], W["b2_2"])

            pe.wait_ge(loaded["attn3"], n_loads["attn3"])
            def project3(b):
                turned("A3", b)
                opened(wide[0])
                for half in range(2):
                    ins = mm(wide[0].t[:, half, 0:HALF], W["wqk3"][:, :], xs(b, half * HALF, HALF))
                filled(wide[0], ins, ("A3u", b))
                for half in range(2):
                    opened(accs[half])
                    for j in range(3):
                        o = accs[half].t[:, j * P:(j + 1) * P]
                        mm(o, xs(b, (3 * half + j) * P, P), W["wv3"][:, :], True, False)
                        ins = mm(o, ones[:, :], W["bv3"][:, :], False, True)
                    filled(accs[half], ins, ("A3v", b, half))

            def scores3(b, t):
                if t == 0:
                    moved("A3u", b)
                ring, n = wide[t % 2], (t + 1) * P
                opened(ring)
                for half in range(2):
                    w = min(HALF, n - half * HALF)
                    if w > 0:
                        ins = mm(ring.t[:, half, 0:w], uT3[:, b % 2, t * P:(t + 1) * P], xs(b, half * HALF, w))
                filled(ring, ins, ("S3", b, t))

            def values3(b, t):
                if t == 0:
                    for half in range(2):
                        moved("A3v", b, half)
                moved("T3", b, t, 0)
                if t >= 3:
                    moved("T3", b, t, 1)
                opened(accs[t % 2])
                for k in range(t + 1):
                    ins = mm(accs[t % 2].t[:, 0:P], pT3[:, t % 2, k, :], v3[:, b % 2, k, :], k == 0, k == t)
                filled(accs[t % 2], ins, ("O3", b, t))

            norm_turn("A3", 0)
            project3(0)
            for s in range(NTT + 3):
                if s < NTT:
                    scores3(*divmod(s, NT))
                if 2 <= s < NTT + 2:
                    b, t = divmod(s - 2, NT)
                    pe.wait_ge(probs_ready, s - 1)
                    turn_rows(p3[:, t % 3, :], ("T3", b, t), t + 1)
                if s >= 3:
                    values3(*divmod(s - 3, NT))
                if s % NT == PROJECT and s < NTT - NT:
                    project3(s // NT + 1)
                side_turns("A3", None, s)

            pe.wait_ge(loaded["mix3"], n_loads["mix3"])
            norm_turn("F3", B - 1)
            for b in range(B):
                turned("F3", b)
            for b in range(B):
                ring = wide[b % 2]
                opened(ring)
                for half in range(2):
                    for k in range(3):
                        ins = mm(ring.t[:, half, 0:HALF], W["rc1"][:, k, :], xs(b, half * HALF + k - 1, HALF), k == 0, k == 2)
                filled(ring, ins, ("rc1", b))
            taken(wide[0])
            taken(wide[1])
            for b in range(B):
                for half in range(2):
                    opened(turn[half])
                    for k in range(3):
                        ins = mm(turn[half].t[0:10, 0:HALF], W["rc2"][:, k, :],
                                 rcT[:, b, HALO + half * HALF + k - 1:HALO + half * HALF + k - 1 + HALF], k == 0, k == 2)
                    filled(turn[half], ins, ("F3", "lgT", b, half))
                logits_turn("F3", b)

            def shared_piece(g, c):
                b, half = divmod(g, 2)
                pair, f = divmod(c, 2)
                if f == 0:
                    opened(wide[pair])
                for k in range(9):
                    ins = mm(wide[pair].t[:, f, 0:HALF], W["sh1"][:, k, c * P:(c + 1) * P],
                             xs(b, half * HALF + k - 4, HALF), k == 0, k == 8)
                if f == 1:
                    filled(wide[pair], ins, ("sh", g, pair))

            def shared_up(g):
                for c in range(NF):
                    shared_piece(g, c)

            def shared_down(g):
                moved("sh", g, 0)
                moved("sh", g, 1)
                ring = accs[(g + 1) % 2]
                opened(ring)
                for j in range(3):
                    o = ring.t[:, j * P:(j + 1) * P]
                    for c in range(NF):
                        mm(o, hid[:, g % 2, c, j * P:(j + 1) * P], W["sh2"][:, c, :], c == 0, False)
                    ins = mm(o, ones[:, :], W["shb2"][:, :], False, True)
                filled(ring, ins, ("shy", g))

            shared_up(0)
            ranks(MIXES[3])
            shared_up(1)
            shared_down(0)
            block_bias(MIXES[3])
            invert(MIXES[3], lambda i: shared_piece(2, i) if i < NF else None)
            shared_down(1)
            shared_up(3)
            shared_down(2)
            shared_down(3)
            expert_blocks(MIXES[3], W["b2_3"])
            for g in (4, 5, 6, 7, 8):
                if g < 8:
                    shared_up(g)
                if g > 4:
                    shared_down(g - 1)

        @block.sync
        def _(sp):
            for g, dst, src in load_list:
                if g == "mix1":
                    sp.wait_ge(tables_clear, 1)
                sp.dma_start(dst, src).then_inc(loaded[g], 16)
            ys_n = [0] * XG

            def experts(m, which):
                for e in which:
                    o = weights(m)[:, e, :]
                    sp.dma_start(o[:, 0:4 * P], a[m.name + "w1"][e]).then_inc(experts_in[m.name], 16)
                    sp.dma_start(o[:, 4 * P:].rearrange("p (c n) -> p c n", c=NF),
                                 a[m.name + "w2"][e].rearrange("(c p) n -> p c n", p=P))\
                      .then_inc(experts_in[m.name], 16)

            late = {"L0": 4, "L1": 5, "L2": 3, "L3": 0}

            def after_attention(i, m):
                sp.wait_ge(stage_done, 2 * i + 2)
                experts(m, range(late[m.name]))
                if m.name in b1_in:
                    sp.dma_start(b1T[0:m.experts, :], a[m.name + "b1"]).then_inc(b1_in[m.name], 16)

            experts(MIXES[0], range(late["L0"], 8))
            for i, m in enumerate(MIXES):
                if i:
                    sp.wait_ge(combined, sum(p.k * p.tiles for p in MIXES[:i]))
                    experts(m, range(late[m.name], m.experts))
                for b in seqs[i]:
                    if b == B - 1:
                        after_attention(i, m)
                    sp.wait_ge(xn_ready, 2 * norm_count(f"F{i}", b))
                    sp.dma_start(xs_dram[b * TP:(b + 1) * TP, :].rearrange("(j p) d -> p j d", p=P),
                                 xn[:, b * NT:(b + 1) * NT, :]).then_inc(xs_out, 16)
                if B - 1 not in seqs[i]:
                    after_attention(i, m)
                for j in range(m.blocks):
                    sp.wait_ge(*free_of[m.name, "down", j])
                    sp.dma_start(ys_dram[j * P:(j + 1) * P, :], yo[:, j % XG, :]).then_inc(ys_out[j % XG], 16)
            for b in range(B):
                sp.wait_ge(final_ready, b + 1)
                sp.dma_start(out[b, 0:(NT - 1) * P, :].rearrange("(j p) d -> p j d", p=P),
                             h[:, b * NT:b * NT + NT - 1, :]).then_inc(out_done, 16)
                sp.dma_start(out[b, (NT - 1) * P:T, :], h[0:LAST, b * NT + NT - 1, :]).then_inc(out_done, 16)
            sp.wait_ge(out_done, 32 * B)

        @block.gpsimd
        def _(pl):
            n = [0]

            def step(ins):
                n[0] += 1
                ins.then_inc(pool_step, 1)
                pl.wait_ge(pool_step, n[0])

            step(pl.memset(ident[:, :], 0.0))
            step(pl.affine_select(out=ident[:, :], in_=ident[:, :], compare_op=ALU.not_equal, fill=1.0,
                                  base=0, pattern=[[-1, P]], channel_multiplier=1))
            step(pl.tensor_copy(ident16[:, :], ident[:, :]))
            step(pl.memset(onesq[:, :], 1.0))
            step(pl.memset(nhalf[:, :], -0.5))
            pl.memset(ew[:, :, :], 0.0)
            pl.memset(ei[:, :, :], 0).then_inc(tables_clear, 1)
            step(pl.memset(xT[:, :, :], 0.0))
            pl.memset(h[:, :, :], 0.0).then_inc(consts_ready, 1)

            def numbers(dst, pattern, channel_multiplier):
                step(pl.iota(dst, pattern=pattern, base=0, channel_multiplier=channel_multiplier,
                             allow_small_or_imprecise_dtypes=True))

            numbers(lane[:, :], [[1, P]], 0)
            numbers(row[:, :], [[0, 1]], 1)
            step(pl.iota(tok_id[:, :], pattern=[[P, NTT]], base=-MID, channel_multiplier=1,
                         allow_small_or_imprecise_dtypes=True))
            step(pl.tensor_copy(lane16[:, :], lane[:, :]))
            step(pl.memset(before[:, :], 1.0))
            step(pl.affine_select(out=before[:, :], in_=before[:, :], compare_op=ALU.is_gt, fill=0.0,
                                  base=0, pattern=[[1, P]], channel_multiplier=-1))
            step(pl.memset(real[:, 0, :], 1.0))
            step(pl.memset(real[:, 1, :], 0.0))
            for b in range(B):
                o = real[:, 0, b * NT + NT - 1:(b + 1) * NT]
                step(pl.affine_select(out=o, in_=o, compare_op=ALU.is_gt, fill=0.0,
                                      base=LAST, pattern=[[0, 1]], channel_multiplier=-1))
            step(pl.tensor_copy(real[:, 1, 0:9], real[:, 0, 0:9]))
            o = real[:, 1, 8:9]
            step(pl.affine_select(out=o, in_=o, compare_op=ALU.is_gt, fill=0.0,
                                  base=N1 - T - 2 * P, pattern=[[0, 1]], channel_multiplier=-1))
            pl.tensor_scalar(pad_off[:, :, :], real[:, :, :], -1000.0, 1000.0, ALU.mult, ALU.add)\
              .then_inc(consts_ready, 1)

            step(pl.memset(hmask[:, :], DH1 ** -0.5))
            step(pl.affine_select(out=hmask[:, :], in_=hmask[:, :], compare_op=ALU.is_ge, fill=0.0,
                                  base=0, pattern=[[-DH1, H1]], channel_multiplier=1))
            step(pl.affine_select(out=hmask[:, :], in_=hmask[:, :], compare_op=ALU.is_ge, fill=0.0,
                                  base=DH1 - 1, pattern=[[DH1, H1]], channel_multiplier=-1))
            step(pl.memset(wmask[:, :, :], 0.0))
            step(pl.affine_select(out=wmask[:, :, :], in_=wmask[:, :, :], compare_op=ALU.is_ge, fill=NEG,
                                  base=0, pattern=[[0, 3], [1, WIN]], channel_multiplier=-1))
            step(pl.affine_select(out=wmask[:, :, :], in_=wmask[:, :, :], compare_op=ALU.is_ge, fill=NEG,
                                  base=64, pattern=[[0, 3], [-1, WIN]], channel_multiplier=1))
            step(pl.memset(wmask[:, 0, 0:32], NEG))
            step(pl.memset(wmask[:, 2, LAST + 32:WIN], NEG))
            pl.tensor_copy(wmask2, wmask.unsqueeze(2).to_broadcast([P, 3, 2, WIN])).then_inc(consts_ready, 1)

            xg_n, xg_all = [0] * XG, [0]
            rn = [0]

            def gather_blocks(m):
                xg_all[0] += 1
                pl.wait_ge(xs_out, 16 * sum(len(q) for q in seqs[:xg_all[0]]))
                pl.wait_ge(idx_ready, xg_all[0])
                for j in range(m.blocks):
                    if j >= XG:
                        pl.wait_ge(*fill_of[m.name, "xt", j - XG])
                    pl.indirect_dma_start(xg[:, j % XG, :], None, xs_dram,
                                          bass.IndirectOffsetOnAxis(ap=idx[:, j:j + 1].bitcast(U32), axis=0),
                                          bounds_check=B * TP - 1, oob_is_err=False).then_inc(xg_in[j % XG], 16)

            ys_n = [0] * XG

            def results_out(m):
                for i in range(XG):
                    ys_n[i] += len(range(i, m.blocks, XG))
                    pl.wait_ge(ys_out[i], 16 * ys_n[i])

            def gather_results(m, b):
                for k in range(m.k):
                    for g in batch_tiles(m, b):
                        pl.indirect_dma_start(yg[:, k + 2 - m.k, g, :], None, ys_dram[0:m.blocks * P, :],
                                              bass.IndirectOffsetOnAxis(ap=pos_i[:, k, g:g + 1].bitcast(U32), axis=0),
                                              bounds_check=m.blocks * P - 1, oob_is_err=False)\
                          .then_inc(yg_in[m.name, b, k], 16)

            def rsqrt():
                rn[0] += 1
                pl.wait_ge(var_ready, rn[0])
                pl.tensor_tensor(rstd[:, :], ve[:, :], nhalf[:, :], ALU.pow).then_inc(rstd_ready, 1)

            def value_parts(b):
                for q in range(3):
                    pl.wait_ge(*free_of["A1v", b, q])
                    r = v1r[0:96, q, :].rearrange("p (s h d) -> p s h d", s=4, h=H1)
                    step(pl.tensor_copy(v1[b % 2][0:96, q, :, :, 1, :], r))
                    step(pl.tensor_tensor(r, r, v1[b % 2][0:96, q, :, :, 1, :], ALU.subtract))
                    ins = pl.tensor_copy(v1[b % 2][0:96, q, :, :, 2, :], r)
                ins.then_inc(v1_ready, 1)

            def norms(layer):
                m = MIXES[layer - 1]
                if layer:
                    results_out(m)
                    gather_results(m, 0)
                for what, b in NORMS:
                    if what[1] == str(layer):
                        rsqrt()
                        if layer == 3 and (what, b) == ("A3", 0):
                            step(pl.iota(rel[:, :], pattern=[[1, TP]], base=-(NT - 1) * P, channel_multiplier=-1,
                                     allow_small_or_imprecise_dtypes=True))
                            step(pl.tensor_scalar(rel[:, :], rel[:, :], 0.5, None, ALU.mult))
                            pl.affine_select(out=rel[:, :], in_=rel[:, :], compare_op=ALU.is_ge, fill=NEG,
                                         base=(NT - 1) * P, pattern=[[-1, TP]], channel_multiplier=1).then_inc(consts_ready, 1)
                        if layer and what[0] == "A" and b + 1 < B:
                            gather_results(m, b + 1)
                        for q in {("A1", 0): (0,), ("A1", 1): (1,), ("F1", 0): (2,), ("F1", 1): (3,)}.get((what, b), ()):
                            value_parts(q)

            rsqrt()
            norms(0)
            gather_blocks(MIXES[0])
            pl.wait_ge(stage_done, 3)
            pl.memset(k1[:, :], 0.0).then_inc(consts_ready, 1)
            norms(1)
            gather_blocks(MIXES[1])
            norms(2)
            gather_blocks(MIXES[2])
            pl.wait_ge(stage_done, 7)
            norms(3)
            pl.wait_ge(stage_done, 8)
            pl.memset(rcT[:, :, :], 0.0).then_inc(consts_ready, 1)
            gather_blocks(MIXES[3])
            results_out(MIXES[3])
            for b in range(B):
                gather_results(MIXES[3], b)
                rsqrt()

        @block.scalar
        def _(act):
            max_n = [0]

            def evac(ring, key, dst, src, func=ACT.Copy, last=True, **kw):
                act.wait_ge(*fill_of[key])
                ins = act.activation(dst, src, func, **kw)
                if last:
                    ins.then_inc(ring.free, 1)

            def norm_turn(stage, b):
                for half in range(2):
                    n = HALF if half == 0 else T - HALF
                    evac(turn[half], (stage, "norm", b, half),
                         xT[:, b, HALO + half * HALF:HALO + half * HALF + n], turn[half].t[:, 0:n])

            def logits(stage, q):
                m = MIXES[int(stage[1])]
                bias = W[{"L0": "bs0", "L2": "rb2", "L3": "rcb2"}[m.name]]
                for half in range(2):
                    evac(turn[half], (stage, "lgT", q, half), lgT[0:m.experts, half * HALF:(half + 1) * HALF],
                         turn[half].t[0:m.experts, 0:HALF], ACT.Identity, bias=bias[:, 0:1])

            def side_turns(stage, b, s):
                for phase, what, q in side_jobs(stage, b, s):
                    if phase == 2:
                        norm_turn(what, q)
                    if phase == 3:
                        logits(what, q)

            def halves(x):
                return x.rearrange("p (a c) -> p a c", a=2)

            def flat(x):
                return x.rearrange("p a c -> p (a c)")

            def from_max():
                max_n[0] += 1
                act.wait_ge(max_ready, max_n[0])

            act.wait_ge(loaded["tok"], n_loads["tok"])
            for b in range(B):
                evac(wide[b % 2], ("tok", b), halves(yT[:, b, 0:T]), wide[b % 2].t[:, :, 0:SC],
                     ACT.Relu, bias=W["tokv"][:, 0:1])
            act.wait_ge(consts_ready, 1)
            for b in range(B):
                evac(turn[0], ("tokT", b, 0), flat(h[:, b * NT:b * NT + 3, :]), turn[0].t[:, 0:HALF])

            act.wait_ge(loaded["mix0"], n_loads["mix0"])
            for b in range(B):
                if b == 0:
                    norm_turn("A0", 0)
                q = 0
                for n, (i, c) in enumerate(V0_PARTS):
                    if i == 0:
                        act.wait_ge(*fill_of["A0v", b, c])
                        src = wide[c % 2].t[:, :, :]
                    else:
                        if i == 1:
                            act.wait_ge(*free_of["A0v", b, c])
                        else:
                            act.wait_ge(v0_rest, 3 * b + c + 1)
                        src = v0r[:, c, :, :]
                    act.activation(v0[:, 2 * c:2 * c + 2, i, :], src, ACT.Copy).then_inc(v0_part, 1)
                    if n >= 4 and q < NF:
                        ring = wide[(q + 1) % 2]
                        evac(ring, ("A0q", b, q), halves(qT[:, q, :]), ring.t[:, :, 0:HALF], scale=DH0 ** -0.5)
                        q += 1
                N = NT * H0
                for s in range(N + 7):
                    if 2 <= s < N + 2:
                        u = s - 2
                        for half in range(2):
                            act.wait_ge(*fill_of["T0", b, u, half])
                            act.activation(flat(pT0[:, u % 3, 3 * half:3 * half + 3, :]), turn[half].t[:, 0:HALF],
                                           ACT.Copy).then_inc(p0_ready, 1)
                    if s < N:
                        from_max()
                        t, hd = divmod(s, H0)
                        evac(wide[s % 2], ("S0", b, s), halves(p0[:, s % 3, 0:T]), wide[s % 2].t[:, :, 0:SC],
                             ACT.Exp, bias=nm[:, t % 2, hd:hd + 1], accum_out=ssum[:, t % 2, hd:hd + 1])
                    if s >= 5 and (s - 5) % H0 == H0 - 1:
                        t = (s - 5) // H0
                        evac(accs[t % 2], ("OT0", b, t), flat(oT0[:, :, :]), accs[t % 2].t[:, :])
                    side_turns("A0", b, s)

            def gate_rows(m, s):
                q, ring = s - GB, turn[(s + 1) % 2]
                if 0 <= q < NTT // 4:
                    if q >= 2:
                        act.wait_ge(*fill_of[m.name, "gb", q - 2])
                    evac(ring, (m.name, "gT", q), gT[0:m.experts, q % 2, :], ring.t[0:m.experts, :])

            def softmax_exp(src):
                from_max()
                act.activation(src, src, ACT.Exp).then_inc(exp_ready, 1)

            def expert_blocks(m):
                for j in range(m.blocks):
                    if j >= 3:
                        act.wait_ge(*fill_of[m.name, "down", j - 3])
                    if m.name == "L1":
                        evac(wide[j % 2], (m.name, "up", j), flat(hidb[:, j % 3, :, :]), wide[j % 2].t[:, 0, :], ACT.Gelu)
                        continue
                    for c in range(NF):
                        evac(wide[j % 2], (m.name, "up", j), hidb[:, j % 3, c, :],
                             wide[j % 2].t[:, 0, c * P:(c + 1) * P], ACT.Gelu, last=c == NF - 1,
                             bias=bias[:, c, j:j + 1])
                    gate_rows(m, j + 1)

            norm_turn("F0", B - 1)
            logits("F0", B - 1)
            softmax_exp(ex[:, :, 0:8])
            act.wait_ge(stage_done, 2)
            act.wait_ge(idx_ready, 1)
            expert_blocks(MIXES[0])

            act.wait_ge(loaded["attn1"], n_loads["attn1"])
            act.wait_ge(consts_ready, 4)
            part_n, part_of = [0], {}

            def rounded(key, dst, src):
                act.wait_ge(*fill_of[key])
                act.activation(dst, src, ACT.Copy).then_inc(parts_ready, 1)
                part_n[0] += 1
                part_of[key] = part_n[0]

            def project1(b):
                act.wait_ge(*fill_of["A1qk", b, 0])
                for hd in range(H1):
                    if hd == H1 - 1:
                        act.wait_ge(heads_ready, b + 1)
                    ins = act.activation(qm[:, hd, HALF:TP], wide[0].t[:, 1, 0:HALF], ACT.Identity,
                                         scale=hmask[:, hd:hd + 1], bias=bq8[:, hd:hd + 1])
                ins.then_inc(wide[0].free, 1)
                evac(wide[1], ("A1qk", b, 1), k1[:, HALO:HALO + HALF], wide[1].t[:, 0, 0:HALF],
                     ACT.Identity, last=False, bias=W["bqk1"][:, 1:2])
                evac(wide[1], ("A1qk", b, 1), k1[:, HALO + HALF:HALO + TP], wide[1].t[:, 1, 0:HALF],
                     ACT.Identity, bias=W["bqk1"][:, 1:2])
                for q in range(3):
                    rounded(("A1v", b, q), v1[b % 2][0:96, q, :, :, 0, :],
                            accs[q % 2].t[0:96, :].rearrange("p (s h d) -> p s h d", s=4, h=H1))

            norm_turn("A1", 0)
            act.wait_ge(bq8_ready, 1)
            project1(0)
            for s in range(NTT + 4):
                side_turns("A1", None, s)
                for i in range(2):
                    if 2 <= s < NTT + 2:
                        b, t = divmod(s - 2, NT)
                        if s >= 4:
                            act.wait_ge(*fill_of[("O1", *divmod(s - 4, NT))])
                        for q in (2 * i, 2 * i + 1):
                            rounded(("T1", b, t, q), flat(pT1[0:96, t % 2, 4 * q:4 * q + 4, :]), turn[q % 2].t[0:96, :])
                    if i == 0 and s >= 4:
                        evac(accs[1], ("OT1", *divmod(s - 4, NT)), oT1[:, :], accs[1].t[:, 0:P])
                    if s < NTT:
                        b, t = divmod(s, NT)
                        from_max()
                        for j in range(4):
                            hd = 4 * i + j
                            evac(wide[i], ("S1", b, t, i), s1[:, t % 2, hd, :],
                                 wide[i].t[:, j // 2, (j % 2) * WIN:(j % 2 + 1) * WIN], ACT.Exp, last=j == 3,
                                 bias=nm[:, t % 2, hd:hd + 1], accum_out=ssum[:, t % 2, hd:hd + 1])
                if s % NT == PROJECT and s < NTT - NT:
                    project1(s // NT + 1)
            parts_at.update(part_of)

            act.wait_ge(stage_done, 4)
            expert_blocks(MIXES[1])

            act.wait_ge(loaded["attn2"], n_loads["attn2"])
            act.wait_ge(loaded["mix2"], n_loads["mix2"])
            act.wait_ge(stage_done, 5)
            evac(accs[0], ("wvo",), wvo[:, :], accs[0].t[:, 0:P])
            evac(accs[1], ("bvo",), bvo[0:1, :], accs[1].t[0:1, 0:P])
            from_max()
            act.activation(lamv[:, 0:2], lamv[:, 0:2], ACT.Exp).then_inc(exp_ready, 1)
            def project2(b):
                evac(wide[1], ("A2qk", b, 1), halves(qk2[:, b % 2, 1, :]), wide[1].t[:, :, 0:HALF],
                     ACT.Identity, bias=W["bqk2"][:, 1:2])
                evac(accs[0], ("A2v", b, 0), flat(v2[:, b % 2, 0:3, :]), accs[0].t[:, 0:HALF])

            norm_turn("A2", 0)
            project2(0)
            for s in range(NTT + 3):
                if 2 <= s < NTT + 2:
                    b, t = divmod(s - 2, NT)
                    evac(turn[0], ("T2", b, t, 0), flat(pT2[:, t % 2, 0:3, :]), turn[0].t[:, 0:HALF])
                if s < NTT:
                    b, t = divmod(s, NT)
                    for i in range(2):
                        from_max()
                        evac(wide[i], ("S2", b, t, i), halves(p2[:, 2 * (t % 2) + i, 0:T]), wide[i].t[:, :, 0:SC],
                             ACT.Exp, bias=nm[:, t % 2, i:i + 1], accum_out=ssum[:, t % 2, i:i + 1])
                if s % NT == PROJECT and s < NTT - NT:
                    project2(s // NT + 1)
                side_turns("A2", None, s)

            norm_turn("F2", B - 1)
            logits("F2", B - 1)
            softmax_exp(ex[:, :, 0:16])
            act.wait_ge(stage_done, 6)
            act.wait_ge(idx_ready, 3)
            expert_blocks(MIXES[2])

            act.wait_ge(stage_done, 7)
            def project3(b):
                evac(wide[0], ("A3u", b), halves(uT3[:, b % 2, :]), wide[0].t[:, :, 0:HALF])
                evac(accs[0], ("A3v", b, 0), flat(v3[:, b % 2, 0:3, :]), accs[0].t[:, 0:HALF])

            norm_turn("A3", 0)
            project3(0)
            for s in range(NTT + 3):
                if 2 <= s < NTT + 2:
                    b, t = divmod(s - 2, NT)
                    n = min(3, t + 1)
                    evac(turn[0], ("T3", b, t, 0), flat(pT3[:, t % 2, 0:n, :]), turn[0].t[:, 0:n * P])
                if s < NTT:
                    from_max()
                    t = s % NT
                    n = (t + 1) * P
                    act.activation(p3[:, t % 3, 0:n], s3[:, t % 2, 0:n], ACT.Exp, bias=nm[:, t % 2, 0:1],
                                   accum_out=ssum[:, t % 2, 0:1]).then_inc(probs_ready, 1)
                if s % NT == PROJECT and s < NTT - NT:
                    project3(s // NT + 1)
                side_turns("A3", None, s)

            act.wait_ge(loaded["mix3"], n_loads["mix3"])
            norm_turn("F3", B - 1)
            act.wait_ge(stage_done, 8)
            act.wait_ge(consts_ready, 6)
            for b in range(B):
                for half in range(2):
                    n = HALF if half == 0 else T - HALF
                    evac(wide[b % 2], ("rc1", b), rcT[:, b, HALO + half * HALF:HALO + half * HALF + n],
                         wide[b % 2].t[:, half, 0:n], ACT.Gelu, last=half == 1, bias=W["rcb1"][:, 0:1])
            for b in range(B):
                logits("F3", b)
            softmax_exp(gw[:, :, 1])

            def shared_rows(g):
                for c in range(NF):
                    evac(wide[c // 2], ("sh", g, c // 2), hid[:, g % 2, c, :], wide[c // 2].t[:, c % 2, 0:HALF],
                         ACT.Silu, last=c % 2 == 1, bias=W["shb1"][:, c:c + 1])

            for g in range(4):
                shared_rows(g)
            act.wait_ge(idx_ready, 4)

            ys_n = [len([j for m in MIXES[:3] for j in range(m.blocks) if j % XG == i]) for i in range(XG)]

            def result(j):
                act.wait_ge(ys_out[j % XG], 16 * ys_n[j % XG])
                ys_n[j % XG] += 1
                evac(accs[j % 2], ("L3", "down", j), yo[:, j % XG, :], accs[j % 2].t[:, 0:P])

            w3 = weights(MIXES[3])
            act.wait_ge(experts_in["L3"], 32 * MIXES[3].experts)
            for s in range(MIXES[3].blocks + 1):
                if s < MIXES[3].blocks:
                    e = act.value_load(blk_e_i[0:1, s:s + 1], min_val=0, max_val=MIXES[3].experts - 1)
                    if s >= 2:
                        act.wait_ge(*fill_of["L3", "up", s - 2])
                    act.activation(w1c[:, s % 2, :], w3[:, bass.ds(e, 1), 0:4 * P].rearrange("p a c -> p (a c)"),
                                   ACT.Copy).then_inc(w1_ready, 1)
                    evac(turn[s % 2], ("L3", "xt", s), xgT[:, s % 2, :], turn[s % 2].t[:, 0:P])
                if s == 0:
                    continue
                j = s - 1
                act.wait_ge(*fill_of["L3", "up", j])
                if j >= 2:
                    act.wait_ge(elu_ready, j - 1)
                for c in range(NF):
                    ins = act.activation(e3[:, j % 2, c, :], wide[j % 2].t[:, 0, c * P:(c + 1) * P], ACT.Exp,
                                         bias=bias[:, c, j:j + 1])
                ins.then_inc(exp_ready, 1)
                if j >= 2:
                    result(j - 2)
                gate_rows(MIXES[3], s)
            result(MIXES[3].blocks - 2)
            result(MIXES[3].blocks - 1)
            for g in range(4, 8):
                shared_rows(g)

        @block.vector
        def _(dve):
            steps, v_c, var_c, exp_c = [0], [0], [0], [0]

            def step(ins):
                steps[0] += 1
                ins.then_inc(v_step, 1)

            def settle():
                dve.wait_ge(v_step, steps[0])

            def then(ins):
                step(ins)
                settle()

            def to_pe(ins):
                v_c[0] += 1
                ins.then_inc(v_to_pe, 1)

            def settle_pe():
                dve.wait_ge(v_to_pe, v_c[0])

            def see(*key):
                dve.wait_ge(*fill_of[key])

            def moved(*key):
                dve.wait_ge(*free_of[key])

            def from_exp():
                exp_c[0] += 1
                dve.wait_ge(exp_ready, exp_c[0])

            def halves(x):
                return x.rearrange("p (a c) -> p a c", a=2)

            def flat(x):
                return x.rearrange("p a c -> p (a c)")

            def over(x, shape):
                return x.unsqueeze(len(shape) - 1).to_broadcast(shape)

            def rsqrt_var():
                var_c[0] += 1
                dve.wait_ge(rstd_ready, var_c[0])

            def norm_stats(b, src=None):
                src = h if src is None else src
                for t in range(NT):
                    ins = dve.bn_stats(st[:, t, :], src[:, b * NT + t, :])
                then(ins)
                for t in range(NT):
                    ins = dve.bn_aggr(mv[:, t, :], st[:, t, :])
                then(ins)
                dve.tensor_scalar(ve[:, :], mv[:, :, 1], EPS, None, ALU.add).then_inc(var_ready, 1)

            def norm_result(b, src=None, dst=None):
                src = h if src is None else src
                rsqrt_var()
                for t in range(NT):
                    ins = dve.tensor_scalar((xn if dst is None else dst)[:, b * NT + t, :], src[:, b * NT + t, :],
                                            mv[:, t, 0:1], rstd[:, t:t + 1], ALU.subtract, ALU.mult)
                    if dst is None and t % 3 == 2:
                        ins.then_inc(xn_ready, 1)
                if dst is not None:
                    then(ins)

            def norm(b, src=None, dst=None):
                norm_stats(b, src)
                norm_result(b, src, dst)

            def logits(stage, q):
                E, tiles = MIXES[int(stage[1])].experts, range(q * NT, (q + 1) * NT)
                see(stage, "lg", q)
                dve.tensor_copy(lg[:, q * NT:(q + 1) * NT, 0:E],
                                turn[0].t[:, 0:NT * E].rearrange("p (a c) -> p a c", a=NT)).then_inc(turn[0].free, 1)
                moved(stage, "lg", q)
                for g in tiles:
                    ins = dve.max(m8[:, g, :], lg[:, g, 0:E])
                then(ins)
                for g in tiles:
                    ins = dve.max_index(i8[:, g, :], m8[:, g, :], lg[:, g, 0:E])
                step(ins)

            last_adds = {"0": [("Y0", NT - 1)], "1": [("Y1", NT - 1)],
                         "2": [("O2", NT - 2), ("O2", NT - 1)], "3": [("O3", NT - 2), ("O3", NT - 1)]}

            def side_norms(stage, b, s):
                for phase, what, q in side_jobs(stage, b, s):
                    if phase == 0:
                        if what[0] == "F":
                            for name, t in last_adds[stage[1]]:
                                moved(name, q, t)
                        elif stage != "A0":
                            combine_before(stage, q)
                        norm_stats(q)
                    if phase == 1:
                        norm_result(q)
                    if phase == 4:
                        logits(what, q)

            def combine_before(stage, q):
                layer = int(stage[1]) - 1
                combine(MIXES[layer], q, h, ew if layer == 1 else gw)

            def add_tiles(acc, g, n, ring, key, src):
                see(*key)
                dve.tensor_tensor(acc[:, g:g + n, :], src, acc[:, g:g + n, :], ALU.add).then_inc(ring.free, 1)

            dve.wait_ge(consts_ready, 1)
            dve.memset(ve[:, :], 1.0)
            dve.memset(yT[:, :, T:TP], 0.0)
            dve.wait_ge(loaded["tok"], n_loads["tok"])
            for b in range(B):
                moved("tok", b)
                for half in range(2):
                    ins = dve.bn_stats(st0[:, 2 * b + half, :], yT[:, b, half * SC:(half + 1) * SC])
            then(ins)
            then(dve.bn_aggr(mv0[:, :], flat(st0[:, :, :])))
            dve.tensor_scalar(ve[:, 0:1], mv0[:, 1:2], EPS, None, ALU.add).then_inc(var_ready, 1)
            rsqrt_var()
            then(dve.tensor_tensor(sc0[:, 0:1], rstd[:, 0:1], W["tokv"][:, 1:2], ALU.mult))
            then(dve.tensor_tensor(sc0[:, 1:2], mv0[:, 0:1], sc0[:, 0:1], ALU.mult))
            then(dve.tensor_tensor(sc0[:, 2:3], W["tokv"][:, 2:3], sc0[:, 1:2], ALU.subtract))
            to_pe(dve.tensor_scalar(yT[:, :, 0:T], yT[:, :, 0:T], sc0[:, 0:1], sc0[:, 2:3], ALU.mult, ALU.add))
            for b in range(B):
                see("tokT", b, 1)
                dve.tensor_copy(flat(h[:, b * NT + 3:b * NT + 6, :]), turn[1].t[:, 0:HALF]).then_inc(turn[1].free, 1)
            for b in range(B):
                for half in range(2):
                    moved("tokT", b, half)
            dve.memset(p0[:, :, T:TP], 0.0).then_inc(stage_done, 1)

            dve.wait_ge(consts_ready, 3)
            for b in range(B):
                if b == 0:
                    norm(0)
                for i, c in V0_RESTS:
                    dve.wait_ge(v0_part, len(V0_PARTS) * b + V0_PARTS.index((i - 1, c)) + 1)
                    if i == 1:
                        ins = dve.tensor_tensor(v0r[:, c, :, :], wide[c % 2].t[:, :, :], v0[:, 2 * c:2 * c + 2, 0, :],
                                                ALU.subtract)
                        ins.then_inc(wide[c % 2].free, 1)
                    else:
                        dve.tensor_tensor(v0r[:, c, :, :], v0r[:, c, :, :], v0[:, 2 * c:2 * c + 2, 1, :], ALU.subtract)\
                           .then_inc(v0_rest, 1)
                for c in range(NF):
                    see("A0k", b, c)
                    ring = wide[(c + 1) % 2]
                    dve.tensor_copy(halves(kT[:, c, :]), ring.t[:, :, 0:HALF]).then_inc(ring.free, 1)
                N = NT * H0
                for s in range(N + 7):
                    if s < N:
                        t, hd = divmod(s, H0)
                        see("S0", b, s)
                        dve.tensor_reduce(nm[:, t % 2, hd:hd + 1], wide[s % 2].t[:, :, 0:SC], AX.XY, ALU.max,
                                          negate=True).then_inc(max_ready, 1)
                    if 4 <= s < N + 4 and (s - 4) % H0 == H0 - 1:
                        t = (s - 4) // H0
                        moved("S0", b, s - 4)
                        moved("S0", b, s - 5)
                        then(dve.reciprocal(rs[:, t % 2, :], ssum[:, t % 2, :]))
                        see("O0", b, t)
                        dve.tensor_tensor(o0.rearrange("p (a c) -> p a c", a=H0),
                                          accs[t % 2].t[:, :].rearrange("p (a c) -> p a c", a=H0),
                                          over(rs[:, t % 2, :], [P, H0, DH0]), ALU.mult).then_inc(accs[t % 2].free, 1)
                    if s >= 6 and (s - 6) % H0 == H0 - 1:
                        t = (s - 6) // H0
                        add_tiles(h, b * NT + t, 1, accs[t % 2], ("Y0", b, t), accs[t % 2].t[:, 0:P].unsqueeze(1))
                    if 2 <= s < N + 2:
                        u = s - 2
                        for half in range(2):
                            dve.wait_ge(p0_ready, 2 * (b * N + u) + half + 1)
                            dve.tensor_tensor(flat(pT0r[:, u % 3, 3 * half:3 * half + 3, :]), turn[half].t[:, 0:HALF],
                                              flat(pT0[:, u % 3, 3 * half:3 * half + 3, :]), ALU.subtract)\
                               .then_inc(turn[half].free, 1)
                    side_norms("A0", b, s)
            moved("Y0", B - 1, NT - 1)
            dve.memset(nm[:, :, :], 0.0).then_inc(stage_done, 1)

            def one_hot(dst, index, n_e, n=NTT):
                return dve.tensor_tensor(dst[:, 0:n, 0:n_e], lane[:, 0:n_e].unsqueeze(1).to_broadcast([P, n, n_e]),
                                         over(index, [P, n, n_e]), ALU.is_equal)

            def times(dst, x, col, n_e, n=NTT):
                return dve.tensor_tensor(dst[:, 0:n, 0:n_e], x[:, 0:n, 0:n_e], over(col, [P, n, n_e]), ALU.mult)

            idx_n, table_n, w1_n, comb_n = [0], [0], [0], [0]

            def by_expert(x, E):
                return x[:, 0:NTT * E].rearrange("p (g e) -> p g e", e=E)

            def choose(m):
                E = m.experts
                for k in range(m.k):
                    step(one_hot(oneh[:, k], i8f[:, :, k], E))
                settle()
                both = oneh[:, 0, :, 0:E]
                if m.k == 2:
                    then(dve.tensor_tensor(by_expert(sent, E), oneh[:, 0, :, 0:E], oneh[:, 1, :, 0:E], ALU.add))
                    both = by_expert(sent, E)
                to_pe(dve.tensor_tensor(by_expert(sent, E), both, over(real[:, 0, :], [P, NTT, E]), ALU.mult))

            def softmax_gates(m):
                E = m.experts
                from_exp()
                then(dve.tensor_reduce(gw[:, :, 0], ex[:, :, 0:E], AX.X, ALU.add))
                step(dve.reciprocal(gw[:, :, 1], gw[:, :, 0]))
                both = oneh[:, 0, :, 0:E]
                if m.k == 2:
                    then(dve.tensor_tensor(gates[:, :, 0:E], oneh[:, 0, :, 0:E], oneh[:, 1, :, 0:E], ALU.add))
                    both = gates[:, :, 0:E]
                then(dve.tensor_tensor(gates[:, :, 0:E], both, ex[:, :, 0:E], ALU.mult))
                times(gates, gates, gw[:, :, 1], E).then_inc(gates_ready, 1)

            def gate_of_choice(m, n):
                E = m.experts
                dve.wait_ge(gates_ready, n)
                for k in range(m.k):
                    then(dve.tensor_tensor(ex[:, :, 0:E], oneh[:, k, :, 0:E], gates[:, :, 0:E], ALU.mult))
                    then(dve.tensor_reduce(gw[:, :, k], ex[:, :, 0:E], AX.X, ALU.add))

            def slots(m):
                E, layer1 = m.experts, int(m.name == "L1")
                tot = wide[0].t[:, 1, 0:NTT * E].rearrange("p (b t e) -> p b t e", b=B, t=NT)
                pre4 = pre[:, 0:NTT * E].rearrange("p (b t e) -> p b t e", b=B, t=NT)
                for z in (pre4[:, :, 0, :], bpre[:, 0, 0:E], scan[:, 0, 0:16], scan[:, 1, 0:16]):
                    ins = dve.memset(z, 0.0)
                then(ins)
                see(m.name, "ranks")
                for t in range(NT - 1):
                    then(dve.tensor_tensor(pre4[:, :, t + 1, :], pre4[:, :, t, :], tot[:, :, t, :], ALU.add))
                then(dve.tensor_tensor(bsum[:, :, 0:E], pre4[:, :, NT - 1, :], tot[:, :, NT - 1, :], ALU.add))
                for b in range(B):
                    then(dve.tensor_tensor(bpre[:, b + 1, 0:E], bpre[:, b, 0:E], bsum[:, b, 0:E], ALU.add))
                then(dve.tensor_scalar(nblk_i[:, 0:E], bpre[:, B, 0:E], float(P - 1), None, ALU.add))
                then(dve.tensor_scalar(nblk_i[:, 0:E], nblk_i[:, 0:E], 7, None, ALU.logical_shift_right))
                step(dve.tensor_copy(nblk[:, 0:E], nblk_i[:, 0:E]))
                then(dve.tensor_copy(scan[:, 0, 16:16 + E], nblk_i[:, 0:E]))
                i = 0
                for sh in (1, 2, 4, 8):
                    then(dve.tensor_tensor(scan[:, 1 - i, 16:16 + E], scan[:, i, 16:16 + E],
                                           scan[:, i, 16 - sh:16 - sh + E], ALU.add))
                    i = 1 - i
                end = scan[:, i, 16:16 + E]
                then(dve.tensor_tensor(bstart[:, 0:E], end, nblk[:, 0:E], ALU.subtract))
                then(dve.scalar_tensor_tensor(out=bb[:, :, 0:E], in0=bstart[:, 0:E].unsqueeze(1).to_broadcast([P, B, E]),
                                              scalar=float(P), in1=bpre[:, 0:B, 0:E], op0=ALU.mult, op1=ALU.add))
                for b in range(B):
                    ins = dve.tensor_tensor(pre4[:, b], pre4[:, b], bb[:, b, 0:E].unsqueeze(1).to_broadcast([P, NT, E]),
                                            ALU.add)
                then(ins)
                dve.tensor_tensor(pre[:, 0:NTT * E], pre[:, 0:NTT * E], wide[0].t[:, 0, 0:NTT * E], ALU.add)\
                   .then_inc(wide[0].free, 1)
                moved(m.name, "ranks")
                K, n = m.k, 2 * NTT if m.k == 2 else NTT
                for k in range(K):
                    ins = dve.tensor_tensor(by_expert(ysent[:, k * NTT * 16:(k + 1) * NTT * 16], E), oneh[:, k, :, 0:E],
                                            by_expert(pre, E), ALU.mult)
                then(ins)
                for k in range(K):
                    ins = dve.tensor_reduce(pos[:, k * NTT:(k + 1) * NTT],
                                            by_expert(ysent[:, k * NTT * 16:(k + 1) * NTT * 16], E), AX.X, ALU.add)
                then(ins)
                if layer1:
                    then(dve.tensor_tensor(eif[:, :, 0], eif[:, :, 0], eif[:, :, 1], ALU.is_equal))
                    then(dve.tensor_tensor(pos[:, NTT:NTT + 9], pos[:, NTT:NTT + 9], eif[:, :, 0], ALU.add))
                for k in range(K):
                    ins = dve.tensor_tensor(pos_i[:, k, :], pos[:, k * NTT:(k + 1) * NTT], real[:, layer1, :], ALU.mult)
                then(ins)
                flat_i = flat(pos_i[:, :, :])[:, 0:n]
                step(dve.tensor_scalar(blk_i[:, 0:n], flat_i, 7, None, ALU.logical_shift_right))
                then(dve.tensor_scalar(slot_i[:, 0:n], flat_i, P - 1, None, ALU.bitwise_and))
                step(dve.tensor_copy(slot_f[:, 0:n], slot_i[:, 0:n]))
                for k in range(K):
                    ins = dve.tensor_tensor(blk_f[:, k * NTT:(k + 1) * NTT], blk_i[:, k * NTT:(k + 1) * NTT],
                                            pad_off[:, layer1, :], ALU.add)
                then(ins)
                g = ge_end[:, 0:m.blocks * E].rearrange("p (j e) -> p j e", e=E)
                then(dve.tensor_tensor(g, over(lane[:, 0:m.blocks], [P, m.blocks, E]),
                                       end.unsqueeze(1).to_broadcast([P, m.blocks, E]), ALU.is_ge))
                then(dve.tensor_reduce(blk_e[:, 0:m.blocks], g, AX.X, ALU.add))
                then(dve.tensor_scalar(blk_e[:, 0:m.blocks], blk_e[:, 0:m.blocks], float(E - 1), None, ALU.min))
                then(dve.tensor_copy(blk_e_i[:, 0:m.blocks], blk_e[:, 0:m.blocks]))
                if m.name != "L1":
                    to_pe(dve.tensor_scalar(blk_e[:, 0:m.blocks], blk_e[:, 0:m.blocks], row[:, 0:1], None, ALU.is_equal))

            def invert(m):
                todo = chunks(m)
                for i, (k, tiles) in enumerate(todo):
                    n, c0 = len(tiles), k * NTT + tiles[0]
                    if i >= 2:
                        dve.wait_ge(table_used, table_n[0] + i - 1)
                    dve.tensor_tensor(slot_hot[:, i % 2, 0:n, :], lane16[:, :].unsqueeze(1).to_broadcast([P, n, P]),
                                      over(slot_f[:, c0:c0 + n], [P, n, P]), ALU.is_equal)
                    o = blk_hot[:, i % 2, 0:n, 0:m.blocks]
                    then(dve.tensor_tensor(o, lane16[:, 0:m.blocks].unsqueeze(1).to_broadcast([P, n, m.blocks]),
                                           over(blk_f[:, c0:c0 + n], [P, n, m.blocks]), ALU.is_equal))
                    to_pe(dve.tensor_tensor(o, o, over(tok_id[:, tiles[0]:tiles[0] + n], [P, n, m.blocks]), ALU.mult))
                table_n[0] += len(todo) - 1
                if m.name != "L1":
                    see(m.name, "bias")
                    dve.tensor_copy(bias[:, :, 0:m.blocks],
                                    accs[0].t[:, 0:NF * m.blocks].rearrange("p (c j) -> p c j", c=NF))\
                       .then_inc(accs[0].free, 1)
                if m.name == "L3":
                    moved(m.name, "bias")
                    step(dve.tensor_scalar(biasm[:, :, 0:m.blocks], bias[:, :, 0:m.blocks], -1.0, None, ALU.add))
                see(m.name, "idx")
                dve.tensor_scalar(idx[:, 0:m.blocks], accs[1].t[:, 0:m.blocks], float(MID), None, ALU.add)\
                   .then_inc(accs[1].free, 1)
                moved(m.name, "idx")
                dve.memset(nm[:, :, :], 0.0).then_inc(idx_ready, 1)
                idx_n[0] += 1

            ys_n = [0] * XG

            def expert_blocks(m, acc=None):
                w = weights(m)
                dve.wait_ge(idx_ready, idx_n[0])
                dve.wait_ge(experts_in[m.name], 32 * m.experts)
                for s in range(m.blocks + 3):
                    if s < m.blocks:
                        if m.name != "L3":
                            e = dve.value_load(blk_e_i[0:1, s:s + 1], min_val=0, max_val=m.experts - 1)
                            if s >= 2:
                                see(m.name, "up", s - 2)
                            dve.tensor_copy(w1c[:, s % 2, :], w[:, bass.ds(e, 1), 0:4 * P].rearrange("p a c -> p (a c)"))\
                               .then_inc(w1_ready, 1)
                            see(m.name, "xt", s)
                            dve.tensor_copy(xgT[:, s % 2, :], turn[s % 2].t[:, 0:P]).then_inc(turn[s % 2].free, 1)
                    if m.name == "L3" and 1 <= s < m.blocks + 1:
                        j = s - 1
                        from_exp()
                        if j >= 1:
                            dve.wait_ge(elu_ready, j)
                        for c in range(NF):
                            ins = dve.tensor_scalar(r3[:, c, :], wide[j % 2].t[:, 0, c * P:(c + 1) * P],
                                                    biasm[:, c, j:j + 1], -1.0, ALU.add, ALU.max)
                        ins.then_inc(wide[j % 2].free, 1)
                        moved(m.name, "up", j)
                        if j >= 3:
                            see(m.name, "down", j - 3)
                        dve.scalar_tensor_tensor(out=flat(hidb[:, j % 3, :, :]), in0=flat(e3[:, j % 2, :, :]),
                                                 scalar=1.0, in1=flat(r3[:, :, :]), op0=ALU.min,
                                                 op1=ALU.add).then_inc(elu_ready, 1)
                    if s >= 3 and m.name != "L3":
                        j = s - 3
                        see(m.name, "down", j)
                        if ys_n[j % XG]:
                            dve.wait_ge(ys_out[j % XG], 16 * ys_n[j % XG])
                        ys_n[j % XG] += 1
                        dve.tensor_copy(yo[:, j % XG, :], accs[j % 2].t[:, 0:P]).then_inc(accs[j % 2].free, 1)
                    if acc is not None:
                        gate_bias(acc, m, s)
                moved(m.name, "down", m.blocks - 2)
                moved(m.name, "down", m.blocks - 1)

            def combine(m, b, acc, weight):
                tiles = batch_tiles(m, b)
                if not len(tiles):
                    return
                for k in range(m.k):
                    dve.wait_ge(yg_in[m.name, b, k], 16 * len(tiles))
                    for g in tiles:
                        if k == 1:
                            dve.wait_ge(combined, comb_n[0] + 1 - len(tiles))
                        dve.scalar_tensor_tensor(out=acc[:, g, :], in0=yg[:, k + 2 - m.k, g, :], scalar=weight[:, g, k:k + 1],
                                                 in1=acc[:, g, :], op0=ALU.mult, op1=ALU.add).then_inc(combined, 1)
                        comb_n[0] += 1
                dve.wait_ge(combined, comb_n[0])

            def gate_bias(acc, m, s):
                q, ring = s - GB - 1, accs[s % 2]
                if 0 <= q < NTT // 4:
                    add_tiles(acc, 4 * q, 4, ring, (m.name, "gb", q), ring.t[:, :].rearrange("p (a c) -> p a c", a=4))

            norm(B - 1)

            def route(m, n):
                E = m.experts
                logits("F" + m.name[1], B - 1)
                dve.tensor_tensor(ex[:, :, 0:E], lg[:, :, 0:E], over(m8[:, :, 0], [P, NTT, E]), ALU.subtract)\
                   .then_inc(max_ready, 1)
                settle()
                then(dve.tensor_copy(i8f[:, :, :], i8[:, :, :]))
                choose(m)
                softmax_gates(m)
                slots(m)
                invert(m)
                gate_of_choice(m, n)
                settle()
                expert_blocks(m, h)

            route(MIXES[0], 1)
            dve.memset(nm[:, :, :], 0.0).then_inc(stage_done, 1)

            dve.wait_ge(loaded["attn1"], n_loads["attn1"])
            dve.wait_ge(consts_ready, 4)
            dve.tensor_tensor(bq8[:, :], hmask[:, :], W["bqk1"][:, 0:1].to_broadcast([P, H1]), ALU.mult)\
               .then_inc(bq8_ready, 1)

            def project1(b):
                see("A1qk", b, 0)
                for hd in range(H1):
                    ins = dve.tensor_scalar(qm[:, hd, 0:HALF], wide[0].t[:, 0, 0:HALF], W["bqk1"][:, 0:1],
                                            hmask[:, hd:hd + 1], ALU.add, ALU.mult)
                ins.then_inc(heads_ready, 1)
                if b:
                    dve.wait_ge(v1_ready, b)
                for q in range(3):
                    dve.wait_ge(parts_ready, parts_at["A1v", b, q])
                    dve.tensor_tensor(v1r[0:96, q, :].rearrange("p (s h d) -> p s h d", s=4, h=H1),
                                      accs[q % 2].t[0:96, :].rearrange("p (s h d) -> p s h d", s=4, h=H1),
                                      v1[b % 2][0:96, q, :, :, 0, :], ALU.subtract).then_inc(accs[q % 2].free, 1)

            def rest1(b, t, q):
                dve.wait_ge(parts_ready, parts_at["T1", b, t, q])
                dve.tensor_tensor(flat(pT1r[0:96, t % 2, 4 * q:4 * q + 4, :]), turn[q % 2].t[0:96, :],
                                  flat(pT1[0:96, t % 2, 4 * q:4 * q + 4, :]), ALU.subtract)\
                   .then_inc(turn[q % 2].free, 1)

            combine_before("A1", 0)
            norm(0)
            project1(0)
            for s in range(NTT + 4):
                if 2 <= s < NTT + 2:
                    b, t = divmod(s - 2, NT)
                    moved("S1", b, t, 0)
                    moved("S1", b, t, 1)
                    then(dve.reciprocal(rs1[:, (s - 2) % 4, :], ssum[:, t % 2, :]))
                for i in range(2):
                    if s < NTT:
                        b, t = divmod(s, NT)
                        see("S1", b, t, i)
                        dve.tensor_reduce(nm[:, t % 2, 4 * i:4 * i + 4].rearrange("p (a c) -> p a c", a=2),
                                          wide[i].t[:, :, 0:HALF].rearrange("p a (b c) -> p a b c", b=2),
                                          AX.X, ALU.max, negate=True).then_inc(max_ready, 1)
                    if 2 <= s < NTT + 2:
                        rest1(*divmod(s - 2, NT), 2 * i)
                        rest1(*divmod(s - 2, NT), 2 * i + 1)
                if 3 <= s < NTT + 3:
                    b, t = divmod(s - 3, NT)
                    see("O1", b, t)
                    heads = o1.rearrange("p (a c) -> p a c", a=H1)
                    then(dve.tensor_reduce(heads, accs[0].t[:, 0:3 * P].rearrange("p (a k c) -> p a c k", a=H1, k=3),
                                           AX.X, ALU.add))
                    dve.tensor_tensor(heads, heads, over(rs1[:, (s - 3) % 4, :], [P, H1, DH1]), ALU.mult)\
                       .then_inc(accs[0].free, 1)
                if s >= 4:
                    b, t = divmod(s - 4, NT)
                    add_tiles(h, b * NT + t, 1, accs[1], ("Y1", b, t), accs[1].t[:, 0:P].unsqueeze(1))
                if s % NT == PROJECT and s < NTT - NT:
                    project1(s // NT + 1)
                side_norms("A1", None, s)
            moved("Y1", B - 1, NT - 1)
            dve.memset(nm[:, :, :], 0.0).then_inc(stage_done, 1)

            dve.wait_ge(loaded["mix1"], n_loads["mix1"])
            then(dve.tensor_copy(eif[:, :, :], ei[:, :, :]))
            step(dve.memset(oneh[:, :, :, :], 0.0))
            then(dve.memset(sent[:, :], 0.0))
            for k in range(2):
                then(one_hot(oneh[:, k], eif[:, :, k], 8, 9))
            then(dve.tensor_tensor(by_expert(sent, 8)[:, 0:9], oneh[:, 0, 0:9, 0:8], oneh[:, 1, 0:9, 0:8], ALU.add))
            to_pe(dve.tensor_tensor(by_expert(sent, 8)[:, 0:9], by_expert(sent, 8)[:, 0:9],
                                    over(real[:, 1, 0:9], [P, 9, 8]), ALU.mult))
            slots(MIXES[1])
            invert(MIXES[1])
            expert_blocks(MIXES[1])
            dve.memset(nm[:, :, :], 0.0).then_inc(stage_done, 1)

            dve.wait_ge(loaded["attn2"], n_loads["attn2"])
            dve.memset(d2[:, :, T:TP], 0.0)
            for i in range(2):
                ins = dve.tensor_tensor(W["lam"][:, 2 * i, :], W["lam"][:, 2 * i, :], W["lam"][:, 2 * i + 1, :], ALU.mult)
            then(ins)
            dve.tensor_reduce(lamv[:, 0:2], W["lam"][:, 0:4:2, :], AX.X, ALU.add).then_inc(max_ready, 1)
            from_exp()
            then(dve.tensor_tensor(lamv[:, 2:3], lamv[:, 1:2], lamv[:, 0:1], ALU.subtract))
            then(dve.tensor_scalar(lamv[:, 3:4], lamv[:, 2:3], -(0.8 - 0.6 * math.exp(-0.3 * 0)), None, ALU.add))

            def project2(b):
                see("A2qk", b, 0)
                dve.tensor_scalar(halves(qk2[:, b % 2, 0, :]), wide[0].t[:, :, 0:HALF], W["bqk2"][:, 0:1], 0.25,
                                  ALU.add, ALU.mult).then_inc(wide[0].free, 1)
                see("A2v", b, 1)
                dve.tensor_copy(flat(v2[:, b % 2, 3:6, :]), accs[1].t[:, 0:HALF]).then_inc(accs[1].free, 1)

            combine_before("A2", 0)
            norm(0)
            project2(0)
            for s in range(NTT + 3):
                if s < NTT:
                    b, t = divmod(s, NT)
                    for i in range(2):
                        see("S2", b, t, i)
                        dve.tensor_reduce(nm[:, t % 2, i:i + 1], wide[i].t[:, :, 0:SC], AX.XY, ALU.max,
                                          negate=True).then_inc(max_ready, 1)
                if 2 <= s < NTT + 2:
                    b, t = divmod(s - 2, NT)
                    see("T2", b, t, 1)
                    dve.tensor_copy(flat(pT2[:, t % 2, 3:6, :]), turn[1].t[:, 0:HALF]).then_inc(turn[1].free, 1)
                if 1 <= s < NTT + 1:
                    b, t = divmod(s - 1, NT)
                    moved("S2", b, t, 0)
                    moved("S2", b, t, 1)
                    then(dve.reciprocal(rs[:, t % 2, 0:2], ssum[:, t % 2, 0:2]))
                    then(dve.tensor_tensor(rs[:, t % 2, 2:3], rs[:, t % 2, 1:2], lamv[:, 3:4], ALU.mult))
                    then(dve.tensor_scalar(p2[:, 2 * (t % 2) + 1, 0:T], p2[:, 2 * (t % 2) + 1, 0:T],
                                           rs[:, t % 2, 2:3], None, ALU.mult))
                    to_pe(dve.scalar_tensor_tensor(out=d2[:, t % 2, 0:T], in0=p2[:, 2 * (t % 2), 0:T],
                                                   scalar=rs[:, t % 2, 0:1], in1=p2[:, 2 * (t % 2) + 1, 0:T],
                                                   op0=ALU.mult, op1=ALU.add))
                if s >= 3:
                    b, t = divmod(s - 3, NT)
                    add_tiles(h, b * NT + t, 1, accs[t % 2], ("O2", b, t), accs[t % 2].t[:, 0:P].unsqueeze(1))
                if s % NT == PROJECT and s < NTT - NT:
                    project2(s // NT + 1)
                side_norms("A2", None, s)
            moved("O2", B - 1, NT - 2)
            moved("O2", B - 1, NT - 1)
            dve.memset(nm[:, :, :], 0.0).then_inc(stage_done, 1)

            norm(B - 1)
            route(MIXES[2], 2)
            dve.memset(nm[:, :, :], 0.0).then_inc(stage_done, 1)


            def project3(b):
                see("A3v", b, 1)
                dve.tensor_copy(flat(v3[:, b % 2, 3:6, :]), accs[1].t[:, 0:HALF]).then_inc(accs[1].free, 1)

            combine_before("A3", 0)
            norm(0)
            dve.wait_ge(consts_ready, 5)
            project3(0)
            for s in range(NTT + 3):
                if 2 <= s < NTT + 2:
                    dve.wait_ge(probs_ready, s - 1)
                    then(dve.reciprocal(rs1[:, (s - 2) % 4, 0:1], ssum[:, s % 2, 0:1]))
                if s < NTT:
                    b, t = divmod(s, NT)
                    see("S3", b, t)
                    if s >= 2:
                        dve.wait_ge(probs_ready, s - 1)
                    n, off = (t + 1) * P, (NT - 1 - t) * P
                    for half in range(2):
                        lo, hi = half * HALF, min((half + 1) * HALF, n)
                        if lo < hi:
                            ins = dve.scalar_tensor_tensor(
                                out=s3[:, t % 2, lo:hi], in0=wide[t % 2].t[:, half, 0:hi - lo], scalar=P ** -0.5,
                                in1=rel[:, off + lo:off + hi], op0=ALU.mult, op1=ALU.add)
                    ins.then_inc(wide[t % 2].free, 1)
                    moved("S3", b, t)
                    dve.tensor_reduce(nm[:, t % 2, 0:1], s3[:, t % 2, 0:n], AX.X, ALU.max, negate=True)\
                       .then_inc(max_ready, 1)
                if s >= 3:
                    b, t = divmod(s - 3, NT)
                    see("O3", b, t)
                    dve.scalar_tensor_tensor(out=h[:, b * NT + t, :], in0=accs[t % 2].t[:, 0:P],
                                             scalar=rs1[:, (s - 3) % 4, 0:1], in1=h[:, b * NT + t, :],
                                             op0=ALU.mult, op1=ALU.add).then_inc(accs[t % 2].free, 1)
                if 2 <= s < NTT + 2 and (s - 2) % NT >= 3:
                    b, t = divmod(s - 2, NT)
                    see("T3", b, t, 1)
                    dve.tensor_copy(flat(pT3[:, t % 2, 3:t + 1, :]), turn[1].t[:, 0:(t - 2) * P])\
                       .then_inc(turn[1].free, 1)
                if s % NT == PROJECT and s < NTT - NT:
                    project3(s // NT + 1)
                side_norms("A3", None, s)
            moved("O3", B - 1, NT - 2)
            moved("O3", B - 1, NT - 1)
            dve.memset(nm[:, :, :], 0.0).then_inc(stage_done, 1)

            dve.wait_ge(loaded["mix3"], n_loads["mix3"])
            norm(B - 1)
            m = MIXES[3]
            for b in range(B):
                logits("F3", b)
            settle()
            dve.tensor_tensor(gw[:, :, 1], m8[:, :, 1], m8[:, :, 0], ALU.subtract).then_inc(max_ready, 1)
            then(dve.tensor_copy(i8f[:, :, :], i8[:, :, :]))
            choose(m)
            from_exp()
            then(dve.tensor_scalar(gw[:, :, 0], gw[:, :, 1], 1.0, None, ALU.add))
            then(dve.reciprocal(gw[:, :, 0], gw[:, :, 0]))
            then(dve.tensor_tensor(gw[:, :, 1], gw[:, :, 1], gw[:, :, 0], ALU.mult))
            step(times(gates, oneh[:, 0], gw[:, :, 0], 10))
            then(times(ex, oneh[:, 1], gw[:, :, 1], 10))
            dve.tensor_tensor(gates[:, :, 0:10], gates[:, :, 0:10], ex[:, :, 0:10], ALU.add).then_inc(gates_ready, 1)
            slots(m)
            dve.wait_ge(xs_out, 16 * sum(len(q) for q in seqs))

            def shared_sum(g):
                add_tiles(xn, 3 * g, 3, accs[(g + 1) % 2], ("shy", g),
                          accs[(g + 1) % 2].t[:, 0:HALF].rearrange("p (a c) -> p a c", a=3))

            shared_sum(0)
            invert(m)
            for g in range(1, 4):
                shared_sum(g)
            for g in range(4):
                moved("shy", g)
            expert_blocks(m, xn)
            for b in range(B):
                if b >= 2:
                    for g in (2 * b, 2 * b + 1):
                        shared_sum(g)
                    for g in (2 * b, 2 * b + 1):
                        moved("shy", g)
                combine(m, b, xn, gw)
                norm(b, xn, zt)
                z = zt[:, b * NT:(b + 1) * NT, :]
                then(dve.tensor_tensor(z, z, W["lng"][:, :].unsqueeze(1).to_broadcast([P, NT, P]), ALU.mult))
                then(dve.tensor_tensor(z, z, W["lnb"][:, :].unsqueeze(1).to_broadcast([P, NT, P]), ALU.add))
                dve.tensor_tensor(h[:, b * NT:(b + 1) * NT, :], h[:, b * NT:(b + 1) * NT, :], z, ALU.add)\
                   .then_inc(final_ready, 1)


def kernel(**inputs):
    import numpy as _np
    import concourse.bacc as _bacc
    from concourse import mybir as _mybir
    from concourse.bass_utils import run_bass_kernel_spmd as _run

    x = {k: _np.asarray(v) for k, v in inputs.items()}

    def cols(v, n=1):
        return v.reshape(n, -1).T

    qkv = x["L1_attn_b_qkv"]
    lay = {
        "x": x["x"].transpose(0, 2, 1),
        "tokW": x["L0_tok_W"].T,
        "tokv": _np.stack([x["L0_tok_b"], x["L0_tok_gamma"], x["L0_tok_beta"]], axis=1),
        "wq": x["L0_attn_w_q"], "wk": x["L0_attn_w_k"], "wv": x["L0_attn_w_v"],
        "wo": x["L0_attn_w_out"].reshape(4, 128, 128).transpose(1, 0, 2),
        "bo": x["L0_attn_b_out"][None],
        "Ws0": x["L0_ffn_Ws"], "bs0": x["L0_ffn_bs"][:, None],
        "L0b1": x["L0_ffn_b1"], "b2_0": x["L0_ffn_b2"],
        "L0w1": x["L0_ffn_W1"], "L0w2": x["L0_ffn_W2"],
        "wqkv1": x["L1_attn_W_qkv"], "bqk1": cols(qkv[:256], 2), "bv1": qkv[None, 256:],
        "wp1": x["L1_attn_W_proj"], "bp1": x["L1_attn_b_proj"][None],
        "ei": x["L1_ffn_expert_indices"], "ew": x["L1_ffn_expert_weights"],
        "L1w1": x["L1_ffn_w1"], "L1w2": x["L1_ffn_w2"],
        "wqk2": x["L2_attn_Wqkv"], "bqk2": cols(x["L2_attn_bqkv"], 2),
        "wvT2": x["L2_attn_Wv"].T.reshape(16, 128, 128).transpose(1, 0, 2),
        "bv2": cols(x["L2_attn_bv"], 16),
        "wo2": x["L2_attn_Wo"].reshape(16, 128, 128).transpose(1, 0, 2),
        "bo2": x["L2_attn_bo"][None],
        "lam": _np.stack([x["L2_attn_lq1"], x["L2_attn_lk1"], x["L2_attn_lq2"], x["L2_attn_lk2"]]),
        "rw2": x["L2_ffn_router_w"].T, "rb2": x["L2_ffn_router_b"][:, None],
        "L2b1": x["L2_ffn_b1"], "b2_2": x["L2_ffn_b2"],
        "L2w1": x["L2_ffn_w1"].transpose(0, 2, 1), "L2w2": x["L2_ffn_w2"].transpose(0, 2, 1),
        "wqk3": x["L3_attn_W_qk"], "wv3": x["L3_attn_W_v"].T, "bv3": x["L3_attn_b_v"][None],
        "rc1": x["L3_ffn_rc_w1"].transpose(1, 2, 0), "rcb1": cols(x["L3_ffn_rc_b1"]),
        "rc2": x["L3_ffn_rc_w2"].transpose(1, 2, 0), "rcb2": x["L3_ffn_rc_b2"][:, None],
        "sh1": x["L3_ffn_sh_w1"].transpose(1, 2, 0), "shb1": cols(x["L3_ffn_sh_b1"], 4),
        "sh2": x["L3_ffn_sh_w2"][:, :, 0].T.reshape(4, 128, 128).transpose(1, 0, 2),
        "shb2": x["L3_ffn_sh_b2"][None],
        "L3b1": x["L3_ffn_e_b1"], "b2_3": x["L3_ffn_e_b2"],
        "L3w1": x["L3_ffn_e_w1"], "L3w2": x["L3_ffn_e_w2"],
        "lng": x["L3_ffn_ln_g"], "lnb": x["L3_ffn_ln_b"],
    }
    nc = _bacc.Bacc("TRN2", target_bir_lowering=False, num_devices=1)
    arrays, aps = {}, {}
    for name, v in lay.items():
        v = _np.ascontiguousarray(v)
        arrays[f"in_{name}"] = v
        aps[name] = nc.dram_tensor(f"in_{name}", v.shape, _mybir.dt.from_np(v.dtype), kind="ExternalInput").ap()
    out = nc.dram_tensor("out", (B, T, P), _mybir.dt.float32, kind="ExternalOutput").ap()
    xs = nc.dram_tensor("xs", (B * TP, P), _mybir.dt.float32, kind="Internal").ap()
    ys = nc.dram_tensor("ys", (MAXB * P, P), _mybir.dt.float32, kind="Internal").ap()
    build(nc, aps, xs, ys, out)
    r = _run(nc, [arrays], core_ids=[0])
    return r.results[0]["out"]
```
